# Optimizing a Trainium2 kernel written in Bass

```python
import numpy as np
import jax
import jax.numpy as jnp

def _softmax(x, axis=-1):
    return jax.nn.softmax(x, axis=axis)

def _gelu(x):
    return jax.nn.gelu(x, approximate=True)

def _silu(x):
    return jax.nn.silu(x)

def _sigmoid(x):
    return jax.nn.sigmoid(x)

def _layernorm(x, axis=-1, eps=1e-05):
    m = jnp.mean(x, axis=axis, keepdims=True)
    v = jnp.var(x, axis=axis, keepdims=True)
    return (x - m) / jnp.sqrt(v + eps)

def _scatter_add(tgt, idx, src, axis=0):
    return tgt.at[idx].add(src)

def _segment_sum(src, seg, n):
    return jax.ops.segment_sum(src, seg, n)
kernel_name = 'mk_prb_d4_jaxref_r8_db04f6'

def setup_inputs(seed: int=0):
    np.random.seed(seed)
    _w = jnp.asarray

    def _L0_attn_setup():
        import jax, jax.numpy as jnp
        import numpy as np
        E = 128
        H = 16
        D = E // H

        def _mha(x, Wq, bq, Wk, bk, Wv, bv, Wo, bo):
            q = jnp.einsum('bse,hde->bhsd', x, Wq) + bq[None, :, None, :]
            k = jnp.einsum('bse,hde->bhsd', x, Wk) + bk[None, :, None, :]
            v = jnp.einsum('bse,hde->bhsd', x, Wv) + bv[None, :, None, :]
            scores = jnp.einsum('bhsd,bhtd->bhst', q, k) / jnp.sqrt(jnp.asarray(D, x.dtype))
            w = jax.nn.softmax(scores, axis=-1)
            o = jnp.einsum('bhst,bhtd->bhsd', w, v)
            B, _, S, _ = o.shape
            o = jnp.transpose(o, (0, 2, 1, 3)).reshape(B, S, H * D)
            return o @ Wo.T + bo
        key = jax.random.key(seed)
        ks = jax.random.split(key, 9)
        s = 0.02
        return {'hidden_state': jax.random.normal(ks[0], (4, 128, E), jnp.float32), 'Wq': jax.random.normal(ks[1], (H, D, E), jnp.float32) * s, 'bq': jax.random.normal(ks[2], (H, D), jnp.float32) * s, 'Wk': jax.random.normal(ks[3], (H, D, E), jnp.float32) * s, 'bk': jax.random.normal(ks[4], (H, D), jnp.float32) * s, 'Wv': jax.random.normal(ks[5], (H, D, E), jnp.float32) * s, 'bv': jax.random.normal(ks[6], (H, D), jnp.float32) * s, 'Wo': jax.random.normal(ks[7], (E, E), jnp.float32) * s, 'bo': jax.random.normal(ks[8], (E,), jnp.float32) * s}
    _L0_attn_in = _L0_attn_setup()

    def _L0_ffn_setup():
        import jax, jax.numpy as jnp
        import numpy as np
        B, S, D, E, F = (2, 256, 128, 14, 256)
        key = jax.random.key(seed)
        k = jax.random.split(key, 4)
        h = jax.random.normal(k[0], (B, S, D), dtype=jnp.float32)
        router_w = jax.random.normal(k[1], (D, E), dtype=jnp.float32) * 0.02
        w1 = jax.random.uniform(k[2], (E, D, F), dtype=jnp.float32, minval=-1.0, maxval=1.0) * float(np.sqrt(6.0 / D))
        w2 = jax.random.uniform(k[3], (E, F, D), dtype=jnp.float32, minval=-1.0, maxval=1.0) * float(np.sqrt(6.0 / F))
        b1 = jnp.zeros((E, F), dtype=jnp.float32)
        b2 = jnp.zeros((E, D), dtype=jnp.float32)
        return {'h': h, 'router_w': router_w, 'w1': w1, 'b1': b1, 'w2': w2, 'b2': b2}
    _L0_ffn_in = _L0_ffn_setup()

    def _L1_attn_setup():
        import jax, jax.numpy as jnp
        import numpy as np
        EMBED_DIM = 128
        NUM_HEADS = 16
        HEAD_DIM = EMBED_DIM // NUM_HEADS
        WINDOW_SIZE = 32
        SCALE = 1.0 / np.sqrt(HEAD_DIM)

        def _band_mask(T):
            i = jnp.arange(T)[:, None]
            j = jnp.arange(T)[None, :]
            full = j > i
            band = full & (j >= i - (WINDOW_SIZE - 1))
            return band
        key = jax.random.key(seed)
        kx, kq, kk, kv, ko = jax.random.split(key, 5)
        B, T, C = (2, 256, EMBED_DIM)
        x = jax.random.normal(kx, (B, T, C), dtype=jnp.float32)
        s = 1.0 / np.sqrt(C)
        Wq = jax.random.uniform(kq, (C, C), dtype=jnp.float32, minval=-s, maxval=s)
        Wk = jax.random.uniform(kk, (C, C), dtype=jnp.float32, minval=-s, maxval=s)
        Wv = jax.random.uniform(kv, (C, C), dtype=jnp.float32, minval=-s, maxval=s)
        Wo = jax.random.uniform(ko, (C, C), dtype=jnp.float32, minval=-s, maxval=s)
        return {'x': x, 'Wq': Wq, 'Wk': Wk, 'Wv': Wv, 'Wo': Wo}
    _L1_attn_in = _L1_attn_setup()

    def _L1_ffn_setup():
        import jax, jax.numpy as jnp
        import numpy as np
        DIM = 128
        HIDDEN = 256
        N_EXPERTS = 8
        TOP_K = 2
        EPS = 1e-06

        def rms_norm(x, scale, eps=EPS):
            ms = jnp.mean(jnp.square(x.astype(jnp.float32)), axis=-1, keepdims=True)
            s = scale.astype(jnp.float32) * jax.lax.rsqrt(ms + eps)
            return x * s.astype(x.dtype)

        def moe_linear(xf, ids, W):
            E = W.shape[0]
            out = jnp.zeros((xf.shape[0], W.shape[1]), dtype=xf.dtype)
            for e in range(E):
                out = out + jnp.where((ids == e)[:, None], xf @ W[e].T, 0.0)
            return out
        key = jax.random.key(seed)
        k1, k2, k3, k4 = jax.random.split(key, 4)
        x = jax.random.normal(k1, (4, 512, DIM), dtype=jnp.float32)
        norm_scale = jnp.ones((DIM,), dtype=jnp.float32)
        w_router = jax.random.normal(k2, (N_EXPERTS, DIM), dtype=jnp.float32) / np.sqrt(DIM)
        lim_up = np.sqrt(6.0 / (DIM + 2 * HIDDEN))
        w_up = jax.random.uniform(k3, (N_EXPERTS, 2 * HIDDEN, DIM), dtype=jnp.float32, minval=-lim_up, maxval=lim_up)
        lim_dn = np.sqrt(6.0 / (HIDDEN + DIM))
        w_down = jax.random.uniform(k4, (N_EXPERTS, DIM, HIDDEN), dtype=jnp.float32, minval=-lim_dn, maxval=lim_dn)
        return {'x': x, 'norm_scale': norm_scale, 'w_router': w_router, 'w_up': w_up, 'w_down': w_down}
    _L1_ffn_in = _L1_ffn_setup()

    def _L2_attn_setup():
        import jax, jax.numpy as jnp
        import numpy as np
        INFTY_APPROX = 1e+30
        LAM = 10000.0

        def sinusoid_embs(length, width):
            pos = jnp.arange(length, dtype=jnp.float32)
            inv_lams = 1.0 / LAM ** (jnp.arange(0, width, 2, dtype=jnp.float32) / width)
            pre = pos[:, None] * inv_lams[None, :]
            cat = jnp.concatenate([jnp.sin(pre), jnp.cos(pre)], axis=-1)
            return jnp.flip(cat, axis=0)

        def rel_shift(x):
            b, t, _ = x.shape
            x = jnp.pad(x, ((0, 0), (0, 0), (1, 0)))
            x = x.reshape(b, t + 1, t)[:, 1:, :]
            return x
        B, T, D, K, V = (2, 512, 128, 128, 256)
        key = jax.random.key(seed)
        ks = jax.random.split(key, 10)
        s_d = 1.0 / np.sqrt(D)
        s_v = 1.0 / np.sqrt(V)
        return {'x': jax.random.normal(ks[0], (B, T, D), dtype=jnp.float32), 'g_ln': jnp.ones((D,), dtype=jnp.float32), 'W_q': s_d * jax.random.normal(ks[1], (D, K), dtype=jnp.float32), 'W_k': s_d * jax.random.normal(ks[2], (D, K), dtype=jnp.float32), 'W_v': s_d * jax.random.normal(ks[3], (D, V), dtype=jnp.float32), 'W_g': s_d * jax.random.normal(ks[4], (D, V), dtype=jnp.float32), 'W_r': s_d * jax.random.normal(ks[5], (D, K), dtype=jnp.float32), 'xl_u': 0.02 * jax.random.normal(ks[6], (K,), dtype=jnp.float32), 'xl_v': 0.02 * jax.random.normal(ks[7], (K,), dtype=jnp.float32), 'W_o': s_v * jax.random.normal(ks[8], (V, D), dtype=jnp.float32)}
    _L2_attn_in = _L2_attn_setup()

    def _L2_ffn_setup():
        import jax, jax.numpy as jnp
        import numpy as np
        K = 32
        key = jax.random.key(seed)
        ks = jax.random.split(key, 9)
        B, S, D, O, E = (8, 256, 128, 128, 16)

        def xavier(k_, shape):
            fan_in, fan_out = (shape[-2], shape[-1])
            lim = (6.0 / (fan_in + fan_out)) ** 0.5
            return jax.random.uniform(k_, shape, jnp.float32, -lim, lim)
        return {'x': jax.random.normal(ks[0], (B, S, D), jnp.float32), 'Wg': xavier(ks[1], (D, E)), 'bg': jnp.zeros((E,), jnp.float32), 'w1': xavier(ks[2], (E, D, O)), 'b1': xavier(ks[3], (E, 1)), 'w2': xavier(ks[4], (E, O, O)), 'b2': xavier(ks[5], (E, 1)), 'w3': xavier(ks[6], (E, O, O)), 'b3': xavier(ks[7], (E, 1))}
    _L2_ffn_in = _L2_ffn_setup()

    def _L3_attn_setup():
        import jax, jax.numpy as jnp
        import numpy as np
        D_MODEL = 128
        NUM_HEADS = 16
        DEPTH = D_MODEL // NUM_HEADS
        B, T = (2, 256)

        def _rope(x):
            H = x.shape[1]
            D = x.shape[-1]
            inv_freq = 1.0 / 10000.0 ** (jnp.arange(0, D, 2, dtype=jnp.float32) / D)
            freqs = jnp.arange(H, dtype=jnp.float32)[:, None] * inv_freq[None, :]
            sin = jnp.sin(freqs)[:, None, :]
            cos = jnp.cos(freqs)[:, None, :]
            x1 = x[..., ::2]
            x2 = x[..., 1::2]
            rot = jnp.stack([x1 * cos - x2 * sin, x1 * sin + x2 * cos], axis=-1)
            return rot.reshape(x.shape)
        key = jax.random.key(seed)
        k_x, k_wq, k_bq, k_wf, k_bf = jax.random.split(key, 5)
        lim_qkv = 1.0 / np.sqrt(D_MODEL)
        lim_fc = 1.0 / np.sqrt(D_MODEL)
        return {'x': jax.random.normal(k_x, (B, T, D_MODEL), dtype=jnp.float32), 'w_qkv': jax.random.uniform(k_wq, (D_MODEL, 3 * D_MODEL), jnp.float32, -lim_qkv, lim_qkv), 'b_qkv': jax.random.uniform(k_bq, (3 * D_MODEL,), jnp.float32, -lim_qkv, lim_qkv), 'w_fc': jax.random.uniform(k_wf, (D_MODEL, D_MODEL), jnp.float32, -lim_fc, lim_fc), 'b_fc': jax.random.uniform(k_bf, (D_MODEL,), jnp.float32, -lim_fc, lim_fc)}
    _L3_attn_in = _L3_attn_setup()

    def _L3_ffn_setup():
        import jax, jax.numpy as jnp
        import numpy as np
        B, N, D, H, E = (4, 128, 128, 16, 8)
        DK = D // H
        HID = 4 * D
        EPS = 1e-05

        def _layernorm(x, w, b):
            m = jnp.mean(x, axis=-1, keepdims=True)
            v = jnp.mean(jnp.square(x - m), axis=-1, keepdims=True)
            return (x - m) * jax.lax.rsqrt(v + EPS) * w + b

        def _msa(x, w_qkv, w_proj):
            b, n, d = x.shape
            qkv = (x @ w_qkv).reshape(b, n, 3, H, DK)
            q = qkv[:, :, 0].transpose(0, 2, 1, 3)
            k = qkv[:, :, 1].transpose(0, 2, 1, 3)
            v = qkv[:, :, 2].transpose(0, 2, 1, 3)
            attn = jnp.einsum('bhnd,bhmd->bhnm', q, k) * (1.0 / np.sqrt(DK))
            attn = jax.nn.softmax(attn, axis=-1)
            y = jnp.einsum('bhnm,bhmd->bhnd', attn, v)
            y = y.transpose(0, 2, 1, 3).reshape(b, n, d)
            return y @ w_proj

        def _moe_mlp(x, gate_w, gate_b, w1, w2):
            b, n, d = x.shape
            xf = x.reshape(b * n, d)
            logits = xf @ gate_w + gate_b
            one_hot = jax.nn.one_hot(jnp.argmax(logits, axis=-1), E, dtype=xf.dtype)
            h = jax.nn.gelu(jnp.einsum('td,edh->teh', xf, w1), approximate=True)
            y = jnp.einsum('teh,ehd->ted', h, w2)
            out = jnp.einsum('te,ted->td', one_hot, y)
            return out.reshape(b, n, d)
        key = jax.random.key(seed)
        ks = jax.random.split(key, 8)
        s = 0.02
        return {'x': jax.random.normal(ks[0], (B, N, D), jnp.float32), 'ln1_w': jnp.ones((D,), jnp.float32), 'ln1_b': jnp.zeros((D,), jnp.float32), 'w_qkv': jax.random.normal(ks[1], (D, 3 * D), jnp.float32) * s, 'w_proj': jax.random.normal(ks[2], (D, D), jnp.float32) * s, 'ln2_w': jnp.ones((D,), jnp.float32), 'ln2_b': jnp.zeros((D,), jnp.float32), 'gate_w': jax.random.normal(ks[3], (D, E), jnp.float32) * s, 'gate_b': jnp.zeros((E,), jnp.float32), 'w1': jax.random.normal(ks[4], (E, D, HID), jnp.float32) * s, 'w2': jax.random.normal(ks[5], (E, HID, D), jnp.float32) * s}
    _L3_ffn_in = _L3_ffn_setup()
    _d = {'L0_attn_hidden_state': _L0_attn_in['hidden_state'], 'L0_attn_Wq': _L0_attn_in['Wq'], 'L0_attn_bq': _L0_attn_in['bq'], 'L0_attn_Wk': _L0_attn_in['Wk'], 'L0_attn_bk': _L0_attn_in['bk'], 'L0_attn_Wv': _L0_attn_in['Wv'], 'L0_attn_bv': _L0_attn_in['bv'], 'L0_attn_Wo': _L0_attn_in['Wo'], 'L0_attn_bo': _L0_attn_in['bo'], 'L0_ffn_router_w': _L0_ffn_in['router_w'], 'L0_ffn_w1': _L0_ffn_in['w1'], 'L0_ffn_b1': _L0_ffn_in['b1'], 'L0_ffn_w2': _L0_ffn_in['w2'], 'L0_ffn_b2': _L0_ffn_in['b2'], 'L1_attn_Wq': _L1_attn_in['Wq'], 'L1_attn_Wk': _L1_attn_in['Wk'], 'L1_attn_Wv': _L1_attn_in['Wv'], 'L1_attn_Wo': _L1_attn_in['Wo'], 'L1_ffn_norm_scale': _L1_ffn_in['norm_scale'], 'L1_ffn_w_router': _L1_ffn_in['w_router'], 'L1_ffn_w_up': _L1_ffn_in['w_up'], 'L1_ffn_w_down': _L1_ffn_in['w_down'], 'L2_attn_g_ln': _L2_attn_in['g_ln'], 'L2_attn_W_q': _L2_attn_in['W_q'], 'L2_attn_W_k': _L2_attn_in['W_k'], 'L2_attn_W_v': _L2_attn_in['W_v'], 'L2_attn_W_g': _L2_attn_in['W_g'], 'L2_attn_W_r': _L2_attn_in['W_r'], 'L2_attn_xl_u': _L2_attn_in['xl_u'], 'L2_attn_xl_v': _L2_attn_in['xl_v'], 'L2_attn_W_o': _L2_attn_in['W_o'], 'L2_ffn_Wg': _L2_ffn_in['Wg'], 'L2_ffn_bg': _L2_ffn_in['bg'], 'L2_ffn_w1': _L2_ffn_in['w1'], 'L2_ffn_b1': _L2_ffn_in['b1'], 'L2_ffn_w2': _L2_ffn_in['w2'], 'L2_ffn_b2': _L2_ffn_in['b2'], 'L2_ffn_w3': _L2_ffn_in['w3'], 'L2_ffn_b3': _L2_ffn_in['b3'], 'L3_attn_w_qkv': _L3_attn_in['w_qkv'], 'L3_attn_b_qkv': _L3_attn_in['b_qkv'], 'L3_attn_w_fc': _L3_attn_in['w_fc'], 'L3_attn_b_fc': _L3_attn_in['b_fc'], 'L3_ffn_ln1_w': _L3_ffn_in['ln1_w'], 'L3_ffn_ln1_b': _L3_ffn_in['ln1_b'], 'L3_ffn_w_qkv': _L3_ffn_in['w_qkv'], 'L3_ffn_w_proj': _L3_ffn_in['w_proj'], 'L3_ffn_ln2_w': _L3_ffn_in['ln2_w'], 'L3_ffn_ln2_b': _L3_ffn_in['ln2_b'], 'L3_ffn_gate_w': _L3_ffn_in['gate_w'], 'L3_ffn_gate_b': _L3_ffn_in['gate_b'], 'L3_ffn_w1': _L3_ffn_in['w1'], 'L3_ffn_w2': _L3_ffn_in['w2']}
    _x0 = _d['L0_attn_hidden_state']
    _d['L0_attn_hidden_state'] = jax.random.normal(jax.random.fold_in(jax.random.key(seed), 1), (8, 256, 128), dtype=_x0.dtype)
    del _x0
    return _d

def reference(L0_attn_hidden_state, L0_attn_Wq, L0_attn_bq, L0_attn_Wk, L0_attn_bk, L0_attn_Wv, L0_attn_bv, L0_attn_Wo, L0_attn_bo, L0_ffn_router_w, L0_ffn_w1, L0_ffn_b1, L0_ffn_w2, L0_ffn_b2, L1_attn_Wq, L1_attn_Wk, L1_attn_Wv, L1_attn_Wo, L1_ffn_norm_scale, L1_ffn_w_router, L1_ffn_w_up, L1_ffn_w_down, L2_attn_g_ln, L2_attn_W_q, L2_attn_W_k, L2_attn_W_v, L2_attn_W_g, L2_attn_W_r, L2_attn_xl_u, L2_attn_xl_v, L2_attn_W_o, L2_ffn_Wg, L2_ffn_bg, L2_ffn_w1, L2_ffn_b1, L2_ffn_w2, L2_ffn_b2, L2_ffn_w3, L2_ffn_b3, L3_attn_w_qkv, L3_attn_b_qkv, L3_attn_w_fc, L3_attn_b_fc, L3_ffn_ln1_w, L3_ffn_ln1_b, L3_ffn_w_qkv, L3_ffn_w_proj, L3_ffn_ln2_w, L3_ffn_ln2_b, L3_ffn_gate_w, L3_ffn_gate_b, L3_ffn_w1, L3_ffn_w2):

    def _L0_attn_ref(hidden_state, Wq, bq, Wk, bk, Wv, bv, Wo, bo):
        import jax, jax.numpy as jnp
        import numpy as np
        E = 128
        H = 16
        D = E // H

        def _mha(x, Wq, bq, Wk, bk, Wv, bv, Wo, bo):
            q = jnp.einsum('bse,hde->bhsd', x, Wq) + bq[None, :, None, :]
            k = jnp.einsum('bse,hde->bhsd', x, Wk) + bk[None, :, None, :]
            v = jnp.einsum('bse,hde->bhsd', x, Wv) + bv[None, :, None, :]
            scores = jnp.einsum('bhsd,bhtd->bhst', q, k) / jnp.sqrt(jnp.asarray(D, x.dtype))
            w = jax.nn.softmax(scores, axis=-1)
            o = jnp.einsum('bhst,bhtd->bhsd', w, v)
            B, _, S, _ = o.shape
            o = jnp.transpose(o, (0, 2, 1, 3)).reshape(B, S, H * D)
            return o @ Wo.T + bo
        return _mha(hidden_state, Wq, bq, Wk, bk, Wv, bv, Wo, bo)

    def _L0_ffn_ref(h, router_w, w1, b1, w2, b2):
        import jax, jax.numpy as jnp
        import numpy as np
        B, S, D, E, F = (2, 256, 128, 14, 256)
        Bb, Ss, Dd = h.shape
        x = h.reshape(-1, Dd)
        logits = x @ router_w
        assignments = jnp.argmax(logits, axis=-1)
        probs = jax.nn.softmax(logits, axis=-1)
        weights = jnp.take_along_axis(probs, assignments[:, None], axis=1)[:, 0]
        hid = jnp.einsum('nd,edf->nef', x, w1) + b1
        hid = jax.nn.gelu(hid, approximate=False)
        all_out = jnp.einsum('nef,efd->ned', hid, w2) + b2
        sel = jnp.take_along_axis(all_out, assignments[:, None, None], axis=1)[:, 0, :]
        moe_out = (sel * weights[:, None]).reshape(Bb, Ss, Dd)
        return moe_out

    def _L1_attn_ref(x, Wq, Wk, Wv, Wo):
        import jax, jax.numpy as jnp
        import numpy as np
        EMBED_DIM = 128
        NUM_HEADS = 16
        HEAD_DIM = EMBED_DIM // NUM_HEADS
        WINDOW_SIZE = 32
        SCALE = 1.0 / np.sqrt(HEAD_DIM)

        def _band_mask(T):
            i = jnp.arange(T)[:, None]
            j = jnp.arange(T)[None, :]
            full = j > i
            band = full & (j >= i - (WINDOW_SIZE - 1))
            return band
        B, T, C = x.shape
        H, D = (NUM_HEADS, HEAD_DIM)
        q = jnp.einsum('btc,oc->bto', x, Wq).reshape(B, T, H, D)
        k = jnp.einsum('btc,oc->bto', x, Wk).reshape(B, T, H, D)
        v = jnp.einsum('btc,oc->bto', x, Wv).reshape(B, T, H, D)
        att = jnp.einsum('bqhd,bkhd->bhqk', q, k) * SCALE
        mask = _band_mask(T)
        att = jnp.where(mask[None, None, :, :], -jnp.inf, att)
        att = jax.nn.softmax(att, axis=-1)
        out = jnp.einsum('bhqk,bkhd->bqhd', att, v).reshape(B, T, C)
        return jnp.einsum('btc,oc->bto', out, Wo)

    def _L1_ffn_ref(x, norm_scale, w_router, w_up, w_down):
        import jax, jax.numpy as jnp
        import numpy as np
        DIM = 128
        HIDDEN = 256
        N_EXPERTS = 8
        TOP_K = 2
        EPS = 1e-06

        def rms_norm(x, scale, eps=EPS):
            ms = jnp.mean(jnp.square(x.astype(jnp.float32)), axis=-1, keepdims=True)
            s = scale.astype(jnp.float32) * jax.lax.rsqrt(ms + eps)
            return x * s.astype(x.dtype)

        def moe_linear(xf, ids, W):
            E = W.shape[0]
            out = jnp.zeros((xf.shape[0], W.shape[1]), dtype=xf.dtype)
            for e in range(E):
                out = out + jnp.where((ids == e)[:, None], xf @ W[e].T, 0.0)
            return out
        B, S, D = x.shape
        skip = x
        xn = rms_norm(x, norm_scale)
        scores = (xn @ w_router.T).astype(jnp.float32)
        scores_topk, idx = jax.lax.top_k(scores, TOP_K)
        weights = jax.nn.softmax(scores_topk, axis=-1)
        xf = jnp.broadcast_to(xn[..., None, :], (B, S, TOP_K, D)).reshape(-1, D)
        ids = idx.reshape(-1)
        up = moe_linear(xf, ids, w_up)
        u, gate = jnp.split(up, 2, axis=-1)
        h = u * jax.nn.silu(gate)
        down = moe_linear(h, ids, w_down)
        down = down.reshape(B, S, TOP_K, D)
        out = jnp.sum(down * weights[..., None].astype(down.dtype), axis=-2)
        return out + skip

    def _L2_attn_ref(x, g_ln, W_q, W_k, W_v, W_g, W_r, xl_u, xl_v, W_o):
        import jax, jax.numpy as jnp
        import numpy as np
        INFTY_APPROX = 1e+30
        LAM = 10000.0

        def sinusoid_embs(length, width):
            pos = jnp.arange(length, dtype=jnp.float32)
            inv_lams = 1.0 / LAM ** (jnp.arange(0, width, 2, dtype=jnp.float32) / width)
            pre = pos[:, None] * inv_lams[None, :]
            cat = jnp.concatenate([jnp.sin(pre), jnp.cos(pre)], axis=-1)
            return jnp.flip(cat, axis=0)

        def rel_shift(x):
            b, t, _ = x.shape
            x = jnp.pad(x, ((0, 0), (0, 0), (1, 0)))
            x = x.reshape(b, t + 1, t)[:, 1:, :]
            return x
        B, T, D = x.shape
        K = W_q.shape[-1]
        tau = jnp.asarray(K, x.dtype) ** 0.5
        x_tilde = x * jax.lax.rsqrt(jnp.mean(jnp.square(x), axis=-1, keepdims=True) + 1e-06)
        x_tilde = x_tilde * g_ln
        q = x_tilde @ W_q / tau
        k = x_tilde @ W_k
        v = x_tilde @ W_v
        xl_r = sinusoid_embs(T, D) @ W_r
        scores_ac = jnp.einsum('bik,bjk->bij', q + xl_u, k)
        scores_bd = jnp.einsum('bik,jk->bij', q + xl_v, xl_r)
        scores_bd = rel_shift(scores_bd)
        scores = scores_ac + scores_bd
        keep = jnp.tril(jnp.ones((T, T), dtype=bool))
        scores = scores - jnp.asarray(INFTY_APPROX, x.dtype) * jnp.logical_not(keep)
        w = jax.nn.softmax(scores, axis=-1)
        wv = jnp.einsum('bij,bjv->biv', w, v)
        wv = wv * jax.nn.silu(x_tilde @ W_g)
        res = wv @ W_o
        return res

    def _L2_ffn_ref(x, Wg, bg, w1, b1, w2, b2, w3, b3):
        import jax, jax.numpy as jnp
        import numpy as np
        K = 32
        B, S, D = x.shape
        E, _, O = w1.shape
        logits = jnp.einsum('bsd,de->bse', x, Wg) + bg
        probs = jax.nn.softmax(logits, axis=-2)
        pv = jnp.transpose(probs, (0, 2, 1))
        vals, idx = jax.lax.top_k(pv, K)
        bidx = jnp.arange(B)[:, None, None]
        tok = x[bidx, idx]
        b1b = b1[None, :, None, :]
        b2b = b2[None, :, None, :]
        b3b = b3[None, :, None, :]
        h = jax.nn.relu(jnp.einsum('bekd,edo->beko', tok, w1) + b1b)
        h = jax.nn.relu(jnp.einsum('bekd,edo->beko', h, w2) + b2b)
        h = jnp.einsum('bekd,edo->beko', h, w3) + b3b
        out = h * vals[..., None]
        outputs = jnp.zeros((B, S, O), x.dtype).at[bidx, idx].add(out)
        return outputs

    def _L3_attn_ref(x, w_qkv, b_qkv, w_fc, b_fc):
        import jax, jax.numpy as jnp
        import numpy as np
        D_MODEL = 128
        NUM_HEADS = 16
        DEPTH = D_MODEL // NUM_HEADS
        B, T = (2, 256)

        def _rope(x):
            H = x.shape[1]
            D = x.shape[-1]
            inv_freq = 1.0 / 10000.0 ** (jnp.arange(0, D, 2, dtype=jnp.float32) / D)
            freqs = jnp.arange(H, dtype=jnp.float32)[:, None] * inv_freq[None, :]
            sin = jnp.sin(freqs)[:, None, :]
            cos = jnp.cos(freqs)[:, None, :]
            x1 = x[..., ::2]
            x2 = x[..., 1::2]
            rot = jnp.stack([x1 * cos - x2 * sin, x1 * sin + x2 * cos], axis=-1)
            return rot.reshape(x.shape)
        Bs, Ts, C = x.shape
        H, D = (NUM_HEADS, DEPTH)
        qkv = x @ w_qkv + b_qkv
        qkv = qkv.reshape(Bs, Ts, 3, H, D)
        qkv = jnp.transpose(qkv, (2, 0, 3, 1, 4))
        q, k, v = (qkv[0], qkv[1], qkv[2])
        q = _rope(q)
        k = _rope(k)
        scores = jnp.einsum('bhtd,bhsd->bhts', q, k) / jnp.sqrt(jnp.float32(D))
        attn = jax.nn.softmax(scores, axis=-1)
        out = jnp.einsum('bhts,bhsd->bhtd', attn, v)
        out = jnp.transpose(out, (0, 2, 1, 3)).reshape(Bs, Ts, C)
        return out @ w_fc + b_fc

    def _L3_ffn_ref(x, ln1_w, ln1_b, w_qkv, w_proj, ln2_w, ln2_b, gate_w, gate_b, w1, w2):
        import jax, jax.numpy as jnp
        import numpy as np
        B, N, D, H, E = (4, 128, 128, 16, 8)
        DK = D // H
        HID = 4 * D
        EPS = 1e-05

        def _layernorm(x, w, b):
            m = jnp.mean(x, axis=-1, keepdims=True)
            v = jnp.mean(jnp.square(x - m), axis=-1, keepdims=True)
            return (x - m) * jax.lax.rsqrt(v + EPS) * w + b

        def _msa(x, w_qkv, w_proj):
            b, n, d = x.shape
            qkv = (x @ w_qkv).reshape(b, n, 3, H, DK)
            q = qkv[:, :, 0].transpose(0, 2, 1, 3)
            k = qkv[:, :, 1].transpose(0, 2, 1, 3)
            v = qkv[:, :, 2].transpose(0, 2, 1, 3)
            attn = jnp.einsum('bhnd,bhmd->bhnm', q, k) * (1.0 / np.sqrt(DK))
            attn = jax.nn.softmax(attn, axis=-1)
            y = jnp.einsum('bhnm,bhmd->bhnd', attn, v)
            y = y.transpose(0, 2, 1, 3).reshape(b, n, d)
            return y @ w_proj

        def _moe_mlp(x, gate_w, gate_b, w1, w2):
            b, n, d = x.shape
            xf = x.reshape(b * n, d)
            logits = xf @ gate_w + gate_b
            one_hot = jax.nn.one_hot(jnp.argmax(logits, axis=-1), E, dtype=xf.dtype)
            h = jax.nn.gelu(jnp.einsum('td,edh->teh', xf, w1), approximate=True)
            y = jnp.einsum('teh,ehd->ted', h, w2)
            out = jnp.einsum('te,ted->td', one_hot, y)
            return out.reshape(b, n, d)
        x = x + _msa(_layernorm(x, ln1_w, ln1_b), w_qkv, w_proj)
        x = x + _moe_mlp(_layernorm(x, ln2_w, ln2_b), gate_w, gate_b, w1, w2)
        return x
    x = L0_attn_hidden_state
    xn = _layernorm(x, axis=-1)
    x = x + _L0_attn_ref(xn, L0_attn_Wq, L0_attn_bq, L0_attn_Wk, L0_attn_bk, L0_attn_Wv, L0_attn_bv, L0_attn_Wo, L0_attn_bo) + _L0_ffn_ref(xn, L0_ffn_router_w, L0_ffn_w1, L0_ffn_b1, L0_ffn_w2, L0_ffn_b2)
    xn = _layernorm(x, axis=-1)
    x = x + _L1_attn_ref(xn, L1_attn_Wq, L1_attn_Wk, L1_attn_Wv, L1_attn_Wo) + _L1_ffn_ref(xn, L1_ffn_norm_scale, L1_ffn_w_router, L1_ffn_w_up, L1_ffn_w_down)
    xn = _layernorm(x, axis=-1)
    x = x + _L2_attn_ref(xn, L2_attn_g_ln, L2_attn_W_q, L2_attn_W_k, L2_attn_W_v, L2_attn_W_g, L2_attn_W_r, L2_attn_xl_u, L2_attn_xl_v, L2_attn_W_o) + _L2_ffn_ref(xn, L2_ffn_Wg, L2_ffn_bg, L2_ffn_w1, L2_ffn_b1, L2_ffn_w2, L2_ffn_b2, L2_ffn_w3, L2_ffn_b3)
    xn = _layernorm(x, axis=-1)
    x = x + _L3_attn_ref(xn, L3_attn_w_qkv, L3_attn_b_qkv, L3_attn_w_fc, L3_attn_b_fc) + _L3_ffn_ref(xn, L3_ffn_ln1_w, L3_ffn_ln1_b, L3_ffn_w_qkv, L3_ffn_w_proj, L3_ffn_ln2_w, L3_ffn_ln2_b, L3_ffn_gate_w, L3_ffn_gate_b, L3_ffn_w1, L3_ffn_w2)
    return x

_drawn_inputs = setup_inputs


def setup_inputs(seed=0):
    import zlib

    import numpy as np

    out = dict(_drawn_inputs(seed))
    spreads = {'L0_ffn_b1': (0.0, 0.57),
     'L0_ffn_b2': (0.0, 0.615),
     'L1_ffn_norm_scale': (1.0, 0.2),
     'L2_attn_g_ln': (1.0, 0.541),
     'L2_ffn_bg': (0.0, 2.0),
     'L3_ffn_ln1_w': (1.0, 0.6),
     'L3_ffn_ln1_b': (0.0, 0.8),
     'L3_ffn_ln2_w': (1.0, 0.6),
     'L3_ffn_ln2_b': (0.0, 2.0),
     'L3_ffn_gate_b': (0.0, 2.0)}
    factors = {'L0_attn_Wq': 8.0,
     'L0_attn_bq': 8.0,
     'L0_attn_Wk': 8.0,
     'L0_attn_bk': 200.0,
     'L0_attn_Wv': 8.0,
     'L0_attn_bv': 8.0,
     'L0_attn_Wo': 6.966,
     'L1_attn_Wq': 6.013,
     'L1_attn_Wk': 5.872,
     'L2_attn_xl_u': 3.051,
     'L2_attn_xl_v': 8.0,
     'L2_ffn_Wg': 4.705,
     'L2_ffn_w1': 7.892,
     'L2_ffn_b1': 8.0,
     'L2_ffn_w2': 6.486,
     'L2_ffn_b2': 8.0,
     'L2_ffn_w3': 4.736,
     'L2_ffn_b3': 28.033,
     'L3_attn_w_qkv': 6.588,
     'L3_attn_b_qkv': 5.508,
     'L3_attn_w_fc': 4.404,
     'L3_attn_b_fc': 26.232,
     'L3_ffn_w_qkv': 8.0,
     'L3_ffn_w_proj': 8.0,
     'L3_ffn_gate_w': 10.341,
     'L3_ffn_w1': 3.176,
     'L3_ffn_w2': 3.131}
    for name, (base, spread) in spreads.items():
        noise = np.random.default_rng([zlib.crc32(name.encode()), seed]).standard_normal(out[name].shape)
        drawn = base * np.exp(spread * noise) if base else spread * noise
        out[name] = jnp.asarray(drawn.astype(out[name].dtype))
    for name, factor in factors.items():
        out[name] = (out[name] * factor).astype(out[name].dtype)
    return out
```

```python
import numpy as np
import concourse.bass as bass
from concourse import mybir
from contextlib import ExitStack

F32 = mybir.dt.float32
BF16 = mybir.dt.bfloat16
ALU = mybir.AluOpType
ACT = mybir.ActivationFunctionType
AX_X = mybir.AxisListType.X

P = 128
BATCH, SEQ = 8, 256
TILES = BATCH * SEQ // P
TPB = SEQ // P
HEADS, HD = 16, 8
PAIRS = HEADS // 2
SLOT = 64
PARTS = ((0, 0), (0, 1), (0, 2), (1, 0), (1, 1), (2, 0))
MAXROW = len(PARTS) * HD
SCORE_ROWS, SHIFTED_ROWS = MAXROW, MAXROW + 2
NEG = -1.0e30

def plan_pack(entries):
    at, plan = 0, {}
    for name, width in entries:
        plan[name] = (at, width)
        at += width
    return plan, at


L0E, L0F, L1E, L1F, L2E, L2K, L3E, L3F = 14, 256, 8, 256, 16, 32, 8, 512
COMMON, COMMON_W = plan_pack([("ident", P), ("ones", P), ("tie", 16), ("slot_no", L2K), ("slot_of_row", 1)])
PACK0, PACK0_W = plan_pack([("wqkv", 384), ("bqk", 256), ("bv", 1), ("wo", P), ("bo", P), ("router", L0E),
                            ("w1", L0E * L0F), ("b1", L0E * 2), ("w2", L0E * L0F), ("b2", P)])
PACK1, PACK1_W = plan_pack([("wqkv", 384), ("wo", P), ("scale", 1), ("router", L1E), ("w1", L1E * 2 * L1F),
                            ("w2", L1E * L1F)])
PACK2, PACK2_W = plan_pack([("g", 1), ("wq", P), ("wk", P), ("wvg", 512), ("wrT", P), ("wrTs", P), ("u", 1),
                            ("v", 1), ("wo", 2 * P), ("rot_a", SEQ), ("rot_b", SEQ), ("pos", SEQ),
                            ("router", 240), ("rb", 1), ("w1", L2E * P), ("w2", L2E * P), ("w3", L2E * P),
                            ("b1", L2E), ("b2", L2E), ("b3", L2E)])
PACK3, PACK3_W = plan_pack([("wqT", P), ("wkT", P), ("wv", P), ("rope", P), ("bq", 1), ("bk", 1), ("bv", 1),
                            ("wo", P), ("bo", P), ("ln1w", 1), ("ln1b", 1), ("wqkv2", 384), ("wo2", P),
                            ("ln2w", 1), ("ln2b", 1), ("router", L3E), ("rbias", L3E), ("w1", L3E * L3F),
                            ("w2", L3E * L3F)])
REGION_A = max(PACK0_W, PACK2_W)
REGION_B = max(PACK1_W, PACK3_W)


def build(nc, packs, x_in, out, stop=99):
    with ExitStack() as ctx:
        def sb(name, shape, dt=F32):
            return ctx.enter_context(nc.sbuf_tensor(name, shape, dt))

        def sem(name):
            return ctx.enter_context(nc.semaphore(name))

        ring = ctx.enter_context(nc.psum_tensor("ring", [P, 6, 512], F32))
        bank6 = ctx.enter_context(nc.psum_tensor("bank6", [P, 512], F32))
        bank7 = ctx.enter_context(nc.psum_tensor("bank7", [P, 512], F32))

        common = sb("common", [P, COMMON_W])
        region_a = sb("region_a", [P, REGION_A])
        region_b = sb("region_b", [P, REGION_B])
        identb = sb("identb", [P, P], BF16)
        maskb = sb("maskb", [P, 2, SEQ], BF16)
        maskTb = sb("maskTb", [P, 2, SEQ], BF16)
        x = sb("x", [P, TILES, P])
        xn = sb("xn", [P, TILES, P])
        xT = sb("xT", [P, BATCH * SEQ + SEQ])
        z = sb("z", [P, TILES, P])
        stats = sb("stats", [P, TILES, 6])
        mv = sb("mv", [P, TILES, 2])
        ve = sb("ve", [P, TILES])
        sd = sb("sd", [P, TILES])
        rs = sb("rs", [P, TILES])
        nt = sb("nt", [P, TILES])
        work = sb("work", [P, 11008])
        y = work[:, 0:TILES * P].rearrange("p (t c) -> p t c", t=TILES)

        def col(region, plan, name, a=0, n=None):
            at, width = plan[name]
            n = width - a if n is None else n
            return region[:, at + a:at + a + n]

        ident = col(common, COMMON, "ident")
        ones = col(common, COMMON, "ones")

        loaded = [sem(f"loaded{i}") for i in range(6)]
        stored = sem("stored")
        phase_end = sem("phase_end")
        dve_done = sem("dve_done")
        act_done = sem("act_done")
        pool_done = sem("pool_done")
        pe_out = sem("pe_out")
        dve_out = sem("dve_out")
        act_out = sem("act_out")
        xb_ready = sem("xb_ready")
        proj_done = sem("proj_done")
        qk_evac = sem("qk_evac")
        v_evac = sem("v_evac")
        z_ready = sem("z_ready")
        t_done = sem("t_done")
        tev_dve = sem("tev_dve")
        tev_act = sem("tev_act")
        s1_done = sem("s1_done")
        red_done = sem("red_done")
        m_ready = sem("m_ready")
        t2_done = sem("t2_done")
        q2_evac = sem("q2_evac")
        s2_done = sem("s2_done")
        exp_done = sem("exp_done")
        av_done = sem("av_done")
        av_evac = sem("av_evac")
        tr_done = sem("tr_done")
        onorm_done = sem("onorm_done")
        ot_done = sem("ot_done")
        ont_evac = sem("ont_evac")
        outp_done = sem("outp_done")
        x_added = sem("x_added")
        up_done = sem("up_done")
        gate_done = sem("gate_done")
        h_ready = sem("h_ready")
        y_done = sem("y_done")
        y_added = sem("y_added")

        class Own:

            def __init__(self, s):
                self.s, self.n, self.i, self.per = s, 0, None, 0

            def enter(self, i, per):
                self.i, self.per, self.at = i, per, self.n

            def leave(self, trips):
                assert self.n - self.at == self.per, (self.n - self.at, self.per)
                self.n = self.at + self.per * trips
                self.i = None

            def inc(self, ins):
                self.n += 1
                ins.then_inc(self.s, 1)
                return self.n

            def wait(self, eng):
                eng.wait_ge(self.s, self.n if self.i is None else self.i * self.per + self.n)

        USES = ["T0", "T1", "S1_0", "S1_1"]
        for p in range(PAIRS):
            if p + 2 < PAIRS:
                USES.append(f"S1_{p + 2}")
            USES.append(f"S2_{p}")
        assert len(USES) % 3 == 0

        def slot_of(use):
            return 2 * (USES.index(use) % 3)

        def carve():
            at = [0]

            def take(n):
                a = at[0]
                at[0] += n
                assert at[0] <= 11008, at[0]
                return work[:, a:a + n]
            return take

        take = carve()
        xb = take(2 * SEQ).rearrange("p (b n) -> p b n", b=2)
        qkf = take(2 * 512).rearrange("p (b n) -> p b n", b=2)
        res1 = take(512)
        res2 = take(512)
        Zb = [sb(f"Z{b}", [P, 2, TPB, HEADS, SLOT], BF16) for b in range(2)]
        qkT = sb("qkT", [P, PAIRS, 512], BF16)
        q2T = sb("q2T", [P, 2, SEQ], BF16)
        Vaug = sb("Vaug", [P, 2, TPB, HEADS * 32])
        PT = take(2 * 1024).rearrange("p (r n) -> p r n", r=2)
        mrow = sb("mrow", [P, PAIRS, 4])
        avs = take(512)
        rec = sb("rec", [P, 32])
        onorm = take(SEQ).rearrange("p (s n) -> p s n", s=2)
        onT = take(SEQ)

        ringb = ring[:, :, :].bitcast(BF16)
        bank7b = bank7[:, :].bitcast(BF16)

        SC = float(HD) ** -0.5
        r3 = sb("r3", [P, 384 + 256])
        ATT = [
            dict(w=col(region_a, PACK0, "wqkv"), bias=col(region_a, PACK0, "bqk"), bv=col(region_a, PACK0, "bv"),
                 wo=col(region_a, PACK0, "wo"), bo=col(region_a, PACK0, "bo"), causal=False, src=x, dst=x),
            dict(w=col(region_b, PACK1, "wqkv"), bias=None, bv=None,
                 wo=col(region_b, PACK1, "wo"), bo=None, causal=True, src=x, dst=x),
            dict(w=r3[:, 0:384], bias=r3[:, 384:640], bv=col(region_b, PACK3, "bv"),
                 wo=col(region_b, PACK3, "wo"), bo=col(region_b, PACK3, "bo"), causal=False, src=x, dst=x),
            dict(w=col(region_b, PACK3, "wqkv2"), bias=None, bv=None,
                 wo=col(region_b, PACK3, "wo2"), bo=None, causal=False, src=xn, dst=z),
        ]

        def expert(region, plan, n, f, gated, act):
            return dict(n=n, f=f // P, gated=gated, act=act, region=region, plan=plan)

        MOE = [expert(region_a, PACK0, L0E, L0F, False, ACT.Gelu),
               expert(region_b, PACK1, L1E, L1F, True, ACT.Silu),
               expert(region_b, PACK3, L3E, L3F, False, ACT.Gelu_apprx_tanh)]

        lg = sb("lg", [P, TILES, 16])
        lg2 = sb("lg2", [P, TILES, 16])
        cand = sb("cand", [P, TILES, 16])
        oh = sb("oh", [P, TILES, 16])
        gate = sb("gate", [P, TILES, 16])
        gateT = sb("gateT", [16, BATCH * SEQ])
        mx = sb("mx", [P, 4, TILES])
        take = carve()
        hbuf = take(3 * 512).rearrange("p (r n) -> p r n", r=3)
        sgate = take(3 * 512).rearrange("p (r n) -> p r n", r=3)

        block = ctx.enter_context(nc.Block())
        def fence(eng, st):
            st["fence"] += 1
            eng.drain().then_inc(phase_end, 1)
            eng.wait_ge(phase_end, 4 * st["fence"])

        def norm_dve(dve, own, c, src, dst, rms, eps, affine):
            g = nc.vector
            for t in range(TILES):
                own.inc(g.bn_stats(stats[:, t, :], src[:, t, :]))
            own.wait(dve)
            for t in range(TILES):
                own.inc(g.bn_aggr(mv[:, t, :], stats[:, t, :]))
            own.wait(dve)
            if rms:
                own.inc(g.tensor_tensor(nt[:, :], mv[:, :, 0], mv[:, :, 0], ALU.mult))
                own.wait(dve)
                own.inc(g.tensor_tensor(nt[:, :], nt[:, :], mv[:, :, 1], ALU.add))
                own.wait(dve)
                g.tensor_scalar(ve[:, :], nt[:, :], eps, None, ALU.add).then_inc(dve_out, 1)
            else:
                g.tensor_scalar(ve[:, :], mv[:, :, 1], eps, None, ALU.add).then_inc(dve_out, 1)
            c["dve_out"] += 1
            dve.wait_ge(act_out, c["act_out"] + 1)
            c["act_out"] += 1
            own.inc(g.reciprocal(rs[:, :], sd[:, :]))
            own.wait(dve)
            own.inc(g.tensor_tensor(nt[:, :], ve[:, :], rs[:, :], ALU.mult))
            own.wait(dve)
            own.inc(g.tensor_tensor(nt[:, :], nt[:, :], rs[:, :], ALU.mult))
            own.wait(dve)
            own.inc(g.tensor_scalar(nt[:, :], nt[:, :], -0.5, 1.5, ALU.mult, ALU.add))
            own.wait(dve)
            own.inc(g.tensor_tensor(rs[:, :], rs[:, :], nt[:, :], ALU.mult))
            own.wait(dve)
            for t in range(TILES):
                if rms:
                    ins = g.tensor_scalar(dst[:, t, :], src[:, t, :], rs[:, t:t + 1], None, ALU.mult)
                else:
                    ins = g.tensor_scalar(dst[:, t, :], src[:, t, :], mv[:, t, 0:1], rs[:, t:t + 1],
                                          ALU.subtract, ALU.mult)
                if t % 4 == 3:
                    ins.then_inc(dve_out, 1)
                    c["dve_out"] += 1
            for q in (1, 3):
                dve.wait_ge(pe_out, c["pe_out"] + q + 1)
                copy_T(g, q, affine)
            c["pe_out"] += 4

        def copy_T(g, q, affine):
            dst = xT[:, 512 * q:512 * q + 512]
            if affine is None:
                g.tensor_copy(dst, ring[:, q, :])
            elif affine[1] is None:
                g.tensor_scalar(dst, ring[:, q, :], affine[0], None, ALU.mult)
            else:
                g.tensor_scalar(dst, ring[:, q, :], affine[0], affine[1], ALU.mult, ALU.add)

        def norm_act(act, c, affine):
            act.wait_ge(dve_out, c["dve_out"] + 1)
            nc.scalar.activation(sd[:, :], ve[:, :], ACT.Sqrt).then_inc(act_out, 1)
            c["dve_out"] += 5
            c["act_out"] += 1
            for q in (0, 2):
                act.wait_ge(pe_out, c["pe_out"] + q + 1)
                dst = xT[:, 512 * q:512 * q + 512]
                if affine is None:
                    nc.scalar.activation(dst, ring[:, q, :], ACT.Copy)
                elif affine[1] is None:
                    nc.scalar.activation(dst, ring[:, q, :], ACT.Identity, scale=affine[0])
                else:
                    nc.scalar.activation(dst, ring[:, q, :], ACT.Identity, scale=affine[0], bias=affine[1])
            c["pe_out"] += 4

        def norm_pe(pe, c, dst):
            for t in range(TILES):
                if t % 4 == 0:
                    pe.wait_ge(dve_out, c["dve_out"] + 2 + t // 4)
                ins = nc.tensor.transpose(ring[:, t // 4, (t % 4) * P:(t % 4 + 1) * P], dst[:, t, :], ident)
                if t % 4 == 3:
                    ins.then_inc(pe_out, 1)
            c["dve_out"] += 5
            c["act_out"] += 1
            c["pe_out"] += 4

        def norm_pool(c):
            c["dve_out"] += 5
            c["act_out"] += 1
            c["pe_out"] += 4

        def pro_pe(pe, a, b, par, t):
            A = ATT[a]
            n = 9 * a + b
            if t == 0:
                pe.wait_ge(xb_ready, n + 1)
            pe.wait_ge(v_evac, 1 + 2 * n + t)
            pe.wait_ge(qk_evac, 1 + 2 * n + t)
            nc.tensor.matmul(bank7[:, 0:384], xb[:, par, t * P:(t + 1) * P], A["w"],
                             start=True, stop=True).then_inc(proj_done, 1)

        def pro_dve(dve, a, b, par, t, first=False):
            A = ATT[a]
            n = 9 * a + b
            if t == 0 and not first:
                dve.wait_ge(z_ready, 1 + n - 1)
            dve.wait_ge(proj_done, 1 + 2 * n + t + 1)
            dst = qkf[:, par, :].rearrange("p (w s c) -> p w s c", w=2, s=2)[:, :, t, :]
            src = bank7[:, 0:256].rearrange("p (w c) -> p w c", w=2)
            if A["bias"] is None:
                nc.vector.tensor_copy(dst, src).then_inc(qk_evac, 1)
            else:
                nc.vector.tensor_tensor(dst, src, A["bias"].rearrange("p (w c) -> p w c", w=2),
                                        ALU.add).then_inc(qk_evac, 1)

        def pro_act(act, a, b, par, t, first=False):
            n = 9 * a + b
            if t == 0 and not first:
                act.wait_ge(av_done, 1 + 8 * (8 * a + b - 1))
            act.wait_ge(qk_evac, 1 + 2 * n + t + 1)
            nc.scalar.activation(Vaug[:, par, t, :].rearrange("p (h c) -> p h c", c=32)[:, :, 0:HD],
                                 bank7[:, 256:384].rearrange("p (h c) -> p h c", c=HD),
                                 ACT.Copy).then_inc(v_evac, 1)

        def pro_pool(pool, own, a, b, par, first=False):
            n = 9 * a + b
            g = nc.gpsimd
            if not first:
                pool.wait_ge(proj_done, 1 + 2 * (n - 1))
            g.tensor_copy(xb[:, par, :], xT[:, bass.ds(b * SEQ, SEQ)]).then_inc(xb_ready, 1)
            pool.wait_ge(qk_evac, 1 + 2 * n + 2)
            if not first:
                pool.wait_ge(t2_done, 1 + 8 * (8 * a + b - 1))
            Z = Zb[par]
            rows = qkf[:, par, :].rearrange("p (w r d) -> p w r d", w=2, d=HD)
            r1 = res1.rearrange("p (w r d) -> p w r d", w=2, d=HD)
            r2 = res2.rearrange("p (w r d) -> p w r d", w=2, d=HD)
            zs = Z[:, :, :, :, :].rearrange("p w t h s -> p w (t h) s")

            def put(w, src, first_slot, step, count):
                R = TPB * HEADS
                if count == 1:
                    dst = zs[:, w, :, first_slot * HD:(first_slot + 1) * HD]
                    return own.inc(g.tensor_copy(dst, src))
                dst = zs[:, w, :, 0:48].rearrange("p r (s d) -> p r s d", d=HD)[
                    :, :, first_slot:first_slot + step * (count - 1) + 1:step, :]
                return own.inc(g.tensor_copy(dst, src.unsqueeze(2).to_broadcast([P, R, count, HD])))

            put(0, rows[:, 0], 0, 1, 3)
            put(1, rows[:, 1], 0, 3, 2)
            put(1, rows[:, 1], 5, 1, 1)
            own.wait(pool)
            for w in range(2):
                own.inc(g.tensor_tensor(r1[:, w], rows[:, w], zs[:, w, :, 0:HD], ALU.subtract))
            own.wait(pool)
            put(0, r1[:, 0], 3, 1, 2)
            put(1, r1[:, 1], 1, 3, 2)
            own.wait(pool)
            own.inc(g.tensor_tensor(r2[:, 0], r1[:, 0], zs[:, 0, :, 3 * HD:4 * HD], ALU.subtract))
            own.inc(g.tensor_tensor(r2[:, 1], r1[:, 1], zs[:, 1, :, HD:2 * HD], ALU.subtract))
            own.wait(pool)
            put(0, r2[:, 0], 5, 1, 1)
            put(1, r2[:, 1], 2, 1, 1)
            own.wait(pool)
            g.tensor_copy(res2[:, 0:1], res1[:, 0:1]).then_inc(z_ready, 1)

        def batch_pe(pe, a, b, par):
            A = ATT[a]
            B = 8 * a + b
            Z = Zb[par]
            kT = lambda p, h: qkT[SLOT * h:SLOT * h + SHIFTED_ROWS, p, 256:512]

            def slot_free(use):
                u = USES.index(use)
                if u < 3:
                    if use == "T0":
                        pe.wait_ge(red_done, 1 + 8 * B)
                    pe.wait_ge(exp_done, 1 + 8 * B)
                    return
                was = USES[u - 3]
                if was[0] == "T":
                    pass
                elif was[:2] == "S1":
                    pe.wait_ge(red_done, 1 + 8 * B + int(was[3:]) + 1)
                else:
                    pe.wait_ge(exp_done, 1 + 8 * B + int(was[3:]) + 1)

            def T(h):
                slot_free(f"T{h}")
                s = slot_of(f"T{h}")
                if h == 0:
                    pe.wait_ge(z_ready, 1 + 9 * a + b + 1)
                for p in range(4):
                    for w in range(2):
                        for t in range(TPB):
                            ins = nc.tensor.transpose(
                                ringb[:, s + p // 2, (p % 2) * 512 + w * 256 + t * P:(p % 2) * 512 + w * 256 + (t + 1) * P],
                                Z[:, w, t, 8 * h + 2 * p:8 * h + 2 * p + 2, :], identb[:, :])
                ins.then_inc(t_done, 1)

            def S1(p):
                slot_free(f"S1_{p}")
                s = slot_of(f"S1_{p}")
                if p < 3:
                    pe.wait_ge(tev_dve, 2 * B + 1 + p // 2)
                    if p > 0:
                        pe.wait_ge(tev_act, 2 * B + 1 + p // 2)
                for h in range(2):
                    rows = slice(SLOT * h, SLOT * h + SCORE_ROWS)
                    for t in range(TPB):
                        if A["causal"]:
                            nc.tensor.matmul(ring[:, s + h, t * SEQ:(t + 1) * SEQ], identb[:, :], maskb[:, t, :],
                                             start=True, stop=False)
                        ins = nc.tensor.matmul(ring[:, s + h, t * SEQ:(t + 1) * SEQ], qkT[rows, p, t * P:(t + 1) * P],
                                               qkT[rows, p, 256:512], start=not A["causal"], stop=True)
                ins.then_inc(s1_done, 1)

            def T2(p):
                pe.wait_ge(m_ready, 8 * B + p + 1)
                pe.wait_ge(q2_evac, 1 + 8 * B + p)
                if p == 0:
                    pe.wait_ge(v_evac, 1 + 2 * (9 * a + b + 1) + 2)
                for t in range(TPB):
                    ins = nc.tensor.transpose(bank7b[:, t * P:(t + 1) * P], Z[:, 0, t, 2 * p:2 * p + 2, :], identb[:, :])
                ins.then_inc(t2_done, 1)

            def S2(p):
                slot_free(f"S2_{p}")
                s = slot_of(f"S2_{p}")
                pe.wait_ge(q2_evac, 1 + 8 * B + p + 1)
                for h in range(2):
                    rows = slice(SLOT * h, SLOT * h + SHIFTED_ROWS)
                    for t in range(TPB):
                        if A["causal"]:
                            nc.tensor.matmul(ring[:, s + h, t * SEQ:(t + 1) * SEQ], identb[:, :], maskTb[:, t, :],
                                             start=True, stop=False)
                        ins = nc.tensor.matmul(ring[:, s + h, t * SEQ:(t + 1) * SEQ],
                                               qkT[rows, p, 256 + t * P:256 + (t + 1) * P],
                                               q2T[rows, p % 2, :], start=not A["causal"], stop=True)
                ins.then_inc(s2_done, 1)

            def AV(p):
                pe.wait_ge(exp_done, 1 + 8 * B + p + 1)
                if p == 0:
                    pe.wait_ge(v_evac, 1 + 2 * (9 * a + b) + 2)
                    pe.wait_ge(x_added, 1 + B)
                if p == 4:
                    pe.wait_ge(onorm_done, 1 + 2 * B + 1)
                for h in range(2):
                    j = 2 * (p % 2) + h
                    g = (p // 2) % 2
                    for t in range(TPB):
                        head = 2 * p + h
                        ins = nc.tensor.matmul(bank6[32 * j:32 * j + 32, g * SEQ:(g + 1) * SEQ],
                                               Vaug[:, par, t, 32 * head:32 * head + 32],
                                               PT[:, p % 2, (2 * h + t) * SEQ:(2 * h + t + 1) * SEQ],
                                               start=(t == 0), stop=(t == TPB - 1))
                ins.then_inc(av_done, 1)

            def TR(hf):
                pe.wait_ge(av_evac, 2 * B + hf + 1)
                for t in range(TPB):
                    for g in range(2):
                        ins = nc.tensor.transpose(bank6[:, (2 * t + g) * P:(2 * t + g + 1) * P],
                                                  avs[:, g * SEQ + t * P:g * SEQ + (t + 1) * P], ident)
                ins.then_inc(tr_done, 1)

            T(0)
            T(1)
            pro_pe(pe, a, b + 1, 1 - par, 0)
            S1(0)
            S1(1)
            pro_pe(pe, a, b + 1, 1 - par, 1)
            T2(0)
            for p in range(PAIRS):
                if p + 2 < PAIRS:
                    S1(p + 2)
                if p + 1 < PAIRS:
                    T2(p + 1)
                S2(p)
                if p == 5:
                    TR(0)
                if p >= 1:
                    AV(p - 1)
            AV(PAIRS - 1)
            TR(1)
            pe.wait_ge(onorm_done, 1 + 2 * B + 2)
            for t in range(TPB):
                ins = nc.tensor.transpose(bank6[:, t * P:(t + 1) * P], onorm[:, t, :], ident)
            ins.then_inc(ot_done, 1)
            pe.wait_ge(ont_evac, B + 1)
            for t in range(TPB):
                ins = nc.tensor.matmul(bank6[:, t * P:(t + 1) * P], onT[:, t * P:(t + 1) * P], A["wo"],
                                       start=True, stop=A["bo"] is None)
                if A["bo"] is not None:
                    ins = nc.tensor.matmul(bank6[:, t * P:(t + 1) * P], ones[0:1, :], A["bo"][0:1, :],
                                           start=False, stop=True)
            ins.then_inc(outp_done, 1)

        def batch_dve(dve, own, a, b, par):
            A = ATT[a]
            B = 8 * a + b
            g = nc.vector
            Z = Zb[par]

            def tev(h):
                dve.wait_ge(t_done, 2 * B + h + 1)
                s = slot_of(f"T{h}")
                g.tensor_copy(qkT[:, 4 * h:4 * h + 2, :], ringb[:, s, :].rearrange("p (a n) -> p a n", a=2)
                              ).then_inc(tev_dve, 1)

            def red(p):
                s = slot_of(f"S1_{p}")
                dve.wait_ge(s1_done, 8 * B + p + 1)
                g.tensor_reduce(mrow[:, p, :], ring[:, s:s + 2, :].rearrange("p h (t n) -> p (h t) n", t=2),
                                AX_X, ALU.max).then_inc(red_done, 1)
                dve.wait_ge(red_done, 1 + 8 * B + p + 1)
                m = mrow[:, p, :].rearrange("p (h t) -> p h t", h=2)
                zc = lambda r: Z[:, 0, :, 2 * p:2 * p + 2, MAXROW + r].rearrange("p t h -> p h t")
                own.inc(g.tensor_copy(zc(0), m))
                own.wait(dve)
                g.tensor_tensor(zc(1), m, zc(0), ALU.subtract).then_inc(m_ready, 1)

            def norm(hf):
                dve.wait_ge(tr_done, 1 + 2 * B + hf + 1)
                v = bank6[:, :].rearrange("p (r c) -> p r c", c=32)
                own.inc(g.reciprocal(rec[:, 0:16], v[:, :, HD]))
                own.wait(dve)
                if hf == 0:
                    dve.wait_ge(ot_done, 1 + B)
                g.tensor_tensor(onorm[:, :, 64 * hf:64 * hf + 64].rearrange("p t (r d) -> p t r d", d=HD),
                                v[:, :, 0:HD].rearrange("p (t r) d -> p t r d", t=2),
                                rec[:, 0:16].rearrange("p (t r) -> p t r", t=2).unsqueeze(3).to_broadcast([P, 2, 8, HD]),
                                ALU.mult).then_inc(onorm_done, 1)

            tev(0)
            tev(1)
            pro_dve(dve, a, b + 1, 1 - par, 0)
            red(0)
            pro_dve(dve, a, b + 1, 1 - par, 1)
            red(1)
            for p in range(PAIRS):
                if p + 2 < PAIRS:
                    red(p + 2)
                if p == 5:
                    norm(0)
            norm(1)
            dve.wait_ge(outp_done, 1 + B + 1)
            g.tensor_tensor(A["dst"][:, bass.ds(2 * b, 2), :], A["src"][:, bass.ds(2 * b, 2), :],
                            bank6[:, 0:256].rearrange("p (t c) -> p t c", t=2), ALU.add).then_inc(x_added, 1)

        DVE_PER_BATCH = PAIRS + 2

        def batch_act(act, a, b, par):
            A = ATT[a]
            B = 8 * a + b
            g = nc.scalar

            def tev(h):
                act.wait_ge(t_done, 2 * B + h + 1)
                s = slot_of(f"T{h}")
                g.activation(qkT[:, 4 * h + 2:4 * h + 4, :], ringb[:, s + 1, :].rearrange("p (a n) -> p a n", a=2),
                             ACT.Copy).then_inc(tev_act, 1)

            def q2(p):
                act.wait_ge(t2_done, 1 + 8 * B + p + 1)
                act.wait_ge(s2_done, 1 + 8 * B + max(p - 1, 0))
                g.activation(q2T[:, p % 2, :], bank7b[:, 0:256], ACT.Copy).then_inc(q2_evac, 1)

            def ex(p):
                s = slot_of(f"S2_{p}")
                act.wait_ge(s2_done, 1 + 8 * B + p + 1)
                act.wait_ge(av_done, 1 + 8 * B + max(p - 1, 0))
                g.activation(PT[:, p % 2, :], ring[:, s:s + 2, :].rearrange("p h n -> p (h n)"), ACT.Exp,
                             scale=SC).then_inc(exp_done, 1)

            def avev(hf):
                act.wait_ge(av_done, 1 + 8 * B + 4 * hf + 4)
                act.wait_ge(tr_done, 1 + 2 * B + hf)
                g.activation(avs, bank6[:, :], ACT.Copy).then_inc(av_evac, 1)

            tev(0)
            tev(1)
            pro_act(act, a, b + 1, 1 - par, 0)
            pro_act(act, a, b + 1, 1 - par, 1)
            q2(0)
            for p in range(PAIRS):
                if p + 1 < PAIRS:
                    q2(p + 1)
                if p == 5:
                    avev(0)
                ex(p)
            avev(1)
            act.wait_ge(ot_done, 1 + B + 1)
            act.wait_ge(outp_done, 1 + B)
            if A["bv"] is None:
                g.activation(onT, bank6[:, 0:256], ACT.Copy).then_inc(ont_evac, 1)
            else:
                g.activation(onT, bank6[:, 0:256], ACT.Identity, bias=A["bv"]).then_inc(ont_evac, 1)

        def attention_pe(pe, a):
            pro_pe(pe, a, 0, 0, 0)
            pro_pe(pe, a, 0, 0, 1)
            with pe.Fori(0, BATCH // 2) as i:
                for par in range(2):
                    batch_pe(pe, a, 2 * i + par, par)

        def attention_dve(dve, own, a):
            pro_dve(dve, a, 0, 0, 0, True)
            pro_dve(dve, a, 0, 0, 1, True)
            with dve.Fori(0, BATCH // 2) as i:
                own.enter(i, 2 * DVE_PER_BATCH)
                for par in range(2):
                    batch_dve(dve, own, a, 2 * i + par, par)
                own.leave(BATCH // 2)

        def attention_act(act, a):
            pro_act(act, a, 0, 0, 0, True)
            pro_act(act, a, 0, 0, 1, True)
            with act.Fori(0, BATCH // 2) as i:
                for par in range(2):
                    batch_act(act, a, 2 * i + par, par)

        def attention_pool(pool, own, a):
            pro_pool(pool, own, a, 0, 0, True)
            for b in range(1, BATCH + 1):
                pro_pool(pool, own, a, b, b % 2)

        def new_counts():
            return dict(dve_out=0, act_out=0, pe_out=0, fence=0)


        def bcast(v, width):
            return v.unsqueeze(2).to_broadcast([P, TILES, width])

        def router_pe(pe, c, m):
            M = MOE[m]
            E = M["n"]
            for t in range(TILES):
                ins = nc.tensor.matmul(bank7[:, t * E:(t + 1) * E], xT[:, t * P:(t + 1) * P],
                                       col(M["region"], M["plan"], "router"), start=True, stop=True)
            ins.then_inc(pe_out, 1)
            c["pe_out"] += 1
            if m == 0:
                c["dve_out"] += 2
                c["act_out"] += 1
                pe.wait_ge(dve_out, c["dve_out"])
                for t in range(TILES):
                    ins = nc.tensor.transpose(ring[0:E, t // 4, (t % 4) * P:(t % 4 + 1) * P], gate[:, t, 0:E], ident)
                ins.then_inc(pe_out, 1)
                pe.wait_ge(act_out, c["act_out"] + 1)
                for t in range(TILES):
                    ins = nc.tensor.matmul(ring[:, t // 4, (t % 4) * P:(t % 4 + 1) * P], gateT[0:E, t * P:(t + 1) * P],
                                           col(region_a, PACK0, "b2")[0:E, :], start=True, stop=True)
                ins.then_inc(pe_out, 1)
                c["pe_out"] += 2
                c["act_out"] += 1
                c["dve_out"] += 1
                pe.wait_ge(dve_out, c["dve_out"])
            elif m == 1:
                c["dve_out"] += 1
                c["act_out"] += 1

        def router_dve(dve, own, c, m):
            M = MOE[m]
            E = M["n"]
            g = nc.vector
            L, L2, C, O, W = (v[:, :, 0:E] for v in (lg, lg2, cand, oh, gate))
            tie = col(common, COMMON, "tie", 0, E)
            tie = tie.unsqueeze(1).to_broadcast([P, TILES, E])

            def step(ins):
                own.inc(ins)
                own.wait(dve)

            def choose(src, top, first):
                step(g.tensor_reduce(mx[:, top, :], src, AX_X, ALU.max))
                step(g.tensor_tensor(C, src, bcast(mx[:, top, :], E), ALU.is_equal))
                step(g.tensor_tensor(C, C, tie, ALU.mult))
                step(g.tensor_reduce(mx[:, 3, :], C, AX_X, ALU.max))
                step(g.tensor_tensor(first, C, bcast(mx[:, 3, :], E), ALU.is_equal))

            dve.wait_ge(pe_out, c["pe_out"] + 1)
            c["pe_out"] += 1
            src = bank7[:, 0:TILES * E].rearrange("p (t e) -> p t e", e=E)
            if m == 2:
                rb = col(region_b, PACK3, "rbias").unsqueeze(1).to_broadcast([P, TILES, E])
                step(g.tensor_tensor(L, src, rb, ALU.add))
                choose(L, 0, W)
                step(g.tensor_tensor(x[:, :, :], x[:, :, :], z[:, :, :], ALU.add))
            if m == 0:
                step(g.tensor_copy(L, src))
                choose(L, 0, O)
                g.tensor_tensor(L2, L, bcast(mx[:, 0, :], E), ALU.subtract).then_inc(dve_out, 1)
                dve.wait_ge(act_out, c["act_out"] + 1)
                step(g.tensor_reduce(mx[:, 1, :], L2, AX_X, ALU.add))
                step(g.reciprocal(mx[:, 2, :], mx[:, 1, :]))
                g.tensor_tensor(W, O, bcast(mx[:, 2, :], E), ALU.mult).then_inc(dve_out, 1)
                dve.wait_ge(pe_out, c["pe_out"] + 2)
                for q in range(4):
                    ins = g.tensor_tensor(x[:, 4 * q:4 * q + 4, :], x[:, 4 * q:4 * q + 4, :],
                                          ring[:, q, :].rearrange("p (t c) -> p t c", t=4), ALU.add)
                ins.then_inc(dve_out, 1)
                c["pe_out"] += 2
                c["dve_out"] += 3
                dve.wait_ge(dve_out, c["dve_out"])
                c["act_out"] += 2
            if m == 1:
                step(g.tensor_copy(L, src))
                choose(L, 0, O)
                step(g.scalar_tensor_tensor(out=L2, in0=O, scalar=-3.0e38, in1=L, op0=ALU.mult, op1=ALU.add))
                choose(L2, 1, W)
                g.tensor_tensor(mx[:, 2, :], mx[:, 1, :], mx[:, 0, :], ALU.subtract).then_inc(dve_out, 1)
                dve.wait_ge(act_out, c["act_out"] + 1)
                step(g.tensor_scalar(mx[:, 0, :], mx[:, 2, :], 1.0, None, ALU.add))
                step(g.reciprocal(mx[:, 1, :], mx[:, 0, :]))
                step(g.tensor_tensor(mx[:, 2, :], mx[:, 2, :], mx[:, 1, :], ALU.mult))
                step(g.tensor_tensor(O, O, bcast(mx[:, 1, :], E), ALU.mult))
                step(g.tensor_tensor(W, W, bcast(mx[:, 2, :], E), ALU.mult))
                step(g.tensor_tensor(W, W, O, ALU.add))
                step(g.tensor_tensor(x[:, :, :], x[:, :, :], xn[:, :, :], ALU.add))
                c["dve_out"] += 1
                c["act_out"] += 1

        def router_act(act, c, m):
            E = MOE[m]["n"]
            c["pe_out"] += 1
            if m == 0:
                act.wait_ge(dve_out, c["dve_out"] + 1)
                nc.scalar.activation(lg2[:, :, 0:E], lg2[:, :, 0:E], ACT.Exp).then_inc(act_out, 1)
                act.wait_ge(pe_out, c["pe_out"] + 1)
                nc.scalar.activation(gateT[0:E, :], ring[0:E, 0:4, :].rearrange("p q n -> p (q n)"),
                                     ACT.Copy).then_inc(act_out, 1)
                c["dve_out"] += 3
                c["act_out"] += 2
                c["pe_out"] += 2
            elif m == 1:
                act.wait_ge(dve_out, c["dve_out"] + 1)
                nc.scalar.activation(mx[:, 2, :], mx[:, 2, :], ACT.Exp).then_inc(act_out, 1)
                c["dve_out"] += 1
                c["act_out"] += 1

        def router_pool(c, m):
            c["pe_out"] += 3 if m == 0 else 1
            c["dve_out"] += (3, 1, 0)[m]
            c["act_out"] += (2, 1, 0)[m]

        UNITS = [M["n"] * M["f"] for M in MOE]
        U0 = [4 * sum(UNITS[:m]) for m in range(3)]
        E0 = [4 * sum(M["n"] for M in MOE[:m]) for m in range(3)]
        HR = 4
        take = carve()
        hb = take(HR * 512).rearrange("p (r n) -> p r n", r=HR)
        sg = take(HR * 512).rearrange("p (r n) -> p r n", r=HR)

        def experts_pe(pe, m):
            M = MOE[m]
            n, f, gated = M["n"], M["f"], M["gated"]
            F = f * P * (2 if gated else 1)
            w1 = col(M["region"], M["plan"], "w1")
            w2 = col(M["region"], M["plan"], "w2")
            banks = 2 if gated else 4
            with pe.Fori(0, 4) as i:
                base = i * UNITS[m] + U0[m]

                def up(k):
                    e, fc = divmod(k, f)
                    pe.wait_ge(h_ready, 1 + base + max(k - banks + 1, 0))
                    rows = xT[:, bass.ds(i * 512, 512)]
                    if gated:
                        for part in range(2):
                            ins = nc.tensor.matmul(ring[:, 2 * (k % 2) + part, :],
                                                   w1[:, e * F + part * f * P + fc * P:e * F + part * f * P + fc * P + P],
                                                   rows, start=True, stop=True)
                    else:
                        ins = nc.tensor.matmul(ring[:, k % 4, :], w1[:, e * F + fc * P:e * F + fc * P + P], rows,
                                               start=True, stop=True)
                    ins.then_inc(up_done, 1)

                def down(k):
                    e, fc = divmod(k, f)
                    pe.wait_ge(h_ready, 1 + base + k + 1)
                    if fc == 0:
                        pe.wait_ge(y_added, 1 + i * n + E0[m] + max(e - 1, 0))
                    for t in range(4):
                        ins = nc.tensor.matmul(ring[:, 4 + e % 2, t * P:(t + 1) * P], hb[:, k % HR, t * P:(t + 1) * P],
                                               w2[:, (e * f + fc) * P:(e * f + fc + 1) * P],
                                               start=(fc == 0 and t == 0), stop=(fc == f - 1), skip_group_check=True)
                    ins.then_inc(y_done, 1)

                ahead = banks - 1 if gated else 2
                for k in range(ahead):
                    up(k)
                for k in range(n * f):
                    if k + ahead < n * f:
                        up(k + ahead)
                    down(k)

        def experts_act(act, m):
            M = MOE[m]
            n, f, gated = M["n"], M["f"], M["gated"]
            with act.Fori(0, 4) as i:
                base = i * UNITS[m] + U0[m]
                for k in range(n * f):
                    act.wait_ge(up_done, base + k + 1)
                    if gated:
                        act.wait_ge(h_ready, 1 + base + max(k - HR + 1, 0))
                        nc.scalar.activation(sg[:, k % HR, :], ring[:, 2 * (k % 2) + 1, :], M["act"]).then_inc(gate_done, 1)
                    else:
                        act.wait_ge(y_done, 1 + base + max(k - HR + 1, 0))
                        b = col(region_a, PACK0, "b1", k, 1) if m == 0 else None
                        if b is None:
                            ins = nc.scalar.activation(hb[:, k % HR, :], ring[:, k % 4, :], M["act"])
                        else:
                            ins = nc.scalar.activation(hb[:, k % HR, :], ring[:, k % 4, :], M["act"], bias=b)
                        ins.then_inc(h_ready, 1)

        def experts_dve(dve, m):
            M = MOE[m]
            n, f, gated = M["n"], M["f"], M["gated"]
            g = nc.vector
            with dve.Fori(0, 4) as i:
                base = i * UNITS[m] + U0[m]

                def add(e):
                    dve.wait_ge(y_done, 1 + base + e * f + f)
                    dve.wait_ge(y_added, 1 + i * n + E0[m] + e)
                    for t in range(4):
                        row = x[:, bass.ds(4 * i + t, 1), :]
                        ins = g.scalar_tensor_tensor(out=row, in0=ring[:, 4 + e % 2, t * P:(t + 1) * P].unsqueeze(1),
                                                     scalar=gate[:, bass.ds(4 * i + t, 1), e], in1=row,
                                                     op0=ALU.mult, op1=ALU.add)
                    ins.then_inc(y_added, 1)

                for k in range(n * f):
                    if gated:
                        dve.wait_ge(gate_done, i * UNITS[m] + k + 1)
                        dve.wait_ge(y_done, 1 + base + max(k - HR + 1, 0))
                        g.tensor_tensor(hb[:, k % HR, :], sg[:, k % HR, :], ring[:, 2 * (k % 2), :],
                                        ALU.mult).then_inc(h_ready, 1)
                    if k % f == 0 and k > 0:
                        add(k // f - 1)
                add(n - 1)

        take = carve()
        xc, qu, qv, kk, ap, t1, t2 = (take(512) for _ in range(7))
        vs, sgl, Pm, PTs, wv, wvT = (take(1024).rearrange("p (t n) -> p t n", t=4) for _ in range(6))
        neg_max = sb("neg_max", [P, 4])
        row_sum = sb("row_sum", [P, 4])
        row_rec = sb("row_rec", [P, 4])
        r_pe, r_dve, r_act, r_pool = (sem("rel_" + k) for k in ("pe", "dve", "act", "pool"))
        REL = dict(pe=["q", "k", "vg", "a", "scores", "PT", "av", "wvT", "res"],
                   dve=["k", "v", "rot", "ap", "max", "rec", "PT", "wv", "x"],
                   act=["qu", "qv", "silu", "exp", "wvT"], pool=["xc"])

        def rel_at(i, who, what, back=0):
            return i * len(REL[who]) + (REL[who].index(what) + 1 if not back else 0)

        def rel_pe(pe):
            R = lambda name: col(region_a, PACK2, name)
            mm = nc.tensor.matmul
            with pe.Fori(0, 4) as i:
                rows = xT[:, bass.ds(i * 512, 512)]
                pe.wait_ge(r_dve, 1 + i * 9)
                pe.wait_ge(r_act, 1 + i * 5)
                mm(ring[:, 0, :], R("wq"), rows, start=True, stop=True).then_inc(r_pe, 1)
                mm(ring[:, 1, :], R("wk"), rows, start=True, stop=True).then_inc(r_pe, 1)
                pe.wait_ge(r_pool, rel_at(i, "pool", "xc"))
                for t in range(4):
                    lhs = xc[:, t * P:(t + 1) * P]
                    mm(ring[:, 2 + t // 2, (t % 2) * 256:(t % 2) * 256 + 256], lhs, R("wvg")[:, 0:256], start=True, stop=True)
                    ins = mm(ring[:, 4 + t // 2, (t % 2) * 256:(t % 2) * 256 + 256], lhs, R("wvg")[:, 256:512],
                             start=True, stop=True)
                ins.then_inc(r_pe, 1)
                pe.wait_ge(r_act, 1 + rel_at(i, "act", "qv"))
                mm(bank6[:, :], R("wrT"), qv, start=True, stop=True)
                mm(bank7[:, :], R("wrTs"), qv, start=True, stop=True).then_inc(r_pe, 1)
                pe.wait_ge(r_dve, 1 + rel_at(i, "dve", "ap"))
                for b in range(2):
                    for t in range(2):
                        o = ring[:, b, t * 256:(t + 1) * 256]
                        here = slice(b * 256 + t * P, b * 256 + (t + 1) * P)
                        mm(o, identb[:, :], maskb[:, t, :], start=True, stop=False)
                        mm(o, qu[:, here], kk[:, b * 256:(b + 1) * 256], start=False, stop=False)
                        ins = mm(o, ap[:, here], R("pos"), start=False, stop=True)
                ins.then_inc(r_pe, 1)
                pe.wait_ge(r_act, 1 + rel_at(i, "act", "exp"))
                for b in range(2):
                    for j in range(2):
                        for t in range(2):
                            ins = nc.tensor.transpose(ring[:, 2 + b, j * 256 + t * P:j * 256 + (t + 1) * P],
                                                      Pm[:, 2 * b + t, j * P:(j + 1) * P], ident)
                ins.then_inc(r_pe, 1)
                pe.wait_ge(r_dve, 1 + rel_at(i, "dve", "PT"))
                for b in range(2):
                    for t in range(2):
                        for j in range(2):
                            ins = mm(ring[:, 4 + b, t * 256:(t + 1) * 256], PTs[:, 2 * b + j, t * P:(t + 1) * P],
                                     vs[:, 2 * b + j, :], start=(j == 0), stop=(j == 1))
                ins.then_inc(r_pe, 1)
                pe.wait_ge(r_dve, 1 + rel_at(i, "dve", "wv"))
                for t in range(4):
                    for j in range(2):
                        ins = nc.tensor.transpose(ring[:, t // 2, (t % 2) * 256 + j * P:(t % 2) * 256 + (j + 1) * P],
                                                  wv[:, t, j * P:(j + 1) * P], ident)
                ins.then_inc(r_pe, 1)
                pe.wait_ge(r_act, 1 + rel_at(i, "act", "wvT"))
                for t in range(4):
                    for j in range(2):
                        ins = mm(bank6[:, t * P:(t + 1) * P], wvT[:, t, j * P:(j + 1) * P], R("wo")[:, j * P:(j + 1) * P],
                                 start=(j == 0), stop=(j == 1))
                ins.then_inc(r_pe, 1)

        def rel_dve(dve, own):
            g = nc.vector
            R = lambda name: col(region_a, PACK2, name)
            two = lambda v: v.rearrange("p (b n) -> p b n", b=2)
            with dve.Fori(0, 4) as i:
                own.enter(i, 1)
                dve.wait_ge(r_pe, 1 + rel_at(i, "pe", "k"))
                g.tensor_copy(kk, ring[:, 1, :]).then_inc(r_dve, 1)
                dve.wait_ge(r_pe, 1 + rel_at(i, "pe", "vg"))
                g.tensor_copy(vs, ring[:, 2:4, :].rearrange("p q (t n) -> p (q t) n", t=2)).then_inc(r_dve, 1)
                dve.wait_ge(r_pe, 1 + rel_at(i, "pe", "a"))
                own.inc(g.tensor_tensor(two(t1), two(bank6[:, :]), R("rot_a").unsqueeze(1).to_broadcast([P, 2, SEQ]), ALU.mult))
                g.tensor_tensor(two(t2), two(bank7[:, :]), R("rot_b").unsqueeze(1).to_broadcast([P, 2, SEQ]),
                                ALU.mult).then_inc(r_dve, 1)
                own.wait(dve)
                dve.wait_ge(r_dve, 1 + rel_at(i, "dve", "rot"))
                g.tensor_tensor(ap, t1, t2, ALU.add).then_inc(r_dve, 1)
                dve.wait_ge(r_pe, 1 + rel_at(i, "pe", "scores"))
                g.tensor_reduce(neg_max[:, :], ring[:, 0:2, :].rearrange("p b (t n) -> p (b t) n", t=2), AX_X, ALU.max,
                                negate=True).then_inc(r_dve, 1)
                dve.wait_ge(r_act, 1 + rel_at(i, "act", "exp"))
                g.reciprocal(row_rec[:, :], row_sum[:, :]).then_inc(r_dve, 1)
                dve.wait_ge(r_pe, 1 + rel_at(i, "pe", "PT"))
                g.tensor_copy(PTs, ring[:, 2:4, :].rearrange("p q (t n) -> p (q t) n", t=2)).then_inc(r_dve, 1)
                dve.wait_ge(r_pe, 1 + rel_at(i, "pe", "av"))
                dve.wait_ge(r_act, 1 + rel_at(i, "act", "silu"))
                dve.wait_ge(r_dve, 1 + rel_at(i, "dve", "rec"))
                for t in range(4):
                    ins = g.scalar_tensor_tensor(out=wv[:, t, :], in0=ring[:, 4 + t // 2, (t % 2) * 256:(t % 2) * 256 + 256],
                                                 scalar=row_rec[:, t:t + 1], in1=sgl[:, t, :], op0=ALU.mult, op1=ALU.mult)
                ins.then_inc(r_dve, 1)
                dve.wait_ge(r_pe, 1 + rel_at(i, "pe", "res"))
                rows = x[:, bass.ds(4 * i, 4), :]
                g.tensor_tensor(rows, rows, bank6[:, :].rearrange("p (t c) -> p t c", t=4), ALU.add).then_inc(r_dve, 1)
                own.leave(4)

        def rel_act(act):
            g = nc.scalar
            R = lambda name: col(region_a, PACK2, name)
            with act.Fori(0, 4) as i:
                act.wait_ge(r_pe, 1 + rel_at(i, "pe", "q"))
                tau = float(P) ** -0.5
                g.activation(qu, ring[:, 0, :], ACT.Identity, scale=tau, bias=R("u")).then_inc(r_act, 1)
                g.activation(qv, ring[:, 0, :], ACT.Identity, scale=tau, bias=R("v")).then_inc(r_act, 1)
                act.wait_ge(r_pe, 1 + rel_at(i, "pe", "vg"))
                g.activation(sgl, ring[:, 4:6, :].rearrange("p q (t n) -> p (q t) n", t=2), ACT.Silu).then_inc(r_act, 1)
                act.wait_ge(r_dve, 1 + rel_at(i, "dve", "max"))
                for t in range(4):
                    ins = g.activation(Pm[:, t, :], ring[:, t // 2, (t % 2) * 256:(t % 2) * 256 + 256], ACT.Exp,
                                       bias=neg_max[:, t:t + 1], accum_out=row_sum[:, t:t + 1])
                ins.then_inc(r_act, 1)
                act.wait_ge(r_pe, 1 + rel_at(i, "pe", "wvT"))
                g.activation(wvT, ring[:, 0:2, :].rearrange("p q (t n) -> p (q t) n", t=2), ACT.Copy).then_inc(r_act, 1)

        def rel_pool(pool):
            for i in range(4):
                pool.wait_ge(r_pe, 1 + i * 9)
                nc.gpsimd.tensor_copy(xc, xT[:, bass.ds(i * 512, 512)]).then_inc(r_pool, 1)

        take = carve()
        H = take(BATCH * 512)
        Sel = take(2 * 1024).rearrange("p (b t n) -> p b t n", b=2, t=2)
        Gsel = take(2 * 1024).rearrange("p (b t n) -> p b t n", b=2, t=2)
        pr, cur0, cur1, cum, slot = (take(SEQ) for _ in range(5))
        xg = [sb(f"xg{b}", [P, TPB, P]) for b in range(2)]
        spread = sb("spread", [P, 2, 512], BF16)
        slotb = sb("slotb", [P, SEQ], BF16)
        spT = sb("spT", [P, 4, P])
        top8 = sb("top8", [P, 8])
        vals = sb("vals", [P, BATCH * 4])
        k1 = sb("k1", [P, 4])
        h12 = take(4 * SEQ).rearrange("p (r n) -> p r n", r=4)
        Hc = Gsel[:, :, 0, 0:512]
        hs = Gsel[:, :, 1, 0:512]
        ST = Sel
        g_pool, g_sel, g_val, g_rows, g_vals, g_H = (sem("g_" + k) for k in ("pool", "sel", "val", "rows", "vals", "H"))
        m_pe, m_act, m_dve = (sem("mlp_" + k) for k in ("pe", "act", "dve"))
        c_pool, c_tr, c_sb, c_hs, c_st, c_out, c_add = (sem("c_" + k) for k in
                                                        ("pool", "tr", "sb", "hs", "st", "out", "add"))

        def top_pe(pe, c):
            mm = nc.tensor.matmul
            router = col(region_a, PACK2, "router")
            for b in range(BATCH):
                ins = mm(bank6[:, 0:SEQ], router[:, 112 - 16 * b:240 - 16 * b], xT[:, b * SEQ:(b + 1) * SEQ],
                         start=(b == 0), stop=(b == BATCH - 1))
            ins.then_inc(pe_out, 1)
            pe.wait_ge(dve_out, c["dve_out"] + 2)
            for t in range(TPB):
                nc.tensor.transpose(bank7[:, t * P:(t + 1) * P], slot[:, t * P:(t + 1) * P], ident)
                ins = nc.tensor.transpose(bank7[:, (2 + t) * P:(3 + t) * P], pr[:, t * P:(t + 1) * P], ident)
            ins.then_inc(pe_out, 1)
            with pe.Fori(0, BATCH // 2) as i:
                for par in range(2):
                    b = 2 * i + par
                    pe.wait_ge(g_pool, b + 1)
                    pe.wait_ge(g_sel, b + 1)
                    pe.wait_ge(g_H, 1 + 2 * i)
                    for t in range(TPB):
                        ins = mm(ring[:, par, :], xg[par][:, t, :], Sel[:, par, t, :], start=(t == 0), stop=(t == TPB - 1))
                    ins.then_inc(g_rows, 1)
                    pe.wait_ge(g_val, b + 1)
                    for q in range(4):
                        for t in range(TPB):
                            ins = mm(ring[:, 2 + par, q:q + 1], Gsel[:, par, t, q * P:(q + 1) * P], ones[:, 0:1],
                                     start=(t == 0), stop=(t == TPB - 1))
                    ins.then_inc(g_rows, 1)
            Hv = H.rearrange("p (b e k) -> p b e k", b=BATCH, e=L2E)
            pe.wait_ge(g_H, 1 + BATCH)
            pe.wait_ge(g_vals, BATCH)
            for s in range(L2E + 2):
                for layer in range(3):
                    e = s - layer
                    if not 0 <= e < L2E:
                        continue
                    w = col(region_a, PACK2, f"w{layer + 1}", e * P, P)
                    o = ring[:, 2 * layer + e % 2, 0:SEQ]
                    if layer == 0:
                        if e >= 2:
                            pe.wait_ge(m_act, MLP_ACT.index((0, e - 2)) + 1)
                        rhs, o = Hv[:, :, e, :], o.rearrange("p (b k) -> p b k", b=BATCH)
                    else:
                        pe.wait_ge(m_act, MLP_ACT.index((layer - 1, e)) + 1)
                        if layer == 2 and e >= 2:
                            pe.wait_ge(m_dve, e - 1)
                        rhs = h12[:, 2 * (layer - 1) + e % 2, :]
                    mm(o, w, rhs, start=True, stop=True).then_inc(m_pe, 1)
            pe.wait_ge(m_dve, L2E)
            with pe.Fori(0, BATCH // 2) as i:
                for par in range(2):
                    b = 2 * i + par
                    pe.wait_ge(c_pool, b + 1)
                    pe.wait_ge(c_hs, 1 + 2 * i)
                    for q in range(4):
                        ins = nc.tensor.transpose(ring[:, par, q * P:(q + 1) * P], Hc[:, par, q * P:(q + 1) * P], ident)
                    ins.then_inc(c_tr, 1)
                    pe.wait_ge(c_st, 1 + 2 * i)
                    for q in range(4):
                        ins = mm(ring[:, 2 + 2 * par + q // 2, (q % 2) * SEQ:(q % 2 + 1) * SEQ],
                                 spread[:, par, q * P:(q + 1) * P], slotb[:, :], start=True, stop=True)
                    ins.then_inc(c_sb, 1)
                    pe.wait_ge(c_hs, 1 + b + 1)
                    pe.wait_ge(c_st, 1 + b + 1)
                    pe.wait_ge(c_add, 1 + 2 * i)
                    bank = (bank6, bank7)[par]
                    for t in range(TPB):
                        for q in range(4):
                            ins = mm(bank[:, t * P:(t + 1) * P], STv(par)[:, q, t * P:(t + 1) * P],
                                     hs[:, par, q * P:(q + 1) * P], start=(q == 0), stop=(q == 3))
                    ins.then_inc(c_out, 1)
            c["pe_out"] += 2
            c["dve_out"] += 2
            c["act_out"] += 2

        def STv(par):
            return ST[:, par, :, :].rearrange("p t (q n) -> p (t q) n", q=2)

        MLP_ORDER = [(s - layer, layer) for s in range(L2E + 2) for layer in range(3) if 0 <= s - layer < L2E]
        MLP_ACT = [(layer, e) for e, layer in MLP_ORDER if layer < 2]

        def top_dve(dve, own, c):
            g = nc.vector

            def step(ins):
                own.inc(ins)
                own.wait(dve)

            dve.wait_ge(pe_out, c["pe_out"] + 1)
            step(g.tensor_scalar(cur0, bank6[:, 0:SEQ], col(region_a, PACK2, "rb"), None, ALU.add))
            g.tensor_reduce(k1[:, 0:1], cur0, AX_X, ALU.max, negate=True).then_inc(dve_out, 1)
            dve.wait_ge(act_out, c["act_out"] + 1)
            step(g.reciprocal(k1[:, 2:3], k1[:, 1:2]))
            step(g.tensor_scalar(pr, cur1, k1[:, 2:3], None, ALU.mult))
            cur, nxt = pr, cur0
            for r in range(L2K // 8):
                step(g.max(top8[:, :], cur))
                step(g.match_replace(out=nxt, in_to_replace=top8[:, :], in_values=cur, imm_value=-1.0))
                cur, nxt = nxt, (cur1 if nxt is cur0 else cur0)
            taken = nxt
            step(g.tensor_scalar(taken, cur, 0.0, None, ALU.is_lt))
            step(g.tensor_tensor_scan(cum, col_ones(), taken, 0.0, ALU.mult, ALU.add))
            step(g.tensor_tensor(cum, cum, taken, ALU.mult))
            step(g.tensor_scalar(slotb[:, :], cum, -1.0, None, ALU.add))
            g.tensor_scalar(slot, cum, -1.0, None, ALU.add).then_inc(dve_out, 1)
            dve.wait_ge(act_out, c["act_out"] + 2)
            number = col(common, COMMON, "slot_no").unsqueeze(1).to_broadcast([P, L2E, L2K])
            with dve.Fori(0, BATCH // 2) as i:
                for par in range(2):
                    b = 2 * i + par
                    dve.wait_ge(g_rows, 1 + 4 * i)
                    for t in range(TPB):
                        of = spT[:, t, bass.ds(16 * b, 16)].unsqueeze(2).to_broadcast([P, L2E, L2K])
                        ins = g.tensor_tensor(Sel[:, par, t, :].rearrange("p (e k) -> p e k", e=L2E), of, number,
                                              ALU.is_equal)
                    ins.then_inc(g_sel, 1)
                    dve.wait_ge(g_sel, b + 1)
                    for t in range(TPB):
                        pt = spT[:, 2 + t, bass.ds(16 * b, 16)].unsqueeze(2).to_broadcast([P, L2E, L2K])
                        ins = g.tensor_tensor(Gsel[:, par, t, :].rearrange("p (e k) -> p e k", e=L2E),
                                              Sel[:, par, t, :].rearrange("p (e k) -> p e k", e=L2E), pt, ALU.mult)
                    ins.then_inc(g_val, 1)
                    dve.wait_ge(g_rows, 1 + 2 * b + 2)
                    g.tensor_copy(vals[:, bass.ds(4 * b, 4)], ring[:, 2 + par, 0:4]).then_inc(g_vals, 1)
            Hv = H.rearrange("p (b e k) -> p b e k", b=BATCH, e=L2E)
            for e in range(L2E):
                dve.wait_ge(m_pe, MLP_ORDER.index((e, 2)) + 1)
                g.tensor_scalar(Hv[:, :, e, :], ring[:, 4 + e % 2, 0:SEQ].rearrange("p (b k) -> p b k", b=BATCH),
                                col(region_a, PACK2, "b3", e, 1), None, ALU.add).then_inc(m_dve, 1)
            dve.wait_ge(g_vals, BATCH)
            with dve.Fori(0, BATCH // 2) as i:
                for par in range(2):
                    b = 2 * i + par
                    dve.wait_ge(c_tr, 1 + b + 1)
                    dve.wait_ge(c_out, 1 + 2 * i)
                    g.tensor_tensor(hs[:, par, :].rearrange("p (q n) -> p q n", q=4),
                                    ring[:, par, :].rearrange("p (q n) -> p q n", q=4),
                                    vals[:, bass.ds(4 * b, 4)].unsqueeze(2).to_broadcast([P, 4, P]),
                                    ALU.mult).then_inc(c_hs, 1)
                    dve.wait_ge(c_sb, 1 + b + 1)
                    g.tensor_scalar(STv(par), ring[:, 2 + 2 * par:4 + 2 * par, :].rearrange("p a (q n) -> p (a q) n", q=2),
                                    col(common, COMMON, "slot_of_row"), None, ALU.is_equal).then_inc(c_st, 1)
                    dve.wait_ge(c_out, 1 + b + 1)
                    rows = x[:, bass.ds(2 * b, 2), :]
                    g.tensor_tensor(rows, rows, (bank6, bank7)[par][:, 0:SEQ].rearrange("p (t c) -> p t c", t=2),
                                    ALU.add).then_inc(c_add, 1)
            c["pe_out"] += 2
            c["dve_out"] += 2
            c["act_out"] += 2

        def col_ones():
            return ones[:, 0:1].to_broadcast([P, SEQ])

        def top_act(act, c):
            g = nc.scalar
            act.wait_ge(dve_out, c["dve_out"] + 1)
            g.activation(cur1, cur0, ACT.Exp, bias=k1[:, 0:1], accum_out=k1[:, 1:2]).then_inc(act_out, 1)
            act.wait_ge(pe_out, c["pe_out"] + 2)
            g.activation(spT[:, :, :], bank7[:, :].rearrange("p (t n) -> p t n", t=4), ACT.Copy).then_inc(act_out, 1)
            with act.Fori(0, BATCH // 2) as i:
                for par in range(2):
                    b = 2 * i + par
                    act.wait_ge(g_rows, 1 + 2 * b + 1)
                    g.activation(H[:, bass.ds(b * 512, 512)], ring[:, par, :], ACT.Copy).then_inc(g_H, 1)
            for layer, e in MLP_ACT:
                act.wait_ge(m_pe, MLP_ORDER.index((e, layer)) + 1)
                if e >= 2:
                    act.wait_ge(m_pe, MLP_ORDER.index((e - 2, layer + 1)) + 1)
                g.activation(h12[:, 2 * layer + e % 2, :], ring[:, 2 * layer + e % 2, 0:SEQ], ACT.Relu,
                             bias=col(region_a, PACK2, f"b{layer + 1}", e, 1)).then_inc(m_act, 1)
            c["pe_out"] += 2
            c["dve_out"] += 2
            c["act_out"] += 2

        def top_pool(pool, c):
            g = nc.gpsimd
            for i in range(BATCH // 2):
                for par in range(2):
                    b = 2 * i + par
                    pool.wait_ge(g_rows, 1 + 4 * i)
                    g.tensor_copy(xg[par][:, :, :], xn[:, bass.ds(2 * b, 2), :]).then_inc(g_pool, 1)
            pool.wait_ge(m_dve, L2E)
            pool.wait_ge(g_rows, 1 + 2 * BATCH)
            for i in range(BATCH // 2):
                for par in range(2):
                    b = 2 * i + par
                    pool.wait_ge(c_tr, 1 + 2 * i)
                    pool.wait_ge(c_sb, 1 + 2 * i)
                    g.tensor_copy(spread[:, par, :].rearrange("p (e k) -> p e k", e=L2E),
                                  identb[:, bass.ds(16 * b, 16)].unsqueeze(2).to_broadcast([P, L2E, L2K]))
                    g.tensor_copy(Hc[:, par, :], H[:, bass.ds(b * 512, 512)]).then_inc(c_pool, 1)
            c["pe_out"] += 2
            c["dve_out"] += 2
            c["act_out"] += 2

        def fold_pe(pe, c):
            R = lambda name: col(region_b, PACK3, name)
            nc.tensor.matmul(bank6[:, 0:P], R("wqT"), R("rope"), start=True, stop=True)
            nc.tensor.matmul(bank6[:, P:2 * P], R("wkT"), R("rope"), start=True, stop=True)
            nc.tensor.matmul(bank6[:, 2 * P:3 * P], R("bq").to_broadcast([P, P]), R("rope"), start=True, stop=True)
            nc.tensor.matmul(bank6[:, 3 * P:4 * P], R("bk").to_broadcast([P, P]), R("rope"), start=True,
                             stop=True).then_inc(pe_out, 1)
            c["pe_out"] += 1

        def fold_dve(dve, c):
            dve.wait_ge(pe_out, c["pe_out"] + 1)
            nc.vector.tensor_copy(r3[:, 0:256], bank6[:, 0:256])
            nc.vector.tensor_copy(r3[:, 384:640], bank6[:, 256:512])
            nc.vector.tensor_copy(r3[:, 256:384], col(region_b, PACK3, "wv"))
            c["pe_out"] += 1

        w3 = lambda name: col(region_b, PACK3, name)
        PHASES = [
            ("setup",),
            ("norm", x, xn, False, 1e-5, None), ("attention", 0), ("experts", 0),
            ("norm", x, xn, False, 1e-5, None), ("attention", 1),
            ("norm", xn, y, True, 1e-6, (col(region_b, PACK1, "scale"), None)), ("experts", 1),
            ("norm", x, xn, False, 1e-5, None), ("top",),
            ("norm", xn, y, True, 1e-6, (col(region_a, PACK2, "g"), None)), ("relative",),
            ("norm", x, xn, False, 1e-5, None), ("fold",), ("attention", 2),
            ("norm", xn, y, False, 1e-5, (w3("ln1w"), w3("ln1b"))), ("attention", 3),
            ("norm", z, y, False, 1e-5, (w3("ln2w"), w3("ln2b"))), ("experts", 2),
        ][:stop]
        AFTER_A, AFTER_B = 4, 8

        @block.sync
        def _(sp):
            sp.dma_start(x[:, :, :], x_in.rearrange("(t p) c -> p t c", p=P)).then_inc(loaded[1], 16)
            sp.dma_start(common[:, :], packs["common"]).then_inc(loaded[0], 16)
            sp.dma_start(work[:, 0:4 * SEQ], packs["masks"]).then_inc(loaded[0], 16)
            early = PACK0["router"][0]
            sp.dma_start(region_a[:, 0:early], packs["pack0"][:, 0:early]).then_inc(loaded[0], 16)
            sp.dma_start(region_a[:, early:PACK0_W], packs["pack0"][:, early:PACK0_W]).then_inc(loaded[2], 16)
            sp.dma_start(region_b[:, 0:PACK1_W], packs["pack1"]).then_inc(loaded[3], 16)
            if len(PHASES) > AFTER_A:
                sp.wait_ge(phase_end, 4 * AFTER_A)
                sp.dma_start(region_a[:, 0:PACK2_W], packs["pack2"]).then_inc(loaded[4], 16)
            if len(PHASES) > AFTER_B:
                sp.wait_ge(phase_end, 4 * AFTER_B)
                sp.dma_start(region_b[:, 0:PACK3_W], packs["pack3"]).then_inc(loaded[5], 16)
            sp.wait_ge(phase_end, 4 * len(PHASES))
            sp.dma_start(out.rearrange("(t p) c -> p t c", p=P), x[:, :, :]).then_inc(stored, 16)
            sp.wait_ge(stored, 16)

        def arrivals(eng, phase, n):
            if phase[0] == "setup":
                eng.wait_ge(loaded[0], 16 * 3)
                eng.wait_ge(loaded[1], 16)
            if phase[0] == "experts" and phase[1] == 0:
                eng.wait_ge(loaded[2], 16)
            if phase[0] == "attention" and phase[1] == 1:
                eng.wait_ge(loaded[3], 16)
            if phase[0] == "top":
                eng.wait_ge(loaded[4], 16)
            if phase[0] == "fold":
                eng.wait_ge(loaded[5], 16)

        @block.tensor
        def _(pe):
            c = new_counts()
            for n, phase in enumerate(PHASES):
                arrivals(pe, phase, n)
                if phase[0] == "norm":
                    norm_pe(pe, c, phase[2])
                elif phase[0] == "attention":
                    attention_pe(pe, phase[1])
                elif phase[0] == "experts":
                    router_pe(pe, c, phase[1])
                    experts_pe(pe, phase[1])
                elif phase[0] == "top":
                    top_pe(pe, c)
                elif phase[0] == "relative":
                    rel_pe(pe)
                elif phase[0] == "fold":
                    fold_pe(pe, c)
                fence(pe, c)

        @block.vector
        def _(dve):
            c = new_counts()
            own = Own(dve_done)
            for n, phase in enumerate(PHASES):
                arrivals(dve, phase, n)
                if phase[0] == "setup":
                    for b in range(2):
                        own.inc(nc.vector.memset(Zb[b][:, 0, :, :, :], 0.0))
                        own.inc(nc.vector.memset(Zb[b][:, 1, :, :, :], 0.0))
                    own.wait(dve)
                    for b in range(2):
                        nc.vector.memset(Zb[b][:, 1, :, :, MAXROW:MAXROW + 2], -1.0)
                    nc.vector.memset(xT[:, BATCH * SEQ:], 0.0)
                    nc.vector.tensor_copy(identb[:, :], ident)
                    flat = lambda v: v[:, :, :].rearrange("p a b -> p (a b)")
                    nc.vector.tensor_copy(flat(maskb), work[:, 0:2 * SEQ])
                    nc.vector.tensor_copy(flat(maskTb), work[:, 2 * SEQ:4 * SEQ])
                elif phase[0] == "norm":
                    norm_dve(dve, own, c, *phase[1:])
                elif phase[0] == "attention":
                    attention_dve(dve, own, phase[1])
                elif phase[0] == "experts":
                    router_dve(dve, own, c, phase[1])
                    experts_dve(dve, phase[1])
                elif phase[0] == "top":
                    top_dve(dve, own, c)
                elif phase[0] == "relative":
                    rel_dve(dve, own)
                elif phase[0] == "fold":
                    fold_dve(dve, c)
                fence(dve, c)

        @block.scalar
        def _(act):
            c = new_counts()
            for n, phase in enumerate(PHASES):
                arrivals(act, phase, n)
                if phase[0] == "norm":
                    norm_act(act, c, phase[5])
                elif phase[0] == "attention":
                    attention_act(act, phase[1])
                elif phase[0] == "experts":
                    router_act(act, c, phase[1])
                    experts_act(act, phase[1])
                elif phase[0] == "top":
                    top_act(act, c)
                elif phase[0] == "relative":
                    rel_act(act)
                elif phase[0] == "fold":
                    c["pe_out"] += 1
                fence(act, c)

        @block.gpsimd
        def _(pool):
            c = new_counts()
            own = Own(pool_done)
            for n, phase in enumerate(PHASES):
                arrivals(pool, phase, n)
                if phase[0] == "setup":
                    for s in (proj_done, qk_evac, v_evac, z_ready, t2_done, red_done, q2_evac, s2_done, exp_done, av_done, tr_done, ot_done, outp_done, x_added, h_ready, y_done, y_added, r_pe, r_dve, r_act, g_rows, g_H, c_tr, c_sb, c_hs, c_st, c_out, c_add, onorm_done):
                        nc.gpsimd.sem_inc(s, 1)
                    for b in range(2):
                        own.inc(nc.gpsimd.memset(Vaug[:, b, :, :], 0.0))
                    own.wait(pool)
                    for b in range(2):
                        nc.gpsimd.memset(Vaug[:, b, :, :].rearrange("p t (h c) -> p (t h) c", c=32)[:, :, HD:HD + 1], 1.0)
                elif phase[0] == "attention":
                    attention_pool(pool, own, phase[1])
                elif phase[0] == "relative":
                    rel_pool(pool)
                elif phase[0] == "top":
                    top_pool(pool, c)
                fence(pool, c)


def constants():
    f = np.float32
    common = np.zeros((P, COMMON_W), f)

    def put(name, v):
        at, w = COMMON[name]
        common[:, at:at + w] = v
    put("ident", np.eye(P, dtype=f))
    put("ones", 1.0)
    put("tie", (16 - np.arange(16)).astype(f)[None, :])
    put("slot_no", np.arange(L2K, dtype=f)[None, :])
    put("slot_of_row", (np.arange(P) % L2K).astype(f)[:, None])
    query = (np.arange(P)[:, None, None] + P * np.arange(TPB)[None, :, None])
    other = np.arange(SEQ)[None, None, :]
    mask = np.where(other > query, f(NEG), f(0)).reshape(P, -1)
    maskT = np.where(query > other, f(NEG), f(0)).reshape(P, -1)
    inv = f(1.0) / np.power(f(10000.0), np.arange(0, P, 2, dtype=f) / f(P))
    pre = (np.arange(SEQ, dtype=f)[:, None] * inv[None, :]).T.astype(np.float64)
    sin, cos = np.sin(pre).astype(f), np.cos(pre).astype(f)
    invr = f(1.0) / np.power(f(10000.0), np.arange(0, HD, 2, dtype=f) / f(HD))
    fr = (np.arange(HEADS, dtype=f)[:, None] * invr[None, :]).astype(np.float64)
    rope = np.zeros((P, P), f)
    for h in range(HEADS):
        for k in range(HD // 2):
            e, o = h * HD + 2 * k, h * HD + 2 * k + 1
            cs, sn = f(np.cos(fr[h, k])), f(np.sin(fr[h, k]))
            rope[e, e], rope[o, e], rope[e, o], rope[o, o] = cs, -sn, sn, cs
    return dict(common=common, masks=np.concatenate([mask, maskT], 1),
                rot_a=np.concatenate([-cos, cos]), rot_b=np.concatenate([sin, sin]),
                pos=np.concatenate([sin, cos]), rope=rope)


def pack(plan, width, parts):
    out = np.zeros((P, width), np.float32)
    for name, (at, w) in plan.items():
        v = parts[name]
        out[:v.shape[0], at:at + w] = v
    return out


def kernel(_stop=99, _sim=None, **inputs):
    import concourse.bacc as bacc
    from concourse.bass_utils import run_bass_kernel_spmd

    I = {k: np.asarray(v) for k, v in inputs.items()}
    C = constants()
    column = lambda v: v.reshape(-1, 1)
    row = lambda v: np.broadcast_to(v.reshape(1, -1), (P, v.size))
    experts_in = lambda w: w.transpose(1, 0, 2).reshape(P, -1)
    experts_out = lambda w: w.reshape(w.shape[0], -1, P, w.shape[2]).transpose(2, 0, 1, 3).reshape(P, -1)

    q = "L0_attn_"
    pack0 = pack(PACK0, PACK0_W, dict(
        wqkv=np.concatenate([I[q + n].reshape(P, P).T for n in ("Wq", "Wk", "Wv")], 1),
        bqk=row(np.concatenate([I[q + "bq"].reshape(-1), I[q + "bk"].reshape(-1)])),
        bv=column(I[q + "bv"]), wo=I[q + "Wo"].T, bo=row(I[q + "bo"]), router=I["L0_ffn_router_w"],
        w1=experts_in(I["L0_ffn_w1"]), b1=I["L0_ffn_b1"].reshape(-1, P).T,
        w2=experts_out(I["L0_ffn_w2"]), b2=I["L0_ffn_b2"]))
    q = "L1_attn_"
    pack1 = pack(PACK1, PACK1_W, dict(
        wqkv=np.concatenate([I[q + n].T for n in ("Wq", "Wk", "Wv")], 1), wo=I[q + "Wo"].T,
        scale=column(I["L1_ffn_norm_scale"]), router=I["L1_ffn_w_router"].T,
        w1=experts_in(I["L1_ffn_w_up"].transpose(0, 2, 1)), w2=experts_out(I["L1_ffn_w_down"].transpose(0, 2, 1))))
    q = "L2_attn_"
    wr = I[q + "W_r"].T
    gate = np.zeros((P, 240), np.float32)
    gate[:, 112:128] = I["L2_ffn_Wg"]
    pack2 = pack(PACK2, PACK2_W, dict(
        g=column(I[q + "g_ln"]), wq=I[q + "W_q"], wk=I[q + "W_k"],
        wvg=np.concatenate([I[q + "W_v"], I[q + "W_g"]], 1), wrT=wr,
        wrTs=np.concatenate([wr[:, 64:], wr[:, :64]], 1), u=column(I[q + "xl_u"]), v=column(I[q + "xl_v"]),
        wo=experts_out(I[q + "W_o"][None]), rot_a=C["rot_a"], rot_b=C["rot_b"], pos=C["pos"],
        router=gate, rb=column(np.tile(I["L2_ffn_bg"], BATCH)),
        w1=experts_in(I["L2_ffn_w1"]), w2=experts_in(I["L2_ffn_w2"]), w3=experts_in(I["L2_ffn_w3"]),
        b1=row(I["L2_ffn_b1"]), b2=row(I["L2_ffn_b2"]), b3=row(I["L2_ffn_b3"])))
    q = "L3_attn_"
    w, b = I[q + "w_qkv"], I[q + "b_qkv"]
    f = "L3_ffn_"
    pack3 = pack(PACK3, PACK3_W, dict(
        wqT=w[:, :P].T, wkT=w[:, P:2 * P].T, wv=w[:, 2 * P:], rope=C["rope"], bq=column(b[:P]), bk=column(b[P:2 * P]),
        bv=column(b[2 * P:]), wo=I[q + "w_fc"], bo=row(I[q + "b_fc"]), ln1w=column(I[f + "ln1_w"]),
        ln1b=column(I[f + "ln1_b"]), wqkv2=I[f + "w_qkv"], wo2=I[f + "w_proj"], ln2w=column(I[f + "ln2_w"]),
        ln2b=column(I[f + "ln2_b"]), router=I[f + "gate_w"], rbias=row(I[f + "gate_b"]),
        w1=experts_in(I[f + "w1"]), w2=experts_out(I[f + "w2"])))

    x = I["L0_attn_hidden_state"]
    arrays = dict(x_in=np.ascontiguousarray(x.reshape(-1, P)), pack0=pack0, pack1=pack1, pack2=pack2, pack3=pack3,
                  common=C["common"], masks=C["masks"])
    nc = bacc.Bacc("TRN2", target_bir_lowering=False, num_devices=1)
    aps = {k: nc.dram_tensor("in_" + k, v.shape, mybir.dt.from_np(v.dtype), kind="ExternalInput").ap()
           for k, v in arrays.items()}
    out = nc.dram_tensor("out", (BATCH * SEQ, P), F32, kind="ExternalOutput").ap()
    build(nc, aps, aps["x_in"], out, _stop)
    if _sim is not None:
        return _sim(nc, {"in_" + k: v for k, v in arrays.items()})
    r = run_bass_kernel_spmd(nc, [{"in_" + k: v for k, v in arrays.items()}], core_ids=[0])
    return r.results[0]["out"].reshape(x.shape)
```

```python
import numpy as np
import concourse.bass as bass
from concourse import mybir
from contextlib import ExitStack

F32 = mybir.dt.float32
BF16 = mybir.dt.bfloat16
ALU = mybir.AluOpType
ACT = mybir.ActivationFunctionType
AX_X = mybir.AxisListType.X

P = 128
BATCH, SEQ = 8, 256
TILES = BATCH * SEQ // P
TPB = SEQ // P
HEADS, HD = 16, 8
PAIRS = HEADS // 2
SLOT = 64
PARTS = ((0, 0), (0, 1), (0, 2), (1, 0), (1, 1), (2, 0))
MAXROW = len(PARTS) * HD
NEG = -1.0e30

def plan_pack(entries):
    at, plan = 0, {}
    for name, width in entries:
        plan[name] = (at, width)
        at += width
    return plan, at


L0E, L0F, L1E, L1F, L2E, L2K, L3E, L3F = 14, 256, 8, 256, 16, 32, 8, 512
COMMON, COMMON_W = plan_pack([("ident", P), ("ones", P), ("tie", 16), ("slot_no", L2K), ("slot_of_row", 1)])
PACK0, PACK0_W = plan_pack([("wqkv", 384), ("bqk", 256), ("bv", 1), ("wo", P), ("bo", P), ("router", L0E),
                            ("w1", L0E * L0F), ("b1", L0E * 2), ("w2", L0E * L0F), ("b2", P)])
PACK1, PACK1_W = plan_pack([("wqkv", 384), ("wo", P), ("scale", 1), ("router", L1E), ("w1", L1E * 2 * L1F),
                            ("w2", L1E * L1F)])
PACK2, PACK2_W = plan_pack([("g", 1), ("wq", P), ("wk", P), ("wvg", 512), ("wrT", P), ("wrTs", P), ("u", 1),
                            ("v", 1), ("wo", 2 * P), ("rot_a", SEQ), ("rot_b", SEQ), ("pos", SEQ),
                            ("router", 240), ("rb", 1), ("w1", L2E * P), ("w2", L2E * P), ("w3", L2E * P),
                            ("b1", L2E), ("b2", L2E), ("b3", L2E)])
PACK3, PACK3_W = plan_pack([("wqT", P), ("wkT", P), ("wv", P), ("rope", P), ("bq", 1), ("bk", 1), ("bv", 1),
                            ("wo", P), ("bo", P), ("ln1w", 1), ("ln1b", 1), ("wqkv2", 384), ("wo2", P),
                            ("ln2w", 1), ("ln2b", 1), ("router", L3E), ("rbias", L3E), ("w1", L3E * L3F),
                            ("w2", L3E * L3F)])
REGION_A = max(PACK0_W, PACK2_W)
REGION_B = max(PACK1_W, PACK3_W)


def build(nc, packs, x_in, out, stop=99):
    with ExitStack() as ctx:
        def sb(name, shape, dt=F32):
            return ctx.enter_context(nc.sbuf_tensor(name, shape, dt))

        def sem(name):
            return ctx.enter_context(nc.semaphore(name))

        ring = ctx.enter_context(nc.psum_tensor("ring", [P, 6, 512], F32))
        bank6 = ctx.enter_context(nc.psum_tensor("bank6", [P, 512], F32))
        bank7 = ctx.enter_context(nc.psum_tensor("bank7", [P, 512], F32))

        common = sb("common", [P, COMMON_W])
        region_a = sb("region_a", [P, REGION_A])
        region_b = sb("region_b", [P, REGION_B])
        identb = sb("identb", [P, P], BF16)
        maskb = sb("maskb", [P, 2, SEQ], BF16)
        maskTb = sb("maskTb", [P, 2, SEQ], BF16)
        x = sb("x", [P, TILES, P])
        xn = sb("xn", [P, TILES, P])
        xT = sb("xT", [P, BATCH * SEQ])
        z = sb("z", [P, TILES, P])
        stats = sb("stats", [P, TILES, 6])
        mv = sb("mv", [P, TILES, 2])
        ve = sb("ve", [P, TILES])
        sd = sb("sd", [P, TILES])
        rs = sb("rs", [P, TILES])
        nt = sb("nt", [P, TILES])
        work = sb("work", [P, 11008])
        y = work[:, 0:TILES * P].rearrange("p (t c) -> p t c", t=TILES)

        def col(region, plan, name, a=0, n=None):
            at, width = plan[name]
            n = width - a if n is None else n
            return region[:, at + a:at + a + n]

        ident = col(common, COMMON, "ident")
        ones = col(common, COMMON, "ones")

        loaded = [sem(f"loaded{i}") for i in range(6)]
        stored = sem("stored")
        phase_end = sem("phase_end")
        dve_done = sem("dve_done")
        act_done = sem("act_done")
        pool_done = sem("pool_done")
        pe_out = sem("pe_out")
        dve_out = sem("dve_out")
        act_out = sem("act_out")
        xb_ready = sem("xb_ready")
        proj_done = sem("proj_done")
        qk_evac = sem("qk_evac")
        v_evac = sem("v_evac")
        z_ready = sem("z_ready")
        t_done = sem("t_done")
        tev_dve = sem("tev_dve")
        tev_act = sem("tev_act")
        s1_done = sem("s1_done")
        red_done = sem("red_done")
        m_ready = sem("m_ready")
        t2_done = sem("t2_done")
        q2_evac = sem("q2_evac")
        s2_done = sem("s2_done")
        exp_done = sem("exp_done")
        av_done = sem("av_done")
        av_evac = sem("av_evac")
        tr_done = sem("tr_done")
        onorm_done = sem("onorm_done")
        ot_done = sem("ot_done")
        ont_evac = sem("ont_evac")
        outp_done = sem("outp_done")
        x_added = sem("x_added")
        up_done = sem("up_done")
        gate_done = sem("gate_done")
        h_ready = sem("h_ready")
        y_done = sem("y_done")
        y_added = sem("y_added")

        class Own:

            def __init__(self, s):
                self.s, self.n, self.i, self.per = s, 0, None, 0

            def enter(self, i, per):
                self.i, self.per, self.at = i, per, self.n

            def leave(self, trips):
                assert self.n - self.at == self.per, (self.n - self.at, self.per)
                self.n = self.at + self.per * trips
                self.i = None

            def inc(self, ins):
                self.n += 1
                ins.then_inc(self.s, 1)
                return self.n

            def wait(self, eng):
                eng.wait_ge(self.s, self.n if self.i is None else self.i * self.per + self.n)

        USES = ["S1_0", "S1_1", "T1"]
        for p in range(PAIRS):
            if p + 2 < PAIRS:
                USES.append(f"S1_{p + 2}")
            if p == PAIRS - 1:
                USES.append("NT0")
            USES.append(f"S2_{p}")
        assert len(USES) % 3 == 0

        def slot_of(use):
            return 2 * (USES.index("NT0" if use == "T0" else use) % 3)

        def carve():
            at = [0]

            def take(n):
                a = at[0]
                at[0] += n
                assert at[0] <= 11008, at[0]
                return work[:, a:a + n]
            return take

        take = carve()
        qT = take(PAIRS * SEQ // 2).bitcast(BF16).rearrange("p (a n) -> p a n", n=SEQ)
        xb = take(2 * SEQ).rearrange("p (b n) -> p b n", b=2)
        qkf = take(2 * 512).rearrange("p (b n) -> p b n", b=2)
        res1 = take(512)
        res2 = take(512)
        Zb = [sb(f"Z{b}", [P, 2, TPB, HEADS, SLOT], BF16) for b in range(2)]
        kT = sb("kT", [P, PAIRS, 2, SEQ], BF16)
        q2T = sb("q2T", [P, 2, SEQ], BF16)
        Vaug = sb("Vaug", [P, 2, TPB, HEADS * 32])
        PTR = 4
        PT = take(PTR * 1024).rearrange("p (r n) -> p r n", r=PTR)
        mrow = sb("mrow", [P, PAIRS, 4])
        avs = take(512)
        rec = sb("rec", [P, 32])
        onorm = take(SEQ).rearrange("p (s n) -> p s n", s=2)
        onT = take(SEQ)

        ringb = ring[:, :, :].bitcast(BF16)
        bank7b = bank7[:, :].bitcast(BF16)

        SC = float(HD) ** -0.5
        r3 = sb("r3", [P, 384 + 256])
        ATT = [
            dict(w=col(region_a, PACK0, "wqkv"), bias=col(region_a, PACK0, "bqk"), bv=col(region_a, PACK0, "bv"),
                 wo=col(region_a, PACK0, "wo"), bo=col(region_a, PACK0, "bo"), causal=False, src=x, dst=x),
            dict(w=col(region_b, PACK1, "wqkv"), bias=None, bv=None,
                 wo=col(region_b, PACK1, "wo"), bo=None, causal=True, src=x, dst=x),
            dict(w=r3[:, 0:384], bias=r3[:, 384:640], bv=col(region_b, PACK3, "bv"),
                 wo=col(region_b, PACK3, "wo"), bo=col(region_b, PACK3, "bo"), causal=False, src=x, dst=x),
            dict(w=col(region_b, PACK3, "wqkv2"), bias=None, bv=None,
                 wo=col(region_b, PACK3, "wo2"), bo=None, causal=False, src=xn, dst=z),
        ]

        def expert(region, plan, n, f, gated, act):
            return dict(n=n, f=f // P, gated=gated, act=act, region=region, plan=plan)

        MOE = [expert(region_a, PACK0, L0E, L0F, False, ACT.Gelu),
               expert(region_b, PACK1, L1E, L1F, True, ACT.Silu),
               expert(region_b, PACK3, L3E, L3F, False, ACT.Gelu_apprx_tanh)]

        lg = sb("lg", [P, TILES, 16])
        lg2 = sb("lg2", [P, TILES, 16])
        cand = sb("cand", [P, TILES, 16])
        oh = sb("oh", [P, TILES, 16])
        gate = sb("gate", [P, TILES, 16])
        gateT = sb("gateT", [16, BATCH * SEQ])
        mx = sb("mx", [P, 4, TILES])
        take = carve()
        hbuf = take(3 * 512).rearrange("p (r n) -> p r n", r=3)
        sgate = take(3 * 512).rearrange("p (r n) -> p r n", r=3)

        block = ctx.enter_context(nc.Block())
        def fence(eng, st):
            st["fence"] += 1
            eng.drain().then_inc(phase_end, 1)
            eng.wait_ge(phase_end, 4 * st["fence"])

        def norm_dve(dve, own, c, src, dst, rms, eps, affine):
            g = nc.vector
            for t in range(TILES):
                own.inc(g.bn_stats(stats[:, t, :], src[:, t, :]))
            own.wait(dve)
            for t in range(TILES):
                own.inc(g.bn_aggr(mv[:, t, :], stats[:, t, :]))
            own.wait(dve)
            if rms:
                own.inc(g.tensor_tensor(nt[:, :], mv[:, :, 0], mv[:, :, 0], ALU.mult))
                own.wait(dve)
                own.inc(g.tensor_tensor(nt[:, :], nt[:, :], mv[:, :, 1], ALU.add))
                own.wait(dve)
                g.tensor_scalar(ve[:, :], nt[:, :], eps, None, ALU.add).then_inc(dve_out, 1)
            else:
                g.tensor_scalar(ve[:, :], mv[:, :, 1], eps, None, ALU.add).then_inc(dve_out, 1)
            c["dve_out"] += 1
            dve.wait_ge(act_out, c["act_out"] + 1)
            c["act_out"] += 1
            own.inc(g.reciprocal(rs[:, :], sd[:, :]))
            own.wait(dve)
            own.inc(g.tensor_tensor(nt[:, :], ve[:, :], rs[:, :], ALU.mult))
            own.wait(dve)
            own.inc(g.tensor_tensor(nt[:, :], nt[:, :], rs[:, :], ALU.mult))
            own.wait(dve)
            own.inc(g.tensor_scalar(nt[:, :], nt[:, :], -0.5, 1.5, ALU.mult, ALU.add))
            own.wait(dve)
            own.inc(g.tensor_tensor(rs[:, :], rs[:, :], nt[:, :], ALU.mult))
            own.wait(dve)
            for t in range(TILES):
                if rms:
                    ins = g.tensor_scalar(dst[:, t, :], src[:, t, :], rs[:, t:t + 1], None, ALU.mult)
                else:
                    ins = g.tensor_scalar(dst[:, t, :], src[:, t, :], mv[:, t, 0:1], rs[:, t:t + 1],
                                          ALU.subtract, ALU.mult)
                if t % 4 == 3:
                    ins.then_inc(dve_out, 1)
                    c["dve_out"] += 1
            for q in (1, 3):
                dve.wait_ge(pe_out, c["pe_out"] + q + 1)
                copy_T(g, q, affine)
            c["pe_out"] += 4

        def copy_T(g, q, affine):
            dst = xT[:, 512 * q:512 * q + 512]
            if affine is None:
                g.tensor_copy(dst, ring[:, q, :])
            elif affine[1] is None:
                g.tensor_scalar(dst, ring[:, q, :], affine[0], None, ALU.mult)
            else:
                g.tensor_scalar(dst, ring[:, q, :], affine[0], affine[1], ALU.mult, ALU.add)

        def norm_act(act, c, affine):
            act.wait_ge(dve_out, c["dve_out"] + 1)
            nc.scalar.activation(sd[:, :], ve[:, :], ACT.Sqrt).then_inc(act_out, 1)
            c["dve_out"] += 5
            c["act_out"] += 1
            for q in (0, 2):
                act.wait_ge(pe_out, c["pe_out"] + q + 1)
                dst = xT[:, 512 * q:512 * q + 512]
                if affine is None:
                    nc.scalar.activation(dst, ring[:, q, :], ACT.Copy)
                elif affine[1] is None:
                    nc.scalar.activation(dst, ring[:, q, :], ACT.Identity, scale=affine[0])
                else:
                    nc.scalar.activation(dst, ring[:, q, :], ACT.Identity, scale=affine[0], bias=affine[1])
            c["pe_out"] += 4

        def norm_pe(pe, c, dst):
            for t in range(TILES):
                if t % 4 == 0:
                    pe.wait_ge(dve_out, c["dve_out"] + 2 + t // 4)
                ins = nc.tensor.transpose(ring[:, t // 4, (t % 4) * P:(t % 4 + 1) * P], dst[:, t, :], ident)
                if t % 4 == 3:
                    ins.then_inc(pe_out, 1)
            c["dve_out"] += 5
            c["act_out"] += 1
            c["pe_out"] += 4

        def norm_pool(c):
            c["dve_out"] += 5
            c["act_out"] += 1
            c["pe_out"] += 4

        def pro_qk_pe(pe, a, b, par):
            n = 8 * a + b
            pe.wait_ge(xb_ready, n + 1)
            pe.wait_ge(v_evac, 1 + n)
            for t in range(TPB):
                ins = nc.tensor.matmul(bank7[:, t * SEQ:(t + 1) * SEQ], xb[:, par, t * P:(t + 1) * P],
                                       ATT[a]["w"][:, 0:2 * P], start=True, stop=True)
            ins.then_inc(proj_done, 1)

        def pro_v_pe(pe, a, b, par):
            n = 8 * a + b
            pe.wait_ge(qk_evac, 1 + n + 1)
            for t in range(TPB):
                ins = nc.tensor.matmul(bank7[:, t * P:(t + 1) * P], xb[:, par, t * P:(t + 1) * P],
                                       ATT[a]["w"][:, 2 * P:3 * P], start=True, stop=True)
            ins.then_inc(proj_done, 1)

        def pro_dve(dve, a, b, par, first=False):
            A = ATT[a]
            n = 8 * a + b
            if not first:
                dve.wait_ge(z_ready, 1 + n - 1)
            dve.wait_ge(proj_done, 1 + 2 * n + 1)
            dst = qkf[:, par, :].rearrange("p (w s c) -> p w s c", w=2, s=2)
            src = bank7[:, :].rearrange("p (s w c) -> p w s c", w=2, s=2)
            if A["bias"] is None:
                nc.vector.tensor_copy(dst, src).then_inc(qk_evac, 1)
            else:
                bias = A["bias"].rearrange("p (w c) -> p w c", w=2).unsqueeze(2).to_broadcast([P, 2, TPB, P])
                nc.vector.tensor_tensor(dst, src, bias, ALU.add).then_inc(qk_evac, 1)

        def pro_act(act, a, b, par, first=False):
            n = 8 * a + b
            if not first:
                act.wait_ge(av_done, 1 + 8 * (n - 1))
            act.wait_ge(proj_done, 1 + 2 * n + 2)
            nc.scalar.activation(Vaug[:, par, :, :].rearrange("p t (h c) -> p (t h) c", c=32)[:, :, 0:HD],
                                 bank7[:, 0:256].rearrange("p (h c) -> p h c", c=HD),
                                 ACT.Copy).then_inc(v_evac, 1)

        def pro_pool(pool, own, a, b, par, first=False):
            n = 8 * a + b
            g = nc.gpsimd
            if not first:
                pool.wait_ge(proj_done, 1 + 2 * (n - 1))
            g.tensor_copy(xb[:, par, :], xT[:, bass.ds(b * SEQ, SEQ)]).then_inc(xb_ready, 1)
            pool.wait_ge(qk_evac, 1 + n + 1)
            if not first:
                pool.wait_ge(t2_done, 1 + 8 * (n - 1))
            Z = Zb[par]
            rows = qkf[:, par, :].rearrange("p (w r d) -> p w r d", w=2, d=HD)
            r1 = res1.rearrange("p (w r d) -> p w r d", w=2, d=HD)
            r2 = res2.rearrange("p (w r d) -> p w r d", w=2, d=HD)
            zs = Z[:, :, :, :, :].rearrange("p w t h s -> p w (t h) s")

            def put(w, src, first_slot, step, count):
                R = TPB * HEADS
                if count == 1:
                    dst = zs[:, w, :, first_slot * HD:(first_slot + 1) * HD]
                    return own.inc(g.tensor_copy(dst, src))
                dst = zs[:, w, :, 0:48].rearrange("p r (s d) -> p r s d", d=HD)[
                    :, :, first_slot:first_slot + step * (count - 1) + 1:step, :]
                return own.inc(g.tensor_copy(dst, src.unsqueeze(2).to_broadcast([P, R, count, HD])))

            own.inc(g.memset(Z[:, 0, :, :, MAXROW:MAXROW + 2], 0.0))
            put(0, rows[:, 0], 0, 1, 3)
            put(1, rows[:, 1], 0, 3, 2)
            put(1, rows[:, 1], 5, 1, 1)
            own.wait(pool)
            for w in range(2):
                own.inc(g.tensor_tensor(r1[:, w], rows[:, w], zs[:, w, :, 0:HD], ALU.subtract))
            own.wait(pool)
            put(0, r1[:, 0], 3, 1, 2)
            put(1, r1[:, 1], 1, 3, 2)
            own.wait(pool)
            own.inc(g.tensor_tensor(r2[:, 0], r1[:, 0], zs[:, 0, :, 3 * HD:4 * HD], ALU.subtract))
            own.inc(g.tensor_tensor(r2[:, 1], r1[:, 1], zs[:, 1, :, HD:2 * HD], ALU.subtract))
            own.wait(pool)
            put(0, r2[:, 0], 5, 1, 1)
            put(1, r2[:, 1], 2, 1, 1)
            own.wait(pool)
            g.tensor_copy(res2[:, 0:1], res1[:, 0:1]).then_inc(z_ready, 1)

        def T_pe(pe, a, b, par, h):
            s = slot_of(f"T{h}")
            Z = Zb[par]
            if h == 0:
                pe.wait_ge(z_ready, 1 + 8 * a + b + 1)
            for p in range(4):
                for w in range(2):
                    for t in range(TPB):
                        ins = nc.tensor.transpose(
                            ringb[:, s + p // 2, (p % 2) * 512 + w * 256 + t * P:(p % 2) * 512 + w * 256 + (t + 1) * P],
                            Z[:, w, t, 8 * h + 2 * p:8 * h + 2 * p + 2, :], identb[:, :])
            ins.then_inc(t_done, 1)

        def batch_pe(pe, a, b, par, a_first=False, a_last=False):
            A = ATT[a]
            B = 8 * a + b
            Z = Zb[par]

            def slot_free(use):
                u = USES.index(use)
                was = USES[u - 3]
                if was == "NT0":
                    pe.wait_ge(tev_dve, 2 * B + 1)
                    pe.wait_ge(tev_act, 2 * B + 1)
                elif u < 3:
                    if not a_first:
                        pe.wait_ge(exp_done, 1 + 8 * (B - 1) + int(was[3:]) + 1)
                elif was[0] == "T":
                    pe.wait_ge(tev_dve, 2 * B + int(was[1]) + 1)
                    pe.wait_ge(tev_act, 2 * B + int(was[1]) + 1)
                elif was[:2] == "S1":
                    pe.wait_ge(red_done, 1 + 8 * B + int(was[3:]) + 1)
                else:
                    pe.wait_ge(exp_done, 1 + 8 * B + int(was[3:]) + 1)

            def S1(p):
                slot_free(f"S1_{p}")
                s = slot_of(f"S1_{p}")
                if p in (0, 4):
                    pe.wait_ge(tev_dve, 2 * B + 1 + p // 4)
                if p in (2, 6):
                    pe.wait_ge(tev_act, 2 * B + 1 + p // 4)
                for t in range(TPB):
                    if A["causal"]:
                        for h in range(2):
                            nc.tensor.matmul(ring[:, s + t, h * SEQ:(h + 1) * SEQ], identb[:, :], maskb[:, t, :],
                                             start=(h == 0), stop=False, skip_group_check=True)
                    ins = nc.tensor.matmul(ring[:, s + t, :], qT[:, p, t * P:(t + 1) * P],
                                           kT[:, p, :, :].rearrange("p h n -> p (h n)"), start=not A["causal"], stop=True,
                                           skip_group_check=True)
                ins.then_inc(s1_done, 1)

            def T2(p):
                pe.wait_ge(m_ready, 8 * B + p + 1)
                pe.wait_ge(q2_evac, 1 + 8 * B + p)
                if p == 0 and not a_last:
                    pe.wait_ge(v_evac, 1 + B + 2)
                for t in range(TPB):
                    ins = nc.tensor.transpose(bank7b[:, t * P:(t + 1) * P], Z[:, 0, t, 2 * p:2 * p + 2, :], identb[:, :])
                ins.then_inc(t2_done, 1)

            def S2(p):
                slot_free(f"S2_{p}")
                s = slot_of(f"S2_{p}")
                pe.wait_ge(q2_evac, 1 + 8 * B + p + 1)
                for h in range(2):
                    for t in range(TPB):
                        if A["causal"]:
                            nc.tensor.matmul(ring[:, s + h, t * SEQ:(t + 1) * SEQ], identb[:, :], maskTb[:, t, :],
                                             start=True, stop=False)
                        ins = nc.tensor.matmul(ring[:, s + h, t * SEQ:(t + 1) * SEQ],
                                               kT[:, p, h, t * P:(t + 1) * P], q2T[:, p % 2, :], start=not A["causal"], stop=True)
                ins.then_inc(s2_done, 1)

            def AVs(b, par, *pairs):
                for p in pairs:
                    AV_pe(pe, a, b, par, p)

            if not a_last:
                pro_qk_pe(pe, a, b + 1, 1 - par)
            if not a_first:
                AVs(b - 1, 1 - par, 4, 5)
            S1(0)
            S1(1)
            if not a_first:
                AVs(b - 1, 1 - par, 6, 7)
            if not a_last:
                pro_v_pe(pe, a, b + 1, 1 - par)
            slot_free("T1")
            T_pe(pe, a, b, par, 1)
            if not a_first:
                TR_pe(pe, a, b - 1, 1)
            T2(0)
            S1(2)
            for p in range(PAIRS):
                if 0 < p < PAIRS - 2:
                    S1(p + 2)
                if p == 1 and not a_first:
                    OT_pe(pe, a, b - 1)
                if p == 2 and not a_first:
                    out_pe(pe, a, b - 1)
                if p == 3:
                    AVs(b, par, 0, 1)
                if p == 5:
                    AVs(b, par, 2, 3)
                if p == 6:
                    TR_pe(pe, a, b, 0)
                if p + 1 < PAIRS:
                    T2(p + 1)
                if p == PAIRS - 1 and not a_last:
                    slot_free("NT0")
                    T_pe(pe, a, b + 1, 1 - par, 0)
                S2(p)

        def AV_pe(pe, a, b, par, p):
            B = 8 * a + b
            pe.wait_ge(exp_done, 1 + 8 * B + p + 1)
            if p == 0:
                pe.wait_ge(v_evac, 1 + B + 1)
                pe.wait_ge(x_added, 1 + B)
            if p == 4:
                pe.wait_ge(onorm_done, 1 + 2 * B + 1)
            for h in range(2):
                j = 2 * (p % 2) + h
                g = (p // 2) % 2
                for t in range(TPB):
                    head = 2 * p + h
                    ins = nc.tensor.matmul(bank6[32 * j:32 * j + 32, g * SEQ:(g + 1) * SEQ],
                                           Vaug[:, par, t, 32 * head:32 * head + 32],
                                           PT[:, p % PTR, (2 * h + t) * SEQ:(2 * h + t + 1) * SEQ],
                                           start=(t == 0), stop=(t == TPB - 1))
            ins.then_inc(av_done, 1)

        def TR_pe(pe, a, b, hf):
            pe.wait_ge(av_evac, 2 * (8 * a + b) + hf + 1)
            for t in range(TPB):
                for g in range(2):
                    ins = nc.tensor.transpose(bank6[:, (2 * t + g) * P:(2 * t + g + 1) * P],
                                              avs[:, g * SEQ + t * P:g * SEQ + (t + 1) * P], ident)
            ins.then_inc(tr_done, 1)

        def OT_pe(pe, a, b):
            pe.wait_ge(onorm_done, 1 + 2 * (8 * a + b) + 2)
            for t in range(TPB):
                ins = nc.tensor.transpose(bank6[:, t * P:(t + 1) * P], onorm[:, t, :], ident)
            ins.then_inc(ot_done, 1)

        def out_pe(pe, a, b):
            A = ATT[a]
            pe.wait_ge(ont_evac, 8 * a + b + 1)
            for t in range(TPB):
                ins = nc.tensor.matmul(bank6[:, t * P:(t + 1) * P], onT[:, t * P:(t + 1) * P], A["wo"],
                                       start=True, stop=A["bo"] is None)
                if A["bo"] is not None:
                    ins = nc.tensor.matmul(bank6[:, t * P:(t + 1) * P], ones[0:1, :], A["bo"][0:1, :],
                                           start=False, stop=True)
            ins.then_inc(outp_done, 1)

        def T_dve(dve, a, b, h):
            B = 8 * a + b
            g = nc.vector
            dve.wait_ge(t_done, 2 * B + h + 1)
            src = ringb[:, slot_of(f"T{h}"), :].rearrange("p (a w n) -> p a w n", a=2, w=2)
            g.tensor_copy(qT[:, 4 * h:4 * h + 2, :], src[:, :, 0, :])
            for half in range(2):
                rows = slice(SLOT * half, SLOT * half + SLOT)
                ins = g.tensor_copy(kT[rows, 4 * h:4 * h + 2, half, :], src[rows, :, 1, :])
            ins.then_inc(tev_dve, 1)

        def batch_dve(dve, own, a, b, par, a_first=False, a_last=False):
            B = 8 * a + b
            g = nc.vector
            Z = Zb[par]

            def red(p):
                s = slot_of(f"S1_{p}")
                dve.wait_ge(s1_done, 8 * B + p + 1)
                g.tensor_reduce(mrow[:, p, :], ring[:, s:s + 2, :].rearrange("p t (h n) -> p (t h) n", h=2),
                                AX_X, ALU.max).then_inc(red_done, 1)
                dve.wait_ge(red_done, 1 + 8 * B + p + 1)
                m = mrow[:, p, :].rearrange("p (t h) -> p t h", h=2)
                zc = lambda r: Z[:, 0, :, 2 * p:2 * p + 2, MAXROW + r]
                own.inc(g.tensor_copy(zc(0), m))
                own.wait(dve)
                g.tensor_tensor(zc(1), m, zc(0), ALU.subtract).then_inc(m_ready, 1)

            if not a_last:
                pro_dve(dve, a, b + 1, 1 - par)
            red(0)
            red(1)
            T_dve(dve, a, b, 1)
            red(2)
            if not a_first:
                onorm_dve(dve, own, a, b - 1, 1)
            red(3)
            red(4)
            if not a_first:
                xadd_dve(dve, a, b - 1)
            for p in range(5, PAIRS):
                red(p)
            onorm_dve(dve, own, a, b, 0)
            if not a_last:
                T_dve(dve, a, b + 1, 0)

        def onorm_dve(dve, own, a, b, hf):
            B = 8 * a + b
            g = nc.vector
            dve.wait_ge(tr_done, 1 + 2 * B + hf + 1)
            v = bank6[:, :].rearrange("p (r c) -> p r c", c=32)
            own.inc(g.reciprocal(rec[:, 0:16], v[:, :, HD]))
            own.wait(dve)
            if hf == 0:
                dve.wait_ge(ot_done, 1 + B)
            g.tensor_tensor(onorm[:, :, 64 * hf:64 * hf + 64].rearrange("p t (r d) -> p t r d", d=HD),
                            v[:, :, 0:HD].rearrange("p (t r) d -> p t r d", t=2),
                            rec[:, 0:16].rearrange("p (t r) -> p t r", t=2).unsqueeze(3).to_broadcast([P, 2, 8, HD]),
                            ALU.mult).then_inc(onorm_done, 1)

        def xadd_dve(dve, a, b):
            A = ATT[a]
            B = 8 * a + b
            dve.wait_ge(outp_done, 1 + B + 1)
            nc.vector.tensor_tensor(A["dst"][:, bass.ds(2 * b, 2), :], A["src"][:, bass.ds(2 * b, 2), :],
                                    bank6[:, 0:256].rearrange("p (t c) -> p t c", t=2), ALU.add).then_inc(x_added, 1)

        DVE_PER_BATCH = PAIRS + 2

        def T_act(act, a, b, h):
            B = 8 * a + b
            g = nc.scalar
            act.wait_ge(t_done, 2 * B + h + 1)
            src = ringb[:, slot_of(f"T{h}") + 1, :].rearrange("p (a w n) -> p a w n", a=2, w=2)
            g.activation(qT[:, 4 * h + 2:4 * h + 4, :], src[:, :, 0, :], ACT.Copy)
            for half in range(2):
                rows = slice(SLOT * half, SLOT * half + SLOT)
                ins = g.activation(kT[rows, 4 * h + 2:4 * h + 4, half, :], src[rows, :, 1, :], ACT.Copy)
            ins.then_inc(tev_act, 1)

        def batch_act(act, a, b, par, a_first=False, a_last=False):
            B = 8 * a + b
            g = nc.scalar

            def q2(p):
                act.wait_ge(t2_done, 1 + 8 * B + p + 1)
                act.wait_ge(s2_done, 1 + 8 * B + max(p - 1, 0))
                g.activation(q2T[:, p % 2, :], bank7b[:, 0:256], ACT.Copy).then_inc(q2_evac, 1)

            def ex(p):
                s = slot_of(f"S2_{p}")
                act.wait_ge(s2_done, 1 + 8 * B + p + 1)
                act.wait_ge(av_done, 1 + 8 * B + max(p - PTR + 1, 0))
                g.activation(PT[:, p % PTR, :], ring[:, s:s + 2, :].rearrange("p h n -> p (h n)"), ACT.Exp,
                             scale=SC).then_inc(exp_done, 1)

            if not a_last:
                pro_act(act, a, b + 1, 1 - par)
            if not a_first:
                av_act(act, a, b - 1, 1)
            q2(0)
            T_act(act, a, b, 1)
            for p in range(PAIRS):
                if p + 1 < PAIRS:
                    q2(p + 1)
                if p == 5:
                    av_act(act, a, b, 0)
                ex(p)
                if p == 0 and not a_first:
                    ont_act(act, a, b - 1)
                if p == PAIRS - 2 and not a_last:
                    T_act(act, a, b + 1, 0)

        def av_act(act, a, b, hf):
            B = 8 * a + b
            act.wait_ge(av_done, 1 + 8 * B + 4 * hf + 4)
            act.wait_ge(tr_done, 1 + 2 * B + hf)
            nc.scalar.activation(avs, bank6[:, :], ACT.Copy).then_inc(av_evac, 1)

        def ont_act(act, a, b):
            A = ATT[a]
            B = 8 * a + b
            act.wait_ge(ot_done, 1 + B + 1)
            act.wait_ge(outp_done, 1 + B)
            if A["bv"] is None:
                nc.scalar.activation(onT, bank6[:, 0:256], ACT.Copy).then_inc(ont_evac, 1)
            else:
                nc.scalar.activation(onT, bank6[:, 0:256], ACT.Identity, bias=A["bv"]).then_inc(ont_evac, 1)

        def attention_pe(pe, a):
            pro_qk_pe(pe, a, 0, 0)
            pro_v_pe(pe, a, 0, 0)
            T_pe(pe, a, 0, 0, 0)
            batch_pe(pe, a, 0, 0, True)
            with pe.Fori(0, BATCH // 2 - 1) as i:
                for par in (1, 0):
                    batch_pe(pe, a, 2 * i + 2 - par, par)
            batch_pe(pe, a, BATCH - 1, 1, a_last=True)
            for p in range(4, PAIRS):
                AV_pe(pe, a, BATCH - 1, 1, p)
            TR_pe(pe, a, BATCH - 1, 1)
            OT_pe(pe, a, BATCH - 1)
            out_pe(pe, a, BATCH - 1)

        def attention_dve(dve, own, a):
            pro_dve(dve, a, 0, 0, True)
            T_dve(dve, a, 0, 0)
            batch_dve(dve, own, a, 0, 0, True)
            with dve.Fori(0, BATCH // 2 - 1) as i:
                own.enter(i, 2 * DVE_PER_BATCH)
                for par in (1, 0):
                    batch_dve(dve, own, a, 2 * i + 2 - par, par)
                own.leave(BATCH // 2 - 1)
            batch_dve(dve, own, a, BATCH - 1, 1, a_last=True)
            onorm_dve(dve, own, a, BATCH - 1, 1)
            xadd_dve(dve, a, BATCH - 1)

        def attention_act(act, a):
            pro_act(act, a, 0, 0, True)
            T_act(act, a, 0, 0)
            batch_act(act, a, 0, 0, True)
            with act.Fori(0, BATCH // 2 - 1) as i:
                for par in (1, 0):
                    batch_act(act, a, 2 * i + 2 - par, par)
            batch_act(act, a, BATCH - 1, 1, a_last=True)
            av_act(act, a, BATCH - 1, 1)
            ont_act(act, a, BATCH - 1)

        def attention_pool(pool, own, a):
            pro_pool(pool, own, a, 0, 0, True)
            for b in range(1, BATCH):
                pro_pool(pool, own, a, b, b % 2)

        def new_counts():
            return dict(dve_out=0, act_out=0, pe_out=0, fence=0)


        def bcast(v, width):
            return v.unsqueeze(2).to_broadcast([P, TILES, width])

        def router_pe(pe, c, m):
            M = MOE[m]
            E = M["n"]
            for t in range(TILES):
                ins = nc.tensor.matmul(bank7[:, t * E:(t + 1) * E], xT[:, t * P:(t + 1) * P],
                                       col(M["region"], M["plan"], "router"), start=True, stop=True)
            ins.then_inc(pe_out, 1)
            c["pe_out"] += 1
            if m == 0:
                c["dve_out"] += 2
                c["act_out"] += 1
                pe.wait_ge(dve_out, c["dve_out"])
                for t in range(TILES):
                    ins = nc.tensor.transpose(ring[0:E, t // 4, (t % 4) * P:(t % 4 + 1) * P], gate[:, t, 0:E], ident)
                ins.then_inc(pe_out, 1)
                pe.wait_ge(act_out, c["act_out"] + 1)
                for t in range(TILES):
                    ins = nc.tensor.matmul(ring[:, t // 4, (t % 4) * P:(t % 4 + 1) * P], gateT[0:E, t * P:(t + 1) * P],
                                           col(region_a, PACK0, "b2")[0:E, :], start=True, stop=True)
                ins.then_inc(pe_out, 1)
                c["pe_out"] += 2
                c["act_out"] += 1
                c["dve_out"] += 1
                pe.wait_ge(dve_out, c["dve_out"])
            elif m == 1:
                c["dve_out"] += 1
                c["act_out"] += 1

        def router_dve(dve, own, c, m):
            M = MOE[m]
            E = M["n"]
            g = nc.vector
            L, L2, C, O, W = (v[:, :, 0:E] for v in (lg, lg2, cand, oh, gate))
            tie = col(common, COMMON, "tie", 0, E)
            tie = tie.unsqueeze(1).to_broadcast([P, TILES, E])

            def step(ins):
                own.inc(ins)
                own.wait(dve)

            def choose(src, top, first):
                step(g.tensor_reduce(mx[:, top, :], src, AX_X, ALU.max))
                step(g.tensor_tensor(C, src, bcast(mx[:, top, :], E), ALU.is_equal))
                step(g.tensor_tensor(C, C, tie, ALU.mult))
                step(g.tensor_reduce(mx[:, 3, :], C, AX_X, ALU.max))
                step(g.tensor_tensor(first, C, bcast(mx[:, 3, :], E), ALU.is_equal))

            dve.wait_ge(pe_out, c["pe_out"] + 1)
            c["pe_out"] += 1
            src = bank7[:, 0:TILES * E].rearrange("p (t e) -> p t e", e=E)
            if m == 2:
                rb = col(region_b, PACK3, "rbias").unsqueeze(1).to_broadcast([P, TILES, E])
                step(g.tensor_tensor(L, src, rb, ALU.add))
                choose(L, 0, W)
                step(g.tensor_tensor(x[:, :, :], x[:, :, :], z[:, :, :], ALU.add))
            if m == 0:
                step(g.tensor_copy(L, src))
                choose(L, 0, O)
                g.tensor_tensor(L2, L, bcast(mx[:, 0, :], E), ALU.subtract).then_inc(dve_out, 1)
                dve.wait_ge(act_out, c["act_out"] + 1)
                step(g.tensor_reduce(mx[:, 1, :], L2, AX_X, ALU.add))
                step(g.reciprocal(mx[:, 2, :], mx[:, 1, :]))
                g.tensor_tensor(W, O, bcast(mx[:, 2, :], E), ALU.mult).then_inc(dve_out, 1)
                dve.wait_ge(pe_out, c["pe_out"] + 2)
                for q in range(4):
                    ins = g.tensor_tensor(x[:, 4 * q:4 * q + 4, :], x[:, 4 * q:4 * q + 4, :],
                                          ring[:, q, :].rearrange("p (t c) -> p t c", t=4), ALU.add)
                ins.then_inc(dve_out, 1)
                c["pe_out"] += 2
                c["dve_out"] += 3
                dve.wait_ge(dve_out, c["dve_out"])
                c["act_out"] += 2
            if m == 1:
                step(g.tensor_copy(L, src))
                choose(L, 0, O)
                step(g.scalar_tensor_tensor(out=L2, in0=O, scalar=-3.0e38, in1=L, op0=ALU.mult, op1=ALU.add))
                choose(L2, 1, W)
                g.tensor_tensor(mx[:, 2, :], mx[:, 1, :], mx[:, 0, :], ALU.subtract).then_inc(dve_out, 1)
                dve.wait_ge(act_out, c["act_out"] + 1)
                step(g.tensor_scalar(mx[:, 0, :], mx[:, 2, :], 1.0, None, ALU.add))
                step(g.reciprocal(mx[:, 1, :], mx[:, 0, :]))
                step(g.tensor_tensor(mx[:, 2, :], mx[:, 2, :], mx[:, 1, :], ALU.mult))
                step(g.tensor_tensor(O, O, bcast(mx[:, 1, :], E), ALU.mult))
                step(g.tensor_tensor(W, W, bcast(mx[:, 2, :], E), ALU.mult))
                step(g.tensor_tensor(W, W, O, ALU.add))
                step(g.tensor_tensor(x[:, :, :], x[:, :, :], xn[:, :, :], ALU.add))
                c["dve_out"] += 1
                c["act_out"] += 1

        def router_act(act, c, m):
            E = MOE[m]["n"]
            c["pe_out"] += 1
            if m == 0:
                act.wait_ge(dve_out, c["dve_out"] + 1)
                nc.scalar.activation(lg2[:, :, 0:E], lg2[:, :, 0:E], ACT.Exp).then_inc(act_out, 1)
                act.wait_ge(pe_out, c["pe_out"] + 1)
                nc.scalar.activation(gateT[0:E, :], ring[0:E, 0:4, :].rearrange("p q n -> p (q n)"),
                                     ACT.Copy).then_inc(act_out, 1)
                c["dve_out"] += 3
                c["act_out"] += 2
                c["pe_out"] += 2
            elif m == 1:
                act.wait_ge(dve_out, c["dve_out"] + 1)
                nc.scalar.activation(mx[:, 2, :], mx[:, 2, :], ACT.Exp).then_inc(act_out, 1)
                c["dve_out"] += 1
                c["act_out"] += 1

        def router_pool(c, m):
            c["pe_out"] += 3 if m == 0 else 1
            c["dve_out"] += (3, 1, 0)[m]
            c["act_out"] += (2, 1, 0)[m]

        UNITS = [M["n"] * M["f"] for M in MOE]
        U0 = [4 * sum(UNITS[:m]) for m in range(3)]
        E0 = [4 * sum(M["n"] for M in MOE[:m]) for m in range(3)]
        HR = 4
        take = carve()
        hb = take(HR * 512).rearrange("p (r n) -> p r n", r=HR)
        sg = take(HR * 512).rearrange("p (r n) -> p r n", r=HR)

        def experts_pe(pe, m):
            M = MOE[m]
            n, f, gated = M["n"], M["f"], M["gated"]
            F = f * P * (2 if gated else 1)
            w1 = col(M["region"], M["plan"], "w1")
            w2 = col(M["region"], M["plan"], "w2")
            banks = 2 if gated else 4
            with pe.Fori(0, 4) as i:
                base = i * UNITS[m] + U0[m]

                def up(k):
                    e, fc = divmod(k, f)
                    pe.wait_ge(h_ready, 1 + base + max(k - banks + 1, 0))
                    rows = xT[:, bass.ds(i * 512, 512)]
                    if gated:
                        for part in range(2):
                            ins = nc.tensor.matmul(ring[:, 2 * (k % 2) + part, :],
                                                   w1[:, e * F + part * f * P + fc * P:e * F + part * f * P + fc * P + P],
                                                   rows, start=True, stop=True)
                    else:
                        ins = nc.tensor.matmul(ring[:, k % 4, :], w1[:, e * F + fc * P:e * F + fc * P + P], rows,
                                               start=True, stop=True)
                    ins.then_inc(up_done, 1)

                def down(k):
                    e, fc = divmod(k, f)
                    pe.wait_ge(h_ready, 1 + base + k + 1)
                    if fc == 0:
                        pe.wait_ge(y_added, 1 + i * n + E0[m] + max(e - 1, 0))
                    for t in range(4):
                        ins = nc.tensor.matmul(ring[:, 4 + e % 2, t * P:(t + 1) * P], hb[:, k % HR, t * P:(t + 1) * P],
                                               w2[:, (e * f + fc) * P:(e * f + fc + 1) * P],
                                               start=(fc == 0 and t == 0), stop=(fc == f - 1), skip_group_check=True)
                    ins.then_inc(y_done, 1)

                ahead = banks - 1 if gated else 2
                for k in range(ahead):
                    up(k)
                for k in range(n * f):
                    if k + ahead < n * f:
                        up(k + ahead)
                    down(k)

        def experts_act(act, m):
            M = MOE[m]
            n, f, gated = M["n"], M["f"], M["gated"]
            with act.Fori(0, 4) as i:
                base = i * UNITS[m] + U0[m]
                for k in range(n * f):
                    act.wait_ge(up_done, base + k + 1)
                    if gated:
                        act.wait_ge(h_ready, 1 + base + max(k - HR + 1, 0))
                        nc.scalar.activation(sg[:, k % HR, :], ring[:, 2 * (k % 2) + 1, :], M["act"]).then_inc(gate_done, 1)
                    else:
                        act.wait_ge(y_done, 1 + base + max(k - HR + 1, 0))
                        b = col(region_a, PACK0, "b1", k, 1) if m == 0 else None
                        if b is None:
                            ins = nc.scalar.activation(hb[:, k % HR, :], ring[:, k % 4, :], M["act"])
                        else:
                            ins = nc.scalar.activation(hb[:, k % HR, :], ring[:, k % 4, :], M["act"], bias=b)
                        ins.then_inc(h_ready, 1)

        def experts_dve(dve, m):
            M = MOE[m]
            n, f, gated = M["n"], M["f"], M["gated"]
            g = nc.vector
            with dve.Fori(0, 4) as i:
                base = i * UNITS[m] + U0[m]

                def add(e):
                    dve.wait_ge(y_done, 1 + base + e * f + f)
                    dve.wait_ge(y_added, 1 + i * n + E0[m] + e)
                    for t in range(4):
                        row = x[:, bass.ds(4 * i + t, 1), :]
                        ins = g.scalar_tensor_tensor(out=row, in0=ring[:, 4 + e % 2, t * P:(t + 1) * P].unsqueeze(1),
                                                     scalar=gate[:, bass.ds(4 * i + t, 1), e], in1=row,
                                                     op0=ALU.mult, op1=ALU.add)
                    ins.then_inc(y_added, 1)

                for k in range(n * f):
                    if gated:
                        dve.wait_ge(gate_done, i * UNITS[m] + k + 1)
                        dve.wait_ge(y_done, 1 + base + max(k - HR + 1, 0))
                        g.tensor_tensor(hb[:, k % HR, :], sg[:, k % HR, :], ring[:, 2 * (k % 2), :],
                                        ALU.mult).then_inc(h_ready, 1)
                    if k % f == 0 and k > 0:
                        add(k // f - 1)
                add(n - 1)

        take = carve()
        xc, qu, qv, kk, ap, t1, t2 = (take(512) for _ in range(7))
        vs, sgl, Pm, PTs, wv, wvT = (take(1024).rearrange("p (t n) -> p t n", t=4) for _ in range(6))
        neg_max = sb("neg_max", [P, 4])
        row_sum = sb("row_sum", [P, 4])
        row_rec = sb("row_rec", [P, 4])
        r_pe, r_dve, r_act, r_pool = (sem("rel_" + k) for k in ("pe", "dve", "act", "pool"))
        REL = dict(pe=["q", "k", "vg", "a", "scores", "PT", "av", "wvT", "res"],
                   dve=["k", "v", "rot", "ap", "max", "rec", "PT", "wv", "x"],
                   act=["qu", "qv", "silu", "exp", "wvT"], pool=["xc"])

        def rel_at(i, who, what, back=0):
            return i * len(REL[who]) + (REL[who].index(what) + 1 if not back else 0)

        def rel_pe(pe):
            R = lambda name: col(region_a, PACK2, name)
            mm = nc.tensor.matmul
            with pe.Fori(0, 4) as i:
                rows = xT[:, bass.ds(i * 512, 512)]
                pe.wait_ge(r_dve, 1 + i * 9)
                pe.wait_ge(r_act, 1 + i * 5)
                mm(ring[:, 0, :], R("wq"), rows, start=True, stop=True).then_inc(r_pe, 1)
                mm(ring[:, 1, :], R("wk"), rows, start=True, stop=True).then_inc(r_pe, 1)
                pe.wait_ge(r_pool, rel_at(i, "pool", "xc"))
                for t in range(4):
                    lhs = xc[:, t * P:(t + 1) * P]
                    mm(ring[:, 2 + t // 2, (t % 2) * 256:(t % 2) * 256 + 256], lhs, R("wvg")[:, 0:256], start=True, stop=True)
                    ins = mm(ring[:, 4 + t // 2, (t % 2) * 256:(t % 2) * 256 + 256], lhs, R("wvg")[:, 256:512],
                             start=True, stop=True)
                ins.then_inc(r_pe, 1)
                pe.wait_ge(r_act, 1 + rel_at(i, "act", "qv"))
                mm(bank6[:, :], R("wrT"), qv, start=True, stop=True)
                mm(bank7[:, :], R("wrTs"), qv, start=True, stop=True).then_inc(r_pe, 1)
                pe.wait_ge(r_dve, 1 + rel_at(i, "dve", "ap"))
                for b in range(2):
                    for t in range(2):
                        o = ring[:, b, t * 256:(t + 1) * 256]
                        here = slice(b * 256 + t * P, b * 256 + (t + 1) * P)
                        mm(o, identb[:, :], maskb[:, t, :], start=True, stop=False)
                        mm(o, qu[:, here], kk[:, b * 256:(b + 1) * 256], start=False, stop=False)
                        ins = mm(o, ap[:, here], R("pos"), start=False, stop=True)
                ins.then_inc(r_pe, 1)
                pe.wait_ge(r_act, 1 + rel_at(i, "act", "exp"))
                for b in range(2):
                    for j in range(2):
                        for t in range(2):
                            ins = nc.tensor.transpose(ring[:, 2 + b, j * 256 + t * P:j * 256 + (t + 1) * P],
                                                      Pm[:, 2 * b + t, j * P:(j + 1) * P], ident)
                ins.then_inc(r_pe, 1)
                pe.wait_ge(r_dve, 1 + rel_at(i, "dve", "PT"))
                for b in range(2):
                    for t in range(2):
                        for j in range(2):
                            ins = mm(ring[:, 4 + b, t * 256:(t + 1) * 256], PTs[:, 2 * b + j, t * P:(t + 1) * P],
                                     vs[:, 2 * b + j, :], start=(j == 0), stop=(j == 1))
                ins.then_inc(r_pe, 1)
                pe.wait_ge(r_dve, 1 + rel_at(i, "dve", "wv"))
                for t in range(4):
                    for j in range(2):
                        ins = nc.tensor.transpose(ring[:, t // 2, (t % 2) * 256 + j * P:(t % 2) * 256 + (j + 1) * P],
                                                  wv[:, t, j * P:(j + 1) * P], ident)
                ins.then_inc(r_pe, 1)
                pe.wait_ge(r_act, 1 + rel_at(i, "act", "wvT"))
                for t in range(4):
                    for j in range(2):
                        ins = mm(bank6[:, t * P:(t + 1) * P], wvT[:, t, j * P:(j + 1) * P], R("wo")[:, j * P:(j + 1) * P],
                                 start=(j == 0), stop=(j == 1))
                ins.then_inc(r_pe, 1)

        def rel_dve(dve, own):
            g = nc.vector
            R = lambda name: col(region_a, PACK2, name)
            two = lambda v: v.rearrange("p (b n) -> p b n", b=2)
            with dve.Fori(0, 4) as i:
                own.enter(i, 1)
                dve.wait_ge(r_pe, 1 + rel_at(i, "pe", "k"))
                g.tensor_copy(kk, ring[:, 1, :]).then_inc(r_dve, 1)
                dve.wait_ge(r_pe, 1 + rel_at(i, "pe", "vg"))
                g.tensor_copy(vs, ring[:, 2:4, :].rearrange("p q (t n) -> p (q t) n", t=2)).then_inc(r_dve, 1)
                dve.wait_ge(r_pe, 1 + rel_at(i, "pe", "a"))
                own.inc(g.tensor_tensor(two(t1), two(bank6[:, :]), R("rot_a").unsqueeze(1).to_broadcast([P, 2, SEQ]), ALU.mult))
                g.tensor_tensor(two(t2), two(bank7[:, :]), R("rot_b").unsqueeze(1).to_broadcast([P, 2, SEQ]),
                                ALU.mult).then_inc(r_dve, 1)
                own.wait(dve)
                dve.wait_ge(r_dve, 1 + rel_at(i, "dve", "rot"))
                g.tensor_tensor(ap, t1, t2, ALU.add).then_inc(r_dve, 1)
                dve.wait_ge(r_pe, 1 + rel_at(i, "pe", "scores"))
                g.tensor_reduce(neg_max[:, :], ring[:, 0:2, :].rearrange("p b (t n) -> p (b t) n", t=2), AX_X, ALU.max,
                                negate=True).then_inc(r_dve, 1)
                dve.wait_ge(r_act, 1 + rel_at(i, "act", "exp"))
                g.reciprocal(row_rec[:, :], row_sum[:, :]).then_inc(r_dve, 1)
                dve.wait_ge(r_pe, 1 + rel_at(i, "pe", "PT"))
                g.tensor_copy(PTs, ring[:, 2:4, :].rearrange("p q (t n) -> p (q t) n", t=2)).then_inc(r_dve, 1)
                dve.wait_ge(r_pe, 1 + rel_at(i, "pe", "av"))
                dve.wait_ge(r_act, 1 + rel_at(i, "act", "silu"))
                dve.wait_ge(r_dve, 1 + rel_at(i, "dve", "rec"))
                for t in range(4):
                    ins = g.scalar_tensor_tensor(out=wv[:, t, :], in0=ring[:, 4 + t // 2, (t % 2) * 256:(t % 2) * 256 + 256],
                                                 scalar=row_rec[:, t:t + 1], in1=sgl[:, t, :], op0=ALU.mult, op1=ALU.mult)
                ins.then_inc(r_dve, 1)
                dve.wait_ge(r_pe, 1 + rel_at(i, "pe", "res"))
                rows = x[:, bass.ds(4 * i, 4), :]
                g.tensor_tensor(rows, rows, bank6[:, :].rearrange("p (t c) -> p t c", t=4), ALU.add).then_inc(r_dve, 1)
                own.leave(4)

        def rel_act(act):
            g = nc.scalar
            R = lambda name: col(region_a, PACK2, name)
            with act.Fori(0, 4) as i:
                act.wait_ge(r_pe, 1 + rel_at(i, "pe", "q"))
                tau = float(P) ** -0.5
                g.activation(qu, ring[:, 0, :], ACT.Identity, scale=tau, bias=R("u")).then_inc(r_act, 1)
                g.activation(qv, ring[:, 0, :], ACT.Identity, scale=tau, bias=R("v")).then_inc(r_act, 1)
                act.wait_ge(r_pe, 1 + rel_at(i, "pe", "vg"))
                g.activation(sgl, ring[:, 4:6, :].rearrange("p q (t n) -> p (q t) n", t=2), ACT.Silu).then_inc(r_act, 1)
                act.wait_ge(r_dve, 1 + rel_at(i, "dve", "max"))
                for t in range(4):
                    ins = g.activation(Pm[:, t, :], ring[:, t // 2, (t % 2) * 256:(t % 2) * 256 + 256], ACT.Exp,
                                       bias=neg_max[:, t:t + 1], accum_out=row_sum[:, t:t + 1])
                ins.then_inc(r_act, 1)
                act.wait_ge(r_pe, 1 + rel_at(i, "pe", "wvT"))
                g.activation(wvT, ring[:, 0:2, :].rearrange("p q (t n) -> p (q t) n", t=2), ACT.Copy).then_inc(r_act, 1)

        def rel_pool(pool):
            for i in range(4):
                pool.wait_ge(r_pe, 1 + i * 9)
                nc.gpsimd.tensor_copy(xc, xT[:, bass.ds(i * 512, 512)]).then_inc(r_pool, 1)

        take = carve()
        H = take(BATCH * 512)
        Sel = take(2 * 1024).rearrange("p (b t n) -> p b t n", b=2, t=2)
        Gsel = take(2 * 1024).rearrange("p (b t n) -> p b t n", b=2, t=2)
        pr, cur0, cur1, cum, slot = (take(SEQ) for _ in range(5))
        xg = [sb(f"xg{b}", [P, TPB, P]) for b in range(2)]
        spread = sb("spread", [P, 2, 512], BF16)
        slotb = sb("slotb", [P, SEQ], BF16)
        spT = sb("spT", [P, 4, P])
        top8 = sb("top8", [P, 8])
        vals = sb("vals", [P, BATCH * 4])
        k1 = sb("k1", [P, 4])
        h12 = take(4 * SEQ).rearrange("p (r n) -> p r n", r=4)
        Hc = Gsel[:, :, 0, 0:512]
        hs = Gsel[:, :, 1, 0:512]
        ST = Sel
        g_pool, g_sel, g_val, g_rows, g_vals, g_H = (sem("g_" + k) for k in ("pool", "sel", "val", "rows", "vals", "H"))
        m_pe, m_act, m_dve = (sem("mlp_" + k) for k in ("pe", "act", "dve"))
        c_pool, c_tr, c_sb, c_hs, c_st, c_out, c_add = (sem("c_" + k) for k in
                                                        ("pool", "tr", "sb", "hs", "st", "out", "add"))

        def top_pe(pe, c):
            mm = nc.tensor.matmul
            router = col(region_a, PACK2, "router")
            for b in range(BATCH):
                ins = mm(bank6[:, 0:SEQ], router[:, 112 - 16 * b:240 - 16 * b], xT[:, b * SEQ:(b + 1) * SEQ],
                         start=(b == 0), stop=(b == BATCH - 1))
            ins.then_inc(pe_out, 1)
            pe.wait_ge(dve_out, c["dve_out"] + 2)
            for t in range(TPB):
                nc.tensor.transpose(bank7[:, t * P:(t + 1) * P], slot[:, t * P:(t + 1) * P], ident)
                ins = nc.tensor.transpose(bank7[:, (2 + t) * P:(3 + t) * P], pr[:, t * P:(t + 1) * P], ident)
            ins.then_inc(pe_out, 1)
            with pe.Fori(0, BATCH // 2) as i:
                for par in range(2):
                    b = 2 * i + par
                    pe.wait_ge(g_pool, b + 1)
                    pe.wait_ge(g_sel, b + 1)
                    pe.wait_ge(g_H, 1 + 2 * i)
                    for t in range(TPB):
                        ins = mm(ring[:, par, :], xg[par][:, t, :], Sel[:, par, t, :], start=(t == 0), stop=(t == TPB - 1))
                    ins.then_inc(g_rows, 1)
                    pe.wait_ge(g_val, b + 1)
                    for q in range(4):
                        for t in range(TPB):
                            ins = mm(ring[:, 2 + par, q:q + 1], Gsel[:, par, t, q * P:(q + 1) * P], ones[:, 0:1],
                                     start=(t == 0), stop=(t == TPB - 1))
                    ins.then_inc(g_rows, 1)
            Hv = H.rearrange("p (b e k) -> p b e k", b=BATCH, e=L2E)
            pe.wait_ge(g_H, 1 + BATCH)
            pe.wait_ge(g_vals, BATCH)
            for s in range(L2E + 2):
                for layer in range(3):
                    e = s - layer
                    if not 0 <= e < L2E:
                        continue
                    w = col(region_a, PACK2, f"w{layer + 1}", e * P, P)
                    o = ring[:, 2 * layer + e % 2, 0:SEQ]
                    if layer == 0:
                        if e >= 2:
                            pe.wait_ge(m_act, MLP_ACT.index((0, e - 2)) + 1)
                        rhs, o = Hv[:, :, e, :], o.rearrange("p (b k) -> p b k", b=BATCH)
                    else:
                        pe.wait_ge(m_act, MLP_ACT.index((layer - 1, e)) + 1)
                        if layer == 2 and e >= 2:
                            pe.wait_ge(m_dve, e - 1)
                        rhs = h12[:, 2 * (layer - 1) + e % 2, :]
                    mm(o, w, rhs, start=True, stop=True).then_inc(m_pe, 1)
            pe.wait_ge(m_dve, L2E)
            with pe.Fori(0, BATCH // 2) as i:
                for par in range(2):
                    b = 2 * i + par
                    pe.wait_ge(c_pool, b + 1)
                    pe.wait_ge(c_hs, 1 + 2 * i)
                    for q in range(4):
                        ins = nc.tensor.transpose(ring[:, par, q * P:(q + 1) * P], Hc[:, par, q * P:(q + 1) * P], ident)
                    ins.then_inc(c_tr, 1)
                    pe.wait_ge(c_st, 1 + 2 * i)
                    for q in range(4):
                        ins = mm(ring[:, 2 + 2 * par + q // 2, (q % 2) * SEQ:(q % 2 + 1) * SEQ],
                                 spread[:, par, q * P:(q + 1) * P], slotb[:, :], start=True, stop=True)
                    ins.then_inc(c_sb, 1)
                    pe.wait_ge(c_hs, 1 + b + 1)
                    pe.wait_ge(c_st, 1 + b + 1)
                    pe.wait_ge(c_add, 1 + 2 * i)
                    bank = (bank6, bank7)[par]
                    for t in range(TPB):
                        for q in range(4):
                            ins = mm(bank[:, t * P:(t + 1) * P], STv(par)[:, q, t * P:(t + 1) * P],
                                     hs[:, par, q * P:(q + 1) * P], start=(q == 0), stop=(q == 3))
                    ins.then_inc(c_out, 1)
            c["pe_out"] += 2
            c["dve_out"] += 2
            c["act_out"] += 2

        def STv(par):
            return ST[:, par, :, :].rearrange("p t (q n) -> p (t q) n", q=2)

        MLP_ORDER = [(s - layer, layer) for s in range(L2E + 2) for layer in range(3) if 0 <= s - layer < L2E]
        MLP_ACT = [(layer, e) for e, layer in MLP_ORDER if layer < 2]

        def top_dve(dve, own, c):
            g = nc.vector

            def step(ins):
                own.inc(ins)
                own.wait(dve)

            dve.wait_ge(pe_out, c["pe_out"] + 1)
            step(g.tensor_scalar(cur0, bank6[:, 0:SEQ], col(region_a, PACK2, "rb"), None, ALU.add))
            g.tensor_reduce(k1[:, 0:1], cur0, AX_X, ALU.max, negate=True).then_inc(dve_out, 1)
            dve.wait_ge(act_out, c["act_out"] + 1)
            step(g.reciprocal(k1[:, 2:3], k1[:, 1:2]))
            step(g.tensor_scalar(pr, cur1, k1[:, 2:3], None, ALU.mult))
            cur, nxt = pr, cur0
            for r in range(L2K // 8):
                step(g.max(top8[:, :], cur))
                step(g.match_replace(out=nxt, in_to_replace=top8[:, :], in_values=cur, imm_value=-1.0))
                cur, nxt = nxt, (cur1 if nxt is cur0 else cur0)
            taken = nxt
            step(g.tensor_scalar(taken, cur, 0.0, None, ALU.is_lt))
            step(g.tensor_tensor_scan(cum, col_ones(), taken, 0.0, ALU.mult, ALU.add))
            step(g.tensor_tensor(cum, cum, taken, ALU.mult))
            step(g.tensor_scalar(slotb[:, :], cum, -1.0, None, ALU.add))
            g.tensor_scalar(slot, cum, -1.0, None, ALU.add).then_inc(dve_out, 1)
            dve.wait_ge(act_out, c["act_out"] + 2)
            number = col(common, COMMON, "slot_no").unsqueeze(1).to_broadcast([P, L2E, L2K])
            with dve.Fori(0, BATCH // 2) as i:
                for par in range(2):
                    b = 2 * i + par
                    dve.wait_ge(g_rows, 1 + 4 * i)
                    for t in range(TPB):
                        of = spT[:, t, bass.ds(16 * b, 16)].unsqueeze(2).to_broadcast([P, L2E, L2K])
                        ins = g.tensor_tensor(Sel[:, par, t, :].rearrange("p (e k) -> p e k", e=L2E), of, number,
                                              ALU.is_equal)
                    ins.then_inc(g_sel, 1)
                    dve.wait_ge(g_sel, b + 1)
                    for t in range(TPB):
                        pt = spT[:, 2 + t, bass.ds(16 * b, 16)].unsqueeze(2).to_broadcast([P, L2E, L2K])
                        ins = g.tensor_tensor(Gsel[:, par, t, :].rearrange("p (e k) -> p e k", e=L2E),
                                              Sel[:, par, t, :].rearrange("p (e k) -> p e k", e=L2E), pt, ALU.mult)
                    ins.then_inc(g_val, 1)
                    dve.wait_ge(g_rows, 1 + 2 * b + 2)
                    g.tensor_copy(vals[:, bass.ds(4 * b, 4)], ring[:, 2 + par, 0:4]).then_inc(g_vals, 1)
            Hv = H.rearrange("p (b e k) -> p b e k", b=BATCH, e=L2E)
            for e in range(L2E):
                dve.wait_ge(m_pe, MLP_ORDER.index((e, 2)) + 1)
                g.tensor_scalar(Hv[:, :, e, :], ring[:, 4 + e % 2, 0:SEQ].rearrange("p (b k) -> p b k", b=BATCH),
                                col(region_a, PACK2, "b3", e, 1), None, ALU.add).then_inc(m_dve, 1)
            dve.wait_ge(g_vals, BATCH)
            with dve.Fori(0, BATCH // 2) as i:
                for par in range(2):
                    b = 2 * i + par
                    dve.wait_ge(c_tr, 1 + b + 1)
                    dve.wait_ge(c_out, 1 + 2 * i)
                    g.tensor_tensor(hs[:, par, :].rearrange("p (q n) -> p q n", q=4),
                                    ring[:, par, :].rearrange("p (q n) -> p q n", q=4),
                                    vals[:, bass.ds(4 * b, 4)].unsqueeze(2).to_broadcast([P, 4, P]),
                                    ALU.mult).then_inc(c_hs, 1)
                    dve.wait_ge(c_sb, 1 + b + 1)
                    g.tensor_scalar(STv(par), ring[:, 2 + 2 * par:4 + 2 * par, :].rearrange("p a (q n) -> p (a q) n", q=2),
                                    col(common, COMMON, "slot_of_row"), None, ALU.is_equal).then_inc(c_st, 1)
                    dve.wait_ge(c_out, 1 + b + 1)
                    rows = x[:, bass.ds(2 * b, 2), :]
                    g.tensor_tensor(rows, rows, (bank6, bank7)[par][:, 0:SEQ].rearrange("p (t c) -> p t c", t=2),
                                    ALU.add).then_inc(c_add, 1)
            c["pe_out"] += 2
            c["dve_out"] += 2
            c["act_out"] += 2

        def col_ones():
            return ones[:, 0:1].to_broadcast([P, SEQ])

        def top_act(act, c):
            g = nc.scalar
            act.wait_ge(dve_out, c["dve_out"] + 1)
            g.activation(cur1, cur0, ACT.Exp, bias=k1[:, 0:1], accum_out=k1[:, 1:2]).then_inc(act_out, 1)
            act.wait_ge(pe_out, c["pe_out"] + 2)
            g.activation(spT[:, :, :], bank7[:, :].rearrange("p (t n) -> p t n", t=4), ACT.Copy).then_inc(act_out, 1)
            with act.Fori(0, BATCH // 2) as i:
                for par in range(2):
                    b = 2 * i + par
                    act.wait_ge(g_rows, 1 + 2 * b + 1)
                    g.activation(H[:, bass.ds(b * 512, 512)], ring[:, par, :], ACT.Copy).then_inc(g_H, 1)
            for layer, e in MLP_ACT:
                act.wait_ge(m_pe, MLP_ORDER.index((e, layer)) + 1)
                if e >= 2:
                    act.wait_ge(m_pe, MLP_ORDER.index((e - 2, layer + 1)) + 1)
                g.activation(h12[:, 2 * layer + e % 2, :], ring[:, 2 * layer + e % 2, 0:SEQ], ACT.Relu,
                             bias=col(region_a, PACK2, f"b{layer + 1}", e, 1)).then_inc(m_act, 1)
            c["pe_out"] += 2
            c["dve_out"] += 2
            c["act_out"] += 2

        def top_pool(pool, c):
            g = nc.gpsimd
            for i in range(BATCH // 2):
                for par in range(2):
                    b = 2 * i + par
                    pool.wait_ge(g_rows, 1 + 4 * i)
                    g.tensor_copy(xg[par][:, :, :], xn[:, bass.ds(2 * b, 2), :]).then_inc(g_pool, 1)
            pool.wait_ge(m_dve, L2E)
            pool.wait_ge(g_rows, 1 + 2 * BATCH)
            for i in range(BATCH // 2):
                for par in range(2):
                    b = 2 * i + par
                    pool.wait_ge(c_tr, 1 + 2 * i)
                    pool.wait_ge(c_sb, 1 + 2 * i)
                    g.tensor_copy(spread[:, par, :].rearrange("p (e k) -> p e k", e=L2E),
                                  identb[:, bass.ds(16 * b, 16)].unsqueeze(2).to_broadcast([P, L2E, L2K]))
                    g.tensor_copy(Hc[:, par, :], H[:, bass.ds(b * 512, 512)]).then_inc(c_pool, 1)
            c["pe_out"] += 2
            c["dve_out"] += 2
            c["act_out"] += 2

        def fold_pe(pe, c):
            R = lambda name: col(region_b, PACK3, name)
            nc.tensor.matmul(bank6[:, 0:P], R("wqT"), R("rope"), start=True, stop=True)
            nc.tensor.matmul(bank6[:, P:2 * P], R("wkT"), R("rope"), start=True, stop=True)
            nc.tensor.matmul(bank6[:, 2 * P:3 * P], R("bq").to_broadcast([P, P]), R("rope"), start=True, stop=True)
            nc.tensor.matmul(bank6[:, 3 * P:4 * P], R("bk").to_broadcast([P, P]), R("rope"), start=True,
                             stop=True).then_inc(pe_out, 1)
            c["pe_out"] += 1

        def fold_dve(dve, c):
            dve.wait_ge(pe_out, c["pe_out"] + 1)
            nc.vector.tensor_copy(r3[:, 0:256], bank6[:, 0:256])
            nc.vector.tensor_copy(r3[:, 384:640], bank6[:, 256:512])
            nc.vector.tensor_copy(r3[:, 256:384], col(region_b, PACK3, "wv"))
            c["pe_out"] += 1

        w3 = lambda name: col(region_b, PACK3, name)
        PHASES = [
            ("setup",),
            ("norm", x, xn, False, 1e-5, None), ("attention", 0), ("experts", 0),
            ("norm", x, xn, False, 1e-5, None), ("attention", 1),
            ("norm", xn, y, True, 1e-6, (col(region_b, PACK1, "scale"), None)), ("experts", 1),
            ("norm", x, xn, False, 1e-5, None), ("top",),
            ("norm", xn, y, True, 1e-6, (col(region_a, PACK2, "g"), None)), ("relative",),
            ("norm", x, xn, False, 1e-5, None), ("fold",), ("attention", 2),
            ("norm", xn, y, False, 1e-5, (w3("ln1w"), w3("ln1b"))), ("attention", 3),
            ("norm", z, y, False, 1e-5, (w3("ln2w"), w3("ln2b"))), ("experts", 2),
        ][:stop]
        AFTER_A, AFTER_B = 4, 8

        @block.sync
        def _(sp):
            sp.dma_start(x[:, :, :], x_in.rearrange("(t p) c -> p t c", p=P)).then_inc(loaded[1], 16)
            sp.dma_start(common[:, :], packs["common"]).then_inc(loaded[0], 16)
            sp.dma_start(work[:, 0:4 * SEQ], packs["masks"]).then_inc(loaded[0], 16)
            early = PACK0["router"][0]
            sp.dma_start(region_a[:, 0:early], packs["pack0"][:, 0:early]).then_inc(loaded[0], 16)
            sp.dma_start(region_a[:, early:PACK0_W], packs["pack0"][:, early:PACK0_W]).then_inc(loaded[2], 16)
            sp.dma_start(region_b[:, 0:PACK1_W], packs["pack1"]).then_inc(loaded[3], 16)
            if len(PHASES) > AFTER_A:
                sp.wait_ge(phase_end, 4 * AFTER_A)
                sp.dma_start(region_a[:, 0:PACK2_W], packs["pack2"]).then_inc(loaded[4], 16)
            if len(PHASES) > AFTER_B:
                sp.wait_ge(phase_end, 4 * AFTER_B)
                sp.dma_start(region_b[:, 0:PACK3_W], packs["pack3"]).then_inc(loaded[5], 16)
            sp.wait_ge(phase_end, 4 * len(PHASES))
            sp.dma_start(out.rearrange("(t p) c -> p t c", p=P), x[:, :, :]).then_inc(stored, 16)
            sp.wait_ge(stored, 16)

        def arrivals(eng, phase, n):
            if phase[0] == "setup":
                eng.wait_ge(loaded[0], 16 * 3)
                eng.wait_ge(loaded[1], 16)
            if phase[0] == "experts" and phase[1] == 0:
                eng.wait_ge(loaded[2], 16)
            if phase[0] == "attention" and phase[1] == 1:
                eng.wait_ge(loaded[3], 16)
            if phase[0] == "top":
                eng.wait_ge(loaded[4], 16)
            if phase[0] == "fold":
                eng.wait_ge(loaded[5], 16)

        @block.tensor
        def _(pe):
            c = new_counts()
            for n, phase in enumerate(PHASES):
                arrivals(pe, phase, n)
                if phase[0] == "norm":
                    norm_pe(pe, c, phase[2])
                elif phase[0] == "attention":
                    attention_pe(pe, phase[1])
                elif phase[0] == "experts":
                    router_pe(pe, c, phase[1])
                    experts_pe(pe, phase[1])
                elif phase[0] == "top":
                    top_pe(pe, c)
                elif phase[0] == "relative":
                    rel_pe(pe)
                elif phase[0] == "fold":
                    fold_pe(pe, c)
                fence(pe, c)

        @block.vector
        def _(dve):
            c = new_counts()
            own = Own(dve_done)
            for n, phase in enumerate(PHASES):
                arrivals(dve, phase, n)
                if phase[0] == "setup":
                    for b in range(2):
                        own.inc(nc.vector.memset(Zb[b][:, 0, :, :, :], 0.0))
                        own.inc(nc.vector.memset(Zb[b][:, 1, :, :, :], 0.0))
                    own.wait(dve)
                    for b in range(2):
                        nc.vector.memset(Zb[b][:, 1, :, :, MAXROW:MAXROW + 2], -1.0)
                    nc.vector.memset(kT[:, :, :, :], 0.0)
                    nc.vector.tensor_copy(identb[:, :], ident)
                    flat = lambda v: v[:, :, :].rearrange("p a b -> p (a b)")
                    nc.vector.tensor_copy(flat(maskb), work[:, 0:2 * SEQ])
                    nc.vector.tensor_copy(flat(maskTb), work[:, 2 * SEQ:4 * SEQ])
                elif phase[0] == "norm":
                    norm_dve(dve, own, c, *phase[1:])
                elif phase[0] == "attention":
                    attention_dve(dve, own, phase[1])
                elif phase[0] == "experts":
                    router_dve(dve, own, c, phase[1])
                    experts_dve(dve, phase[1])
                elif phase[0] == "top":
                    top_dve(dve, own, c)
                elif phase[0] == "relative":
                    rel_dve(dve, own)
                elif phase[0] == "fold":
                    fold_dve(dve, c)
                fence(dve, c)

        @block.scalar
        def _(act):
            c = new_counts()
            for n, phase in enumerate(PHASES):
                arrivals(act, phase, n)
                if phase[0] == "norm":
                    norm_act(act, c, phase[5])
                elif phase[0] == "attention":
                    attention_act(act, phase[1])
                elif phase[0] == "experts":
                    router_act(act, c, phase[1])
                    experts_act(act, phase[1])
                elif phase[0] == "top":
                    top_act(act, c)
                elif phase[0] == "relative":
                    rel_act(act)
                elif phase[0] == "fold":
                    c["pe_out"] += 1
                fence(act, c)

        @block.gpsimd
        def _(pool):
            c = new_counts()
            own = Own(pool_done)
            for n, phase in enumerate(PHASES):
                arrivals(pool, phase, n)
                if phase[0] == "setup":
                    for s in (proj_done, qk_evac, v_evac, z_ready, t2_done, red_done, q2_evac, s2_done, exp_done, av_done, tr_done, ot_done, outp_done, x_added, h_ready, y_done, y_added, r_pe, r_dve, r_act, g_rows, g_H, c_tr, c_sb, c_hs, c_st, c_out, c_add, onorm_done):
                        nc.gpsimd.sem_inc(s, 1)
                    for b in range(2):
                        own.inc(nc.gpsimd.memset(Vaug[:, b, :, :], 0.0))
                    own.wait(pool)
                    for b in range(2):
                        nc.gpsimd.memset(Vaug[:, b, :, :].rearrange("p t (h c) -> p (t h) c", c=32)[:, :, HD:HD + 1], 1.0)
                elif phase[0] == "attention":
                    attention_pool(pool, own, phase[1])
                elif phase[0] == "relative":
                    rel_pool(pool)
                elif phase[0] == "top":
                    top_pool(pool, c)
                fence(pool, c)


def constants():
    f = np.float32
    common = np.zeros((P, COMMON_W), f)

    def put(name, v):
        at, w = COMMON[name]
        common[:, at:at + w] = v
    put("ident", np.eye(P, dtype=f))
    put("ones", 1.0)
    put("tie", (16 - np.arange(16)).astype(f)[None, :])
    put("slot_no", np.arange(L2K, dtype=f)[None, :])
    put("slot_of_row", (np.arange(P) % L2K).astype(f)[:, None])
    query = (np.arange(P)[:, None, None] + P * np.arange(TPB)[None, :, None])
    other = np.arange(SEQ)[None, None, :]
    mask = np.where(other > query, f(NEG), f(0)).reshape(P, -1)
    maskT = np.where(query > other, f(NEG), f(0)).reshape(P, -1)
    inv = f(1.0) / np.power(f(10000.0), np.arange(0, P, 2, dtype=f) / f(P))
    pre = (np.arange(SEQ, dtype=f)[:, None] * inv[None, :]).T.astype(np.float64)
    sin, cos = np.sin(pre).astype(f), np.cos(pre).astype(f)
    invr = f(1.0) / np.power(f(10000.0), np.arange(0, HD, 2, dtype=f) / f(HD))
    fr = (np.arange(HEADS, dtype=f)[:, None] * invr[None, :]).astype(np.float64)
    rope = np.zeros((P, P), f)
    for h in range(HEADS):
        for k in range(HD // 2):
            e, o = h * HD + 2 * k, h * HD + 2 * k + 1
            cs, sn = f(np.cos(fr[h, k])), f(np.sin(fr[h, k]))
            rope[e, e], rope[o, e], rope[e, o], rope[o, o] = cs, -sn, sn, cs
    return dict(common=common, masks=np.concatenate([mask, maskT], 1),
                rot_a=np.concatenate([-cos, cos]), rot_b=np.concatenate([sin, sin]),
                pos=np.concatenate([sin, cos]), rope=rope)


def pack(plan, width, parts):
    out = np.zeros((P, width), np.float32)
    for name, (at, w) in plan.items():
        v = parts[name]
        out[:v.shape[0], at:at + w] = v
    return out


def kernel(_stop=99, _sim=None, **inputs):
    import concourse.bacc as bacc
    from concourse.bass_utils import run_bass_kernel_spmd

    I = {k: np.asarray(v) for k, v in inputs.items()}
    C = constants()
    column = lambda v: v.reshape(-1, 1)
    row = lambda v: np.broadcast_to(v.reshape(1, -1), (P, v.size))
    experts_in = lambda w: w.transpose(1, 0, 2).reshape(P, -1)
    experts_out = lambda w: w.reshape(w.shape[0], -1, P, w.shape[2]).transpose(2, 0, 1, 3).reshape(P, -1)

    q = "L0_attn_"
    pack0 = pack(PACK0, PACK0_W, dict(
        wqkv=np.concatenate([I[q + n].reshape(P, P).T for n in ("Wq", "Wk", "Wv")], 1),
        bqk=row(np.concatenate([I[q + "bq"].reshape(-1), I[q + "bk"].reshape(-1)])),
        bv=column(I[q + "bv"]), wo=I[q + "Wo"].T, bo=row(I[q + "bo"]), router=I["L0_ffn_router_w"],
        w1=experts_in(I["L0_ffn_w1"]), b1=I["L0_ffn_b1"].reshape(-1, P).T,
        w2=experts_out(I["L0_ffn_w2"]), b2=I["L0_ffn_b2"]))
    q = "L1_attn_"
    pack1 = pack(PACK1, PACK1_W, dict(
        wqkv=np.concatenate([I[q + n].T for n in ("Wq", "Wk", "Wv")], 1), wo=I[q + "Wo"].T,
        scale=column(I["L1_ffn_norm_scale"]), router=I["L1_ffn_w_router"].T,
        w1=experts_in(I["L1_ffn_w_up"].transpose(0, 2, 1)), w2=experts_out(I["L1_ffn_w_down"].transpose(0, 2, 1))))
    q = "L2_attn_"
    wr = I[q + "W_r"].T
    gate = np.zeros((P, 240), np.float32)
    gate[:, 112:128] = I["L2_ffn_Wg"]
    pack2 = pack(PACK2, PACK2_W, dict(
        g=column(I[q + "g_ln"]), wq=I[q + "W_q"], wk=I[q + "W_k"],
        wvg=np.concatenate([I[q + "W_v"], I[q + "W_g"]], 1), wrT=wr,
        wrTs=np.concatenate([wr[:, 64:], wr[:, :64]], 1), u=column(I[q + "xl_u"]), v=column(I[q + "xl_v"]),
        wo=experts_out(I[q + "W_o"][None]), rot_a=C["rot_a"], rot_b=C["rot_b"], pos=C["pos"],
        router=gate, rb=column(np.tile(I["L2_ffn_bg"], BATCH)),
        w1=experts_in(I["L2_ffn_w1"]), w2=experts_in(I["L2_ffn_w2"]), w3=experts_in(I["L2_ffn_w3"]),
        b1=row(I["L2_ffn_b1"]), b2=row(I["L2_ffn_b2"]), b3=row(I["L2_ffn_b3"])))
    q = "L3_attn_"
    w, b = I[q + "w_qkv"], I[q + "b_qkv"]
    f = "L3_ffn_"
    pack3 = pack(PACK3, PACK3_W, dict(
        wqT=w[:, :P].T, wkT=w[:, P:2 * P].T, wv=w[:, 2 * P:], rope=C["rope"], bq=column(b[:P]), bk=column(b[P:2 * P]),
        bv=column(b[2 * P:]), wo=I[q + "w_fc"], bo=row(I[q + "b_fc"]), ln1w=column(I[f + "ln1_w"]),
        ln1b=column(I[f + "ln1_b"]), wqkv2=I[f + "w_qkv"], wo2=I[f + "w_proj"], ln2w=column(I[f + "ln2_w"]),
        ln2b=column(I[f + "ln2_b"]), router=I[f + "gate_w"], rbias=row(I[f + "gate_b"]),
        w1=experts_in(I[f + "w1"]), w2=experts_out(I[f + "w2"])))

    x = I["L0_attn_hidden_state"]
    arrays = dict(x_in=np.ascontiguousarray(x.reshape(-1, P)), pack0=pack0, pack1=pack1, pack2=pack2, pack3=pack3,
                  common=C["common"], masks=C["masks"])
    nc = bacc.Bacc("TRN2", target_bir_lowering=False, num_devices=1)
    aps = {k: nc.dram_tensor("in_" + k, v.shape, mybir.dt.from_np(v.dtype), kind="ExternalInput").ap()
           for k, v in arrays.items()}
    out = nc.dram_tensor("out", (BATCH * SEQ, P), F32, kind="ExternalOutput").ap()
    build(nc, aps, aps["x_in"], out, _stop)
    if _sim is not None:
        return _sim(nc, {"in_" + k: v for k, v in arrays.items()})
    r = run_bass_kernel_spmd(nc, [{"in_" + k: v for k, v in arrays.items()}], core_ids=[0])
    return r.results[0]["out"].reshape(x.shape)
```

```python
import numpy as np
import concourse.bass as bass
from concourse import mybir
from contextlib import ExitStack

F32 = mybir.dt.float32
I32 = mybir.dt.int32
BF16 = mybir.dt.bfloat16
ALU = mybir.AluOpType
ACT = mybir.ActivationFunctionType
AX_X = mybir.AxisListType.X

P = 128
BATCH, SEQ = 8, 256
TILES = BATCH * SEQ // P
TPB = SEQ // P
HEADS, HD = 16, 8
PAIRS = HEADS // 2
SLOT = 64
PARTS = ((0, 0), (0, 1), (0, 2), (1, 0), (1, 1), (2, 0))
MAXROW = len(PARTS) * HD
NEG = -1.0e30

def plan_pack(entries):
    at, plan = 0, {}
    for name, width in entries:
        plan[name] = (at, width)
        at += width
    return plan, at


L0E, L0F, L1E, L1F, L2E, L2K, L3E, L3F = 14, 256, 8, 256, 16, 32, 8, 512
COMMON, COMMON_W = plan_pack([("ident", P), ("ones", P), ("tie", 16), ("slot_no", L2K), ("slot_of_row", 1)])
PACK0, PACK0_W = plan_pack([("wqkv", 384), ("bqk", 256), ("bv", 1), ("wo", P), ("bo", P), ("router", L0E),
                            ("w1", L0E * (L0F + L0F // P)), ("w2", L0E * L0F), ("b2", P)])
PACK1, PACK1_W = plan_pack([("wqkv", 384), ("wo", P), ("scale", 1), ("router", L1E), ("w1", L1E * 2 * L1F),
                            ("w2", L1E * L1F)])
PACK2, PACK2_W = plan_pack([("g", 1), ("wq", P), ("wk", P), ("wvg", 512), ("wrT", P), ("wrTs", P), ("u", 1),
                            ("v", 1), ("wo", 2 * P), ("rot_a", SEQ), ("rot_b", SEQ), ("pos", SEQ),
                            ("router", 240), ("rb", 1), ("w1", L2E * P), ("w2", L2E * P), ("w3", L2E * P),
                            ("b1", L2E), ("b2", L2E), ("b3", L2E)])
PACK3, PACK3_W = plan_pack([("wqT", P), ("wkT", P), ("wv", P), ("rope", P), ("bq", 1), ("bk", 1), ("bv", 1),
                            ("wo", P), ("bo", P), ("ln1w", 1), ("ln1b", 1), ("wqkv2", 384), ("wo2", P),
                            ("ln2w", 1), ("ln2b", 1), ("router", L3E), ("rbias", L3E), ("w1", L3E * L3F),
                            ("w2", L3E * L3F)])
REGION_A = max(PACK0_W, PACK2_W)
REGION_B = max(PACK1_W, PACK3_W)


def sorted_tiles(experts):
    return TILES + experts - 1


def build(nc, packs, x_in, out, sorted_in, sorted_out, stop=99):
    with ExitStack() as ctx:
        def sb(name, shape, dt=F32):
            return ctx.enter_context(nc.sbuf_tensor(name, shape, dt))

        def sem(name):
            return ctx.enter_context(nc.semaphore(name))

        ring = ctx.enter_context(nc.psum_tensor("ring", [P, 6, 512], F32))
        bank6 = ctx.enter_context(nc.psum_tensor("bank6", [P, 512], F32))
        bank7 = ctx.enter_context(nc.psum_tensor("bank7", [P, 512], F32))

        common = sb("common", [P, COMMON_W])
        region_a = sb("region_a", [P, REGION_A])
        region_b = sb("region_b", [P, REGION_B])
        identb = sb("identb", [P, P], BF16)
        maskb = sb("maskb", [P, 2, SEQ], BF16)
        maskTb = sb("maskTb", [P, 2, SEQ], BF16)
        x = sb("x", [P, TILES, P])
        xn = sb("xn", [P, TILES, P])
        xT = sb("xT", [P, BATCH * SEQ])
        z = sb("z", [P, TILES, P])
        stats = sb("stats", [P, TILES, 6])
        mv = sb("mv", [P, TILES, 2])
        ve = sb("ve", [P, TILES])
        sd = sb("sd", [P, TILES])
        rs = sb("rs", [P, TILES])
        nt = sb("nt", [P, TILES])
        table_in = sb("table_in", [P, 1])
        work = sb("work", [P, 11008])
        y = work[:, 0:TILES * P].rearrange("p (t c) -> p t c", t=TILES)

        def col(region, plan, name, a=0, n=None):
            at, width = plan[name]
            n = width - a if n is None else n
            return region[:, at + a:at + a + n]

        ident = col(common, COMMON, "ident")
        ones = col(common, COMMON, "ones")

        loaded = [sem(f"loaded{i}") for i in range(6)]
        stored = sem("stored")
        zeroed = sem("zeroed")
        cleared = sem("cleared")
        choice_ready = sem("choice_ready")
        ranked = sem("ranked")
        place_ready = sem("place_ready")
        tiles_ready = sem("tiles_ready")
        scattered = sem("scattered")
        rows_in = [sem(f"rows_in{k}") for k in range(4)]
        rows_T = sem("rows_T")
        rows_evac = sem("rows_evac")
        w1_ready = sem("w1_ready")
        w2_ready = sem("w2_ready")
        tile_up = sem("tile_up")
        tile_h = sem("tile_h")
        tile_down = sem("tile_down")
        tile_y = sem("tile_y")
        rows_out = sem("rows_out")
        gathered = [sem(f"gathered{k}") for k in range(4)]
        phase_end = sem("phase_end")
        dve_done = sem("dve_done")
        act_done = sem("act_done")
        pool_done = sem("pool_done")
        pe_out = sem("pe_out")
        dve_out = sem("dve_out")
        act_out = sem("act_out")
        xb_ready = sem("xb_ready")
        proj_done = sem("proj_done")
        qk_evac = sem("qk_evac")
        v_evac = sem("v_evac")
        z_ready = sem("z_ready")
        t_done = sem("t_done")
        tev_dve = sem("tev_dve")
        tev_act = sem("tev_act")
        s1_done = sem("s1_done")
        red_done = sem("red_done")
        m_ready = sem("m_ready")
        t2_done = sem("t2_done")
        q2_evac = sem("q2_evac")
        s2_done = sem("s2_done")
        exp_done = sem("exp_done")
        av_done = sem("av_done")
        av_evac = sem("av_evac")
        tr_done = sem("tr_done")
        onorm_done = sem("onorm_done")
        ot_done = sem("ot_done")
        ont_evac = sem("ont_evac")
        outp_done = sem("outp_done")
        x_added = sem("x_added")
        up_done = sem("up_done")
        gate_done = sem("gate_done")
        h_ready = sem("h_ready")
        y_done = sem("y_done")
        y_added = sem("y_added")

        class Own:

            def __init__(self, s):
                self.s, self.n, self.i, self.per = s, 0, None, 0

            def enter(self, i, per):
                self.i, self.per, self.at = i, per, self.n

            def leave(self, trips):
                assert self.n - self.at == self.per, (self.n - self.at, self.per)
                self.n = self.at + self.per * trips
                self.i = None

            def inc(self, ins):
                self.n += 1
                ins.then_inc(self.s, 1)
                return self.n

            def wait(self, eng):
                eng.wait_ge(self.s, self.n if self.i is None else self.i * self.per + self.n)

        USES = ["S1_0", "S1_1", "T1"]
        for p in range(PAIRS):
            if p + 2 < PAIRS:
                USES.append(f"S1_{p + 2}")
            if p == PAIRS - 1:
                USES.append("NT0")
            USES.append(f"S2_{p}")
        assert len(USES) % 3 == 0

        def slot_of(use):
            return 2 * (USES.index("NT0" if use == "T0" else use) % 3)

        def carve():
            at = [0]

            def take(n):
                a = at[0]
                at[0] += n
                assert at[0] <= 11008, at[0]
                return work[:, a:a + n]
            return take

        take = carve()
        qT = take(PAIRS * SEQ // 2).bitcast(BF16).rearrange("p (a n) -> p a n", n=SEQ)
        xb = take(2 * SEQ).rearrange("p (b n) -> p b n", b=2)
        qkf = take(2 * 512).rearrange("p (b n) -> p b n", b=2)
        res1 = take(512)
        res2 = take(512)
        Zb = [sb(f"Z{b}", [P, 2, TPB, HEADS, SLOT], BF16) for b in range(2)]
        kT = sb("kT", [P, PAIRS, 2, SEQ], BF16)
        q2T = sb("q2T", [P, 2, SEQ], BF16)
        Vaug = sb("Vaug", [P, 2, TPB, HEADS * 32])
        PTR = 4
        PT = take(PTR * 1024).rearrange("p (r n) -> p r n", r=PTR)
        mrow = sb("mrow", [P, PAIRS, 4])
        avs = take(512)
        rec = sb("rec", [P, 32])
        onorm = take(SEQ).rearrange("p (s n) -> p s n", s=2)
        onT = take(SEQ)

        ringb = ring[:, :, :].bitcast(BF16)
        bank7b = bank7[:, :].bitcast(BF16)

        SC = float(HD) ** -0.5
        r3 = sb("r3", [P, 384 + 256])
        ATT = [
            dict(w=col(region_a, PACK0, "wqkv"), bias=col(region_a, PACK0, "bqk"), bv=col(region_a, PACK0, "bv"),
                 wo=col(region_a, PACK0, "wo"), bo=col(region_a, PACK0, "bo"), causal=False, src=x, dst=x),
            dict(w=col(region_b, PACK1, "wqkv"), bias=None, bv=None,
                 wo=col(region_b, PACK1, "wo"), bo=None, causal=True, src=x, dst=x),
            dict(w=r3[:, 0:384], bias=r3[:, 384:640], bv=col(region_b, PACK3, "bv"),
                 wo=col(region_b, PACK3, "wo"), bo=col(region_b, PACK3, "bo"), causal=False, src=x, dst=x),
            dict(w=col(region_b, PACK3, "wqkv2"), bias=None, bv=None,
                 wo=col(region_b, PACK3, "wo2"), bo=None, causal=False, src=xn, dst=z),
        ]

        def expert(region, plan, n, f, gated, act):
            return dict(n=n, f=f // P, gated=gated, act=act, region=region, plan=plan)

        MOE = [expert(region_a, PACK0, L0E, L0F, False, ACT.Gelu),
               expert(region_b, PACK1, L1E, L1F, True, ACT.Silu),
               expert(region_b, PACK3, L3E, L3F, False, ACT.Gelu_apprx_tanh)]

        SORTED = {m: dict(w1_width=MOE[m]["f"] * P + b, w2_width=MOE[m]["f"] * P, bias=b)
                  for m, b in ((0, L0F // P), (2, 0))}
        choice = sb("choice", [P, TILES * 16], BF16)
        before = sb("before", [P, P], BF16)
        onesb = sb("onesb", [P, P], BF16)
        sort = sb("sort", [P, 6, 32])
        sortw = work[:, 8192:8192 + 32 * 16]
        tile_e = sb("tile_e", [P, 32])
        tile_col = sb("tile_col", [P, 2, 32], I32)
        place = sb("place", [P, TILES], I32)
        lg = sb("lg", [P, TILES, 16])
        lg2 = sb("lg2", [P, TILES, 16])
        cand = sb("cand", [P, TILES, 16])
        oh = sb("oh", [P, TILES, 16])
        gate = sb("gate", [P, TILES, 16])
        gateT = sb("gateT", [16, BATCH * SEQ])
        mx = sb("mx", [P, 4, TILES])

        block = ctx.enter_context(nc.Block())
        def fence(eng, st):
            st["fence"] += 1
            eng.drain().then_inc(phase_end, 1)
            eng.wait_ge(phase_end, 4 * st["fence"])

        def norm_dve(dve, own, c, src, dst, rms, eps, affine):
            g = nc.vector
            for t in range(TILES):
                own.inc(g.bn_stats(stats[:, t, :], src[:, t, :]))
            own.wait(dve)
            for t in range(TILES):
                own.inc(g.bn_aggr(mv[:, t, :], stats[:, t, :]))
            own.wait(dve)
            if rms:
                own.inc(g.tensor_tensor(nt[:, :], mv[:, :, 0], mv[:, :, 0], ALU.mult))
                own.wait(dve)
                own.inc(g.tensor_tensor(nt[:, :], nt[:, :], mv[:, :, 1], ALU.add))
                own.wait(dve)
                g.tensor_scalar(ve[:, :], nt[:, :], eps, None, ALU.add).then_inc(dve_out, 1)
            else:
                g.tensor_scalar(ve[:, :], mv[:, :, 1], eps, None, ALU.add).then_inc(dve_out, 1)
            c["dve_out"] += 1
            dve.wait_ge(act_out, c["act_out"] + 1)
            c["act_out"] += 1
            own.inc(g.reciprocal(rs[:, :], sd[:, :]))
            own.wait(dve)
            own.inc(g.tensor_tensor(nt[:, :], ve[:, :], rs[:, :], ALU.mult))
            own.wait(dve)
            own.inc(g.tensor_tensor(nt[:, :], nt[:, :], rs[:, :], ALU.mult))
            own.wait(dve)
            own.inc(g.tensor_scalar(nt[:, :], nt[:, :], -0.5, 1.5, ALU.mult, ALU.add))
            own.wait(dve)
            own.inc(g.tensor_tensor(rs[:, :], rs[:, :], nt[:, :], ALU.mult))
            own.wait(dve)
            if not rms:
                own.inc(g.tensor_tensor(nt[:, :], mv[:, :, 0], rs[:, :], ALU.mult))
                own.wait(dve)
            g.tensor_scalar(ve[:, :], nt[:, :], -1.0, None, ALU.mult).then_inc(dve_out, 1)
            for t in range(TILES):
                if t // 4 % 2 == 0:
                    continue
                if rms:
                    ins = g.tensor_scalar(dst[:, t, :], src[:, t, :], rs[:, t:t + 1], None, ALU.mult)
                else:
                    ins = g.tensor_scalar(dst[:, t, :], src[:, t, :], mv[:, t, 0:1], rs[:, t:t + 1],
                                          ALU.subtract, ALU.mult)
                if t % 4 == 3:
                    ins.then_inc(dve_out, 1)
            c["dve_out"] += 3
            c["act_out"] += 2
            for q in (1, 3):
                dve.wait_ge(pe_out, c["pe_out"] + q + 1)
                copy_T(g, q, affine)
            c["pe_out"] += 4

        def copy_T(g, q, affine):
            dst = xT[:, 512 * q:512 * q + 512]
            if affine is None:
                g.tensor_copy(dst, ring[:, q, :])
            elif affine[1] is None:
                g.tensor_scalar(dst, ring[:, q, :], affine[0], None, ALU.mult)
            else:
                g.tensor_scalar(dst, ring[:, q, :], affine[0], affine[1], ALU.mult, ALU.add)

        def norm_act(act, c, src, dst, rms, affine):
            nc.scalar.activation(table_in[:, :], ones[:, 0:1], ACT.Sqrt)
            act.wait_ge(dve_out, c["dve_out"] + 1)
            nc.scalar.activation(sd[:, :], ve[:, :], ACT.Sqrt).then_inc(act_out, 1)
            act.wait_ge(dve_out, c["dve_out"] + 2)
            for t in range(TILES):
                if t // 4 % 2 == 0:
                    if rms:
                        ins = nc.scalar.activation(dst[:, t, :], src[:, t, :], ACT.Copy, scale=rs[:, t:t + 1])
                    else:
                        ins = nc.scalar.activation(dst[:, t, :], src[:, t, :], ACT.Identity, scale=rs[:, t:t + 1],
                                                   bias=ve[:, t:t + 1])
                    if t % 4 == 3:
                        ins.then_inc(act_out, 1)
            c["dve_out"] += 4
            c["act_out"] += 3
            for q in (0, 2):
                act.wait_ge(pe_out, c["pe_out"] + q + 1)
                dst = xT[:, 512 * q:512 * q + 512]
                if affine is None:
                    nc.scalar.activation(dst, ring[:, q, :], ACT.Copy)
                elif affine[1] is None:
                    nc.scalar.activation(dst, ring[:, q, :], ACT.Identity, scale=affine[0])
                else:
                    nc.scalar.activation(dst, ring[:, q, :], ACT.Identity, scale=affine[0], bias=affine[1])
            c["pe_out"] += 4

        def norm_pe(pe, c, dst):
            for t in range(TILES):
                q = t // 4
                if t % 4 == 0 and q % 2:
                    pe.wait_ge(dve_out, c["dve_out"] + 3 + q // 2)
                elif t % 4 == 0:
                    pe.wait_ge(act_out, c["act_out"] + 2 + q // 2)
                ins = nc.tensor.transpose(ring[:, q, (t % 4) * P:(t % 4 + 1) * P], dst[:, t, :], ident)
                if t % 4 == 3:
                    ins.then_inc(pe_out, 1)
            c["dve_out"] += 4
            c["act_out"] += 3
            c["pe_out"] += 4

        def x_tile(b, par, t, first):
            return xT[:, t * P:(t + 1) * P] if first else xb[:, par, t * P:(t + 1) * P]

        def pro_qk_pe(pe, a, b, par, first=False):
            n = 8 * a + b
            if not first:
                pe.wait_ge(xb_ready, 7 * a + b)
            pe.wait_ge(v_evac, 1 + n)
            for t in range(TPB):
                ins = nc.tensor.matmul(bank7[:, t * SEQ:(t + 1) * SEQ], x_tile(b, par, t, first),
                                       ATT[a]["w"][:, 0:2 * P], start=True, stop=True)
            ins.then_inc(proj_done, 1)

        def pro_v_pe(pe, a, b, par, first=False):
            n = 8 * a + b
            pe.wait_ge(qk_evac, 1 + n + 1)
            for t in range(TPB):
                ins = nc.tensor.matmul(bank7[:, t * P:(t + 1) * P], x_tile(b, par, t, first),
                                       ATT[a]["w"][:, 2 * P:3 * P], start=True, stop=True)
            ins.then_inc(proj_done, 1)

        def pro_dve(dve, a, b, par, first=False):
            A = ATT[a]
            n = 8 * a + b
            if not first:
                dve.wait_ge(z_ready, 1 + n - 1)
            dve.wait_ge(proj_done, 1 + 2 * n + 1)
            dst = qkf[:, par, :].rearrange("p (w s c) -> p w s c", w=2, s=2)
            src = bank7[:, :].rearrange("p (s w c) -> p w s c", w=2, s=2)
            if A["bias"] is None:
                nc.vector.tensor_copy(dst, src).then_inc(qk_evac, 1)
            else:
                bias = A["bias"].rearrange("p (w c) -> p w c", w=2).unsqueeze(2).to_broadcast([P, 2, TPB, P])
                nc.vector.tensor_tensor(dst, src, bias, ALU.add).then_inc(qk_evac, 1)

        def pro_act(act, a, b, par, first=False):
            n = 8 * a + b
            if not first:
                act.wait_ge(av_done, 1 + 8 * (n - 1))
            act.wait_ge(proj_done, 1 + 2 * n + 2)
            nc.scalar.activation(Vaug[:, par, :, :].rearrange("p t (h c) -> p (t h) c", c=32)[:, :, 0:HD],
                                 bank7[:, 0:256].rearrange("p (h c) -> p h c", c=HD),
                                 ACT.Copy).then_inc(v_evac, 1)

        def split(g, eng, own, par):
            Z = Zb[par]
            rows = qkf[:, par, :].rearrange("p (w r d) -> p w r d", w=2, d=HD)
            r1 = res1.rearrange("p (w r d) -> p w r d", w=2, d=HD)
            r2 = res2.rearrange("p (w r d) -> p w r d", w=2, d=HD)
            zs = Z[:, :, :, :, :].rearrange("p w t h s -> p w (t h) s")

            def put(w, src, first_slot, step, count):
                R = TPB * HEADS
                if count == 1:
                    dst = zs[:, w, :, first_slot * HD:(first_slot + 1) * HD]
                    return own.inc(g.tensor_copy(dst, src))
                dst = zs[:, w, :, 0:48].rearrange("p r (s d) -> p r s d", d=HD)[
                    :, :, first_slot:first_slot + step * (count - 1) + 1:step, :]
                return own.inc(g.tensor_copy(dst, src.unsqueeze(2).to_broadcast([P, R, count, HD])))

            own.inc(g.memset(Z[:, 0, :, :, MAXROW:MAXROW + 2], 0.0))
            put(0, rows[:, 0], 0, 1, 3)
            put(1, rows[:, 1], 0, 3, 2)
            put(1, rows[:, 1], 5, 1, 1)
            own.wait(eng)
            for w in range(2):
                own.inc(g.tensor_tensor(r1[:, w], rows[:, w], zs[:, w, :, 0:HD], ALU.subtract))
            own.wait(eng)
            put(0, r1[:, 0], 3, 1, 2)
            put(1, r1[:, 1], 1, 3, 2)
            own.wait(eng)
            own.inc(g.tensor_tensor(r2[:, 0], r1[:, 0], zs[:, 0, :, 3 * HD:4 * HD], ALU.subtract))
            own.inc(g.tensor_tensor(r2[:, 1], r1[:, 1], zs[:, 1, :, HD:2 * HD], ALU.subtract))
            own.wait(eng)
            put(0, r2[:, 0], 5, 1, 1)
            put(1, r2[:, 1], 2, 1, 1)
            own.wait(eng)
            return g.tensor_copy(res2[:, 0:1], res1[:, 0:1])

        def pro_pool(pool, own, a, b, par):
            n = 8 * a + b
            g = nc.gpsimd
            if b > 1:
                pool.wait_ge(proj_done, 1 + 2 * (n - 1))
            g.tensor_copy(xb[:, par, :], xT[:, bass.ds(b * SEQ, SEQ)]).then_inc(xb_ready, 1)
            if b == 1:
                pool.wait_ge(z_ready, 1 + n)
            pool.wait_ge(qk_evac, 1 + n + 1)
            pool.wait_ge(t2_done, 1 + 8 * (n - 1))
            split(g, pool, own, par).then_inc(z_ready, 1)

        def T_pe(pe, a, b, par, h):
            s = slot_of(f"T{h}")
            Z = Zb[par]
            if h == 0:
                pe.wait_ge(z_ready, 1 + 8 * a + b + 1)
            for p in range(4):
                for w in range(2):
                    for t in range(TPB):
                        ins = nc.tensor.transpose(
                            ringb[:, s + p // 2, (p % 2) * 512 + w * 256 + t * P:(p % 2) * 512 + w * 256 + (t + 1) * P],
                            Z[:, w, t, 8 * h + 2 * p:8 * h + 2 * p + 2, :], identb[:, :])
            ins.then_inc(t_done, 1)

        def batch_pe(pe, a, b, par, a_first=False, a_last=False):
            A = ATT[a]
            B = 8 * a + b
            Z = Zb[par]

            def slot_free(use):
                u = USES.index(use)
                was = USES[u - 3]
                if was == "NT0":
                    pe.wait_ge(tev_dve, 2 * B + 1)
                    pe.wait_ge(tev_act, 2 * B + 1)
                elif u < 3:
                    if not a_first:
                        pe.wait_ge(exp_done, 1 + 8 * (B - 1) + int(was[3:]) + 1)
                elif was[0] == "T":
                    pe.wait_ge(tev_dve, 2 * B + int(was[1]) + 1)
                    pe.wait_ge(tev_act, 2 * B + int(was[1]) + 1)
                elif was[:2] == "S1":
                    pe.wait_ge(red_done, 1 + 8 * B + int(was[3:]) + 1)
                else:
                    pe.wait_ge(exp_done, 1 + 8 * B + int(was[3:]) + 1)

            def S1(p):
                slot_free(f"S1_{p}")
                s = slot_of(f"S1_{p}")
                if p in (0, 4):
                    pe.wait_ge(tev_dve, 2 * B + 1 + p // 4)
                if p in (2, 6):
                    pe.wait_ge(tev_act, 2 * B + 1 + p // 4)
                for t in range(TPB):
                    keys = (t + 1) * P if A["causal"] else SEQ
                    ins = nc.tensor.matmul(ring[:, s + t, 0:2 * keys], qT[:, p, t * P:(t + 1) * P],
                                           kT[:, p, :, 0:keys], start=True,
                                           stop=not A["causal"], skip_group_check=True)
                    if A["causal"]:
                        for h in range(2):
                            ins = nc.tensor.matmul(ring[:, s + t, (h + 1) * keys - P:(h + 1) * keys], identb[:, :],
                                                   maskb[:, t, t * P:(t + 1) * P], start=False, stop=(h == 1),
                                                   skip_group_check=True)
                ins.then_inc(s1_done, 1)

            def T2(p):
                pe.wait_ge(m_ready, 8 * B + p + 1)
                pe.wait_ge(q2_evac, 1 + 8 * B + p)
                if p == 0 and not a_last:
                    pe.wait_ge(v_evac, 1 + B + 2)
                for t in range(TPB):
                    ins = nc.tensor.transpose(bank7b[:, t * P:(t + 1) * P], Z[:, 0, t, 2 * p:2 * p + 2, :], identb[:, :])
                ins.then_inc(t2_done, 1)

            def S2(p):
                slot_free(f"S2_{p}")
                s = slot_of(f"S2_{p}")
                pe.wait_ge(q2_evac, 1 + 8 * B + p + 1)
                for h in range(2):
                    for t in range(TPB):
                        from_q = t * P if A["causal"] else 0
                        ins = nc.tensor.matmul(ring[:, s + h, t * SEQ:(t + 1) * SEQ - from_q],
                                               kT[:, p, h, t * P:(t + 1) * P], q2T[:, p % 2, from_q:SEQ],
                                               start=True, stop=not A["causal"], skip_group_check=True)
                        if A["causal"]:
                            ins = nc.tensor.matmul(ring[:, s + h, t * SEQ:t * SEQ + P], identb[:, :],
                                                   maskTb[:, t, t * P:(t + 1) * P], start=False, stop=True,
                                                   skip_group_check=True)
                ins.then_inc(s2_done, 1)

            def AVs(b, par, *pairs):
                for p in pairs:
                    AV_pe(pe, a, b, par, p)

            if not a_last:
                pro_qk_pe(pe, a, b + 1, 1 - par)
            if not a_first:
                AVs(b - 1, 1 - par, 4, 5)
            S1(0)
            S1(1)
            if not a_first:
                AVs(b - 1, 1 - par, 6, 7)
            if not a_last:
                pro_v_pe(pe, a, b + 1, 1 - par)
            slot_free("T1")
            T_pe(pe, a, b, par, 1)
            if not a_first:
                TR_pe(pe, a, b - 1, 1)
            T2(0)
            S1(2)
            for p in range(PAIRS):
                if 0 < p < PAIRS - 2:
                    S1(p + 2)
                if p == 1 and not a_first:
                    OT_pe(pe, a, b - 1)
                if p == 2 and not a_first:
                    out_pe(pe, a, b - 1)
                if p == 3:
                    AVs(b, par, 0, 1)
                if p == 5:
                    AVs(b, par, 2, 3)
                if p == 6:
                    TR_pe(pe, a, b, 0)
                if p + 1 < PAIRS:
                    T2(p + 1)
                if p == PAIRS - 1 and not a_last:
                    slot_free("NT0")
                    T_pe(pe, a, b + 1, 1 - par, 0)
                S2(p)

        def AV_pe(pe, a, b, par, p):
            B = 8 * a + b
            pe.wait_ge(exp_done, 1 + 8 * B + p + 1)
            if p == 0:
                pe.wait_ge(v_evac, 1 + B + 1)
                pe.wait_ge(x_added, 1 + B)
            if p == 4:
                pe.wait_ge(onorm_done, 1 + 2 * B + 1)
            for h in range(2):
                j = 2 * (p % 2) + h
                g = (p // 2) % 2
                for t in range(TPB):
                    head = 2 * p + h
                    from_q = t * P if ATT[a]["causal"] else 0
                    at = (2 * h + t) * SEQ
                    ins = nc.tensor.matmul(bank6[32 * j:32 * j + 32, g * SEQ + from_q:(g + 1) * SEQ],
                                           Vaug[:, par, t, 32 * head:32 * head + 32],
                                           PT[:, p % PTR, at:at + SEQ - from_q],
                                           start=(t == 0), stop=(t == TPB - 1))
            ins.then_inc(av_done, 1)

        def TR_pe(pe, a, b, hf):
            pe.wait_ge(av_evac, 2 * (8 * a + b) + hf + 1)
            for t in range(TPB):
                for g in range(2):
                    ins = nc.tensor.transpose(bank6[:, (2 * t + g) * P:(2 * t + g + 1) * P],
                                              avs[:, g * SEQ + t * P:g * SEQ + (t + 1) * P], ident)
            ins.then_inc(tr_done, 1)

        def OT_pe(pe, a, b):
            pe.wait_ge(onorm_done, 1 + 2 * (8 * a + b) + 2)
            for t in range(TPB):
                ins = nc.tensor.transpose(bank6[:, t * P:(t + 1) * P], onorm[:, t, :], ident)
            ins.then_inc(ot_done, 1)

        def out_pe(pe, a, b):
            A = ATT[a]
            pe.wait_ge(ont_evac, 8 * a + b + 1)
            for t in range(TPB):
                ins = nc.tensor.matmul(bank6[:, t * P:(t + 1) * P], onT[:, t * P:(t + 1) * P], A["wo"],
                                       start=True, stop=A["bo"] is None)
                if A["bo"] is not None:
                    ins = nc.tensor.matmul(bank6[:, t * P:(t + 1) * P], ones[0:1, :], A["bo"][0:1, :],
                                           start=False, stop=True)
            ins.then_inc(outp_done, 1)

        def T_dve(dve, a, b, h):
            B = 8 * a + b
            g = nc.vector
            dve.wait_ge(t_done, 2 * B + h + 1)
            src = ringb[:, slot_of(f"T{h}"), :].rearrange("p (a w n) -> p a w n", a=2, w=2)
            g.tensor_copy(qT[:, 4 * h:4 * h + 2, :], src[:, :, 0, :])
            for half in range(2):
                rows = slice(SLOT * half, SLOT * half + SLOT)
                ins = g.tensor_copy(kT[rows, 4 * h:4 * h + 2, half, :], src[rows, :, 1, :])
            ins.then_inc(tev_dve, 1)

        def batch_dve(dve, own, a, b, par, a_first=False, a_last=False):
            B = 8 * a + b
            g = nc.vector
            Z = Zb[par]

            def red(p):
                s = slot_of(f"S1_{p}")
                dve.wait_ge(s1_done, 8 * B + p + 1)
                if ATT[a]["causal"]:
                    g.tensor_reduce(mrow[:, p, 0:2], ring[:, s, 0:2 * P].rearrange("p (h n) -> p h n", h=2),
                                    AX_X, ALU.max)
                    g.tensor_reduce(mrow[:, p, 2:4], ring[:, s + 1, :].rearrange("p (h n) -> p h n", h=2),
                                    AX_X, ALU.max).then_inc(red_done, 1)
                else:
                    g.tensor_reduce(mrow[:, p, :], ring[:, s:s + 2, :].rearrange("p t (h n) -> p (t h) n", h=2),
                                    AX_X, ALU.max).then_inc(red_done, 1)
                dve.wait_ge(red_done, 1 + 8 * B + p + 1)
                m = mrow[:, p, :].rearrange("p (t h) -> p t h", h=2)
                zc = lambda r: Z[:, 0, :, 2 * p:2 * p + 2, MAXROW + r]
                own.inc(g.tensor_copy(zc(0), m))
                own.wait(dve)
                g.tensor_tensor(zc(1), m, zc(0), ALU.subtract).then_inc(m_ready, 1)

            if not a_last:
                pro_dve(dve, a, b + 1, 1 - par)
            red(0)
            red(1)
            T_dve(dve, a, b, 1)
            red(2)
            if not a_first:
                onorm_dve(dve, own, a, b - 1, 1)
            red(3)
            red(4)
            if not a_first:
                xadd_dve(dve, a, b - 1)
            for p in range(5, PAIRS):
                red(p)
            onorm_dve(dve, own, a, b, 0)
            if not a_last:
                T_dve(dve, a, b + 1, 0)

        def onorm_dve(dve, own, a, b, hf):
            B = 8 * a + b
            g = nc.vector
            dve.wait_ge(tr_done, 1 + 2 * B + hf + 1)
            v = bank6[:, :].rearrange("p (r c) -> p r c", c=32)
            own.inc(g.reciprocal(rec[:, 0:16], v[:, :, HD]))
            own.wait(dve)
            if hf == 0:
                dve.wait_ge(ot_done, 1 + B)
            g.tensor_tensor(onorm[:, :, 64 * hf:64 * hf + 64].rearrange("p t (r d) -> p t r d", d=HD),
                            v[:, :, 0:HD].rearrange("p (t r) d -> p t r d", t=2),
                            rec[:, 0:16].rearrange("p (t r) -> p t r", t=2).unsqueeze(3).to_broadcast([P, 2, 8, HD]),
                            ALU.mult).then_inc(onorm_done, 1)

        def xadd_dve(dve, a, b):
            A = ATT[a]
            B = 8 * a + b
            dve.wait_ge(outp_done, 1 + B + 1)
            nc.vector.tensor_tensor(A["dst"][:, bass.ds(2 * b, 2), :], A["src"][:, bass.ds(2 * b, 2), :],
                                    bank6[:, 0:256].rearrange("p (t c) -> p t c", t=2), ALU.add).then_inc(x_added, 1)

        DVE_PER_BATCH = PAIRS + 2

        def T_act(act, a, b, h):
            B = 8 * a + b
            g = nc.scalar
            act.wait_ge(t_done, 2 * B + h + 1)
            src = ringb[:, slot_of(f"T{h}") + 1, :].rearrange("p (a w n) -> p a w n", a=2, w=2)
            g.activation(qT[:, 4 * h + 2:4 * h + 4, :], src[:, :, 0, :], ACT.Copy)
            for half in range(2):
                rows = slice(SLOT * half, SLOT * half + SLOT)
                ins = g.activation(kT[rows, 4 * h + 2:4 * h + 4, half, :], src[rows, :, 1, :], ACT.Copy)
            ins.then_inc(tev_act, 1)

        def batch_act(act, a, b, par, a_first=False, a_last=False):
            B = 8 * a + b
            g = nc.scalar

            def q2(p):
                act.wait_ge(t2_done, 1 + 8 * B + p + 1)
                act.wait_ge(s2_done, 1 + 8 * B + max(p - 1, 0))
                g.activation(q2T[:, p % 2, :], bank7b[:, 0:256], ACT.Copy).then_inc(q2_evac, 1)

            def ex(p):
                s = slot_of(f"S2_{p}")
                act.wait_ge(s2_done, 1 + 8 * B + p + 1)
                act.wait_ge(av_done, 1 + 8 * B + max(p - PTR + 1, 0))
                width = 2 * SEQ - P if ATT[a]["causal"] else 2 * SEQ
                g.activation(PT[:, p % PTR, :].rearrange("p (h n) -> p h n", h=2)[:, :, 0:width],
                             ring[:, s:s + 2, 0:width], ACT.Exp, scale=SC).then_inc(exp_done, 1)

            if not a_last:
                pro_act(act, a, b + 1, 1 - par)
            if not a_first:
                av_act(act, a, b - 1, 1)
            q2(0)
            T_act(act, a, b, 1)
            for p in range(PAIRS):
                if p + 1 < PAIRS:
                    q2(p + 1)
                if p == 5:
                    av_act(act, a, b, 0)
                ex(p)
                if p == 0 and not a_first:
                    ont_act(act, a, b - 1)
                if p == PAIRS - 2 and not a_last:
                    T_act(act, a, b + 1, 0)

        def av_act(act, a, b, hf):
            B = 8 * a + b
            act.wait_ge(av_done, 1 + 8 * B + 4 * hf + 4)
            act.wait_ge(tr_done, 1 + 2 * B + hf)
            nc.scalar.activation(avs, bank6[:, :], ACT.Copy).then_inc(av_evac, 1)

        def ont_act(act, a, b):
            A = ATT[a]
            B = 8 * a + b
            act.wait_ge(ot_done, 1 + B + 1)
            act.wait_ge(outp_done, 1 + B)
            if A["bv"] is None:
                nc.scalar.activation(onT, bank6[:, 0:256], ACT.Copy).then_inc(ont_evac, 1)
            else:
                nc.scalar.activation(onT, bank6[:, 0:256], ACT.Identity, bias=A["bv"]).then_inc(ont_evac, 1)

        def attention_pe(pe, a):
            pro_qk_pe(pe, a, 0, 0, True)
            pro_v_pe(pe, a, 0, 0, True)
            T_pe(pe, a, 0, 0, 0)
            batch_pe(pe, a, 0, 0, True)
            with pe.Fori(0, BATCH // 2 - 1) as i:
                for par in (1, 0):
                    batch_pe(pe, a, 2 * i + 2 - par, par)
            batch_pe(pe, a, BATCH - 1, 1, a_last=True)
            for p in range(4, PAIRS):
                AV_pe(pe, a, BATCH - 1, 1, p)
            TR_pe(pe, a, BATCH - 1, 1)
            OT_pe(pe, a, BATCH - 1)
            out_pe(pe, a, BATCH - 1)

        def attention_dve(dve, own, a):
            pro_dve(dve, a, 0, 0, True)
            dve.wait_ge(qk_evac, 1 + 8 * a + 1)
            split(nc.vector, dve, own, 0).then_inc(z_ready, 1)
            T_dve(dve, a, 0, 0)
            batch_dve(dve, own, a, 0, 0, True)
            with dve.Fori(0, BATCH // 2 - 1) as i:
                own.enter(i, 2 * DVE_PER_BATCH)
                for par in (1, 0):
                    batch_dve(dve, own, a, 2 * i + 2 - par, par)
                own.leave(BATCH // 2 - 1)
            batch_dve(dve, own, a, BATCH - 1, 1, a_last=True)
            onorm_dve(dve, own, a, BATCH - 1, 1)
            xadd_dve(dve, a, BATCH - 1)

        def attention_act(act, a):
            pro_act(act, a, 0, 0, True)
            T_act(act, a, 0, 0)
            batch_act(act, a, 0, 0, True)
            with act.Fori(0, BATCH // 2 - 1) as i:
                for par in (1, 0):
                    batch_act(act, a, 2 * i + 2 - par, par)
            batch_act(act, a, BATCH - 1, 1, a_last=True)
            av_act(act, a, BATCH - 1, 1)
            ont_act(act, a, BATCH - 1)

        def attention_pool(pool, own, a):
            for b in range(1, BATCH):
                pro_pool(pool, own, a, b, b % 2)

        def new_counts():
            return dict(dve_out=0, act_out=0, pe_out=0, fence=0)


        def bcast(v, width):
            return v.unsqueeze(2).to_broadcast([P, TILES, width])

        def rank_pe(pe, m):
            E = MOE[m]["n"]
            pe.wait_ge(choice_ready, m // 2 + 1)
            for t in range(TILES + 1):
                if t == 0:
                    nc.tensor.matmul(bank6[:, 0:TILES * E], before[:, :], choice[:, 0:TILES * E], start=True, stop=False,
                                     skip_group_check=True)
                else:
                    ins = nc.tensor.matmul(bank6[:, t * E:(TILES + 1) * E], onesb[:, :],
                                           choice[:, (t - 1) * E:t * E].unsqueeze(1).to_broadcast([P, TILES + 1 - t, E]),
                                           start=False, stop=(t == TILES), skip_group_check=True)
            ins.then_inc(ranked, 1)

        def rank_dve(dve, own, m):
            E = MOE[m]["n"]
            J = sorted_tiles(E)
            g = nc.vector
            O = oh[:, :, 0:E]

            def step(ins):
                own.inc(ins)
                own.wait(dve)

            g.tensor_copy(choice[:, 0:TILES * E], O).then_inc(choice_ready, 1)
            dve.wait_ge(ranked, m // 2 + 1)
            R = bank6[:, 0:(TILES + 1) * E].rearrange("p (t e) -> p t e", e=E)
            n_e, scaled, ends, starts = (sort[:, k, 0:E] for k in range(4))
            step(g.tensor_scalar(scaled, R[:, TILES, :], 1.0 / P, None, ALU.mult))
            filled = sortw[:, 0:E * TILES].rearrange("p (e j) -> p e j", j=TILES)
            slot_no = col(common, COMMON, "slot_no")
            step(g.tensor_tensor(filled, scaled.unsqueeze(2).to_broadcast([P, E, TILES]),
                                 slot_no[:, 0:TILES].unsqueeze(1).to_broadcast([P, E, TILES]), ALU.is_gt))
            step(g.tensor_reduce(n_e, filled, AX_X, ALU.add))
            src, k = n_e, 1
            while k < E:
                dst = sort[:, 4 + k.bit_length() % 2, 0:E]
                own.inc(g.tensor_copy(dst[:, 0:k], src[:, 0:k]))
                step(g.tensor_tensor(dst[:, k:E], src[:, k:E], src[:, 0:E - k], ALU.add))
                src, k = dst, 2 * k
            ends = src
            step(g.tensor_tensor(starts, ends, n_e, ALU.subtract))
            step(g.tensor_scalar(starts, starts, float(P), -1.0, ALU.mult, ALU.add))
            at = sortw[:, 0:TILES * E].rearrange("p (t e) -> p t e", e=E)
            step(g.tensor_tensor(at, R[:, 0:TILES, :], starts.unsqueeze(1).to_broadcast([P, TILES, E]), ALU.add))
            step(g.tensor_tensor(at, at, O, ALU.mult))
            step(g.tensor_reduce(mx[:, 3, :], at, AX_X, ALU.add))
            g.tensor_copy(place[:, :], mx[:, 3, :]).then_inc(place_ready, 1)
            past = sortw[:, 0:J * E].rearrange("p (j e) -> p j e", e=E)
            step(g.tensor_tensor(past, ends.unsqueeze(1).to_broadcast([P, J, E]),
                                 slot_no[:, 0:J].unsqueeze(2).to_broadcast([P, J, E]), ALU.is_le))
            step(g.tensor_reduce(tile_e[:, 0:J], past, AX_X, ALU.add))
            step(g.tensor_scalar(tile_e[:, 0:J], tile_e[:, 0:J], float(E - 1), None, ALU.min))
            for which, width in enumerate((SORTED[m]["w1_width"], SORTED[m]["w2_width"])):
                step(g.tensor_scalar(sort[:, 4 + which, 0:32][:, 0:J], tile_e[:, 0:J], float(width), None, ALU.mult))
                ins = g.tensor_copy(tile_col[:, which, 0:J], sort[:, 4 + which, 0:32][:, 0:J])
            ins.then_inc(tiles_ready, 1)

        def router_pe(pe, c, m):
            M = MOE[m]
            E = M["n"]
            for t in range(TILES):
                ins = nc.tensor.matmul(bank7[:, t * E:(t + 1) * E], xT[:, t * P:(t + 1) * P],
                                       col(M["region"], M["plan"], "router"), start=True, stop=True)
            ins.then_inc(pe_out, 1)
            c["pe_out"] += 1
            if m != 1:
                rank_pe(pe, m)
            if m == 0:
                c["dve_out"] += 2
                c["act_out"] += 1
                pe.wait_ge(dve_out, c["dve_out"])
                for t in range(TILES):
                    ins = nc.tensor.transpose(ring[0:E, t // 4, (t % 4) * P:(t % 4 + 1) * P], gate[:, t, 0:E], ident)
                ins.then_inc(pe_out, 1)
                pe.wait_ge(act_out, c["act_out"] + 1)
                for t in range(TILES):
                    ins = nc.tensor.matmul(ring[:, t // 4, (t % 4) * P:(t % 4 + 1) * P], gateT[0:E, t * P:(t + 1) * P],
                                           col(region_a, PACK0, "b2")[0:E, :], start=True, stop=True)
                ins.then_inc(pe_out, 1)
                c["pe_out"] += 2
                c["act_out"] += 1
                c["dve_out"] += 1
                pe.wait_ge(dve_out, c["dve_out"])
            elif m == 1:
                c["dve_out"] += 1
                c["act_out"] += 1

        def router_dve(dve, own, c, m):
            M = MOE[m]
            E = M["n"]
            g = nc.vector
            L, L2, C, O, W = (v[:, :, 0:E] for v in (lg, lg2, cand, oh, gate))
            tie = col(common, COMMON, "tie", 0, E)
            tie = tie.unsqueeze(1).to_broadcast([P, TILES, E])

            def step(ins):
                own.inc(ins)
                own.wait(dve)

            def choose(src, top, first):
                step(g.tensor_reduce(mx[:, top, :], src, AX_X, ALU.max))
                step(g.tensor_tensor(C, src, bcast(mx[:, top, :], E), ALU.is_equal))
                step(g.tensor_tensor(C, C, tie, ALU.mult))
                step(g.tensor_reduce(mx[:, 3, :], C, AX_X, ALU.max))
                step(g.tensor_tensor(first, C, bcast(mx[:, 3, :], E), ALU.is_equal))

            dve.wait_ge(pe_out, c["pe_out"] + 1)
            c["pe_out"] += 1
            src = bank7[:, 0:TILES * E].rearrange("p (t e) -> p t e", e=E)
            if m == 2:
                rb = col(region_b, PACK3, "rbias").unsqueeze(1).to_broadcast([P, TILES, E])
                step(g.tensor_tensor(L, src, rb, ALU.add))
                choose(L, 0, O)
                rank_dve(dve, own, m)
                step(g.tensor_tensor(x[:, :, :], x[:, :, :], z[:, :, :], ALU.add))
            if m == 0:
                step(g.tensor_copy(L, src))
                choose(L, 0, O)
                rank_dve(dve, own, m)
                g.tensor_tensor(L2, L, bcast(mx[:, 0, :], E), ALU.subtract).then_inc(dve_out, 1)
                dve.wait_ge(act_out, c["act_out"] + 1)
                step(g.tensor_reduce(mx[:, 1, :], L2, AX_X, ALU.add))
                step(g.reciprocal(mx[:, 2, :], mx[:, 1, :]))
                g.tensor_tensor(W, O, bcast(mx[:, 2, :], E), ALU.mult).then_inc(dve_out, 1)
                dve.wait_ge(pe_out, c["pe_out"] + 2)
                for q in range(4):
                    ins = g.tensor_tensor(x[:, 4 * q:4 * q + 4, :], x[:, 4 * q:4 * q + 4, :],
                                          ring[:, q, :].rearrange("p (t c) -> p t c", t=4), ALU.add)
                ins.then_inc(dve_out, 1)
                c["pe_out"] += 2
                c["dve_out"] += 3
                dve.wait_ge(dve_out, c["dve_out"])
                c["act_out"] += 2
            if m == 1:
                step(g.tensor_copy(L, src))
                choose(L, 0, O)
                step(g.scalar_tensor_tensor(out=L2, in0=O, scalar=-3.0e38, in1=L, op0=ALU.mult, op1=ALU.add))
                choose(L2, 1, W)
                g.tensor_tensor(mx[:, 2, :], mx[:, 1, :], mx[:, 0, :], ALU.subtract).then_inc(dve_out, 1)
                dve.wait_ge(act_out, c["act_out"] + 1)
                step(g.tensor_scalar(mx[:, 0, :], mx[:, 2, :], 1.0, None, ALU.add))
                step(g.reciprocal(mx[:, 1, :], mx[:, 0, :]))
                step(g.tensor_tensor(mx[:, 2, :], mx[:, 2, :], mx[:, 1, :], ALU.mult))
                step(g.tensor_tensor(O, O, bcast(mx[:, 1, :], E), ALU.mult))
                step(g.tensor_tensor(W, W, bcast(mx[:, 2, :], E), ALU.mult))
                step(g.tensor_tensor(W, W, O, ALU.add))
                step(g.tensor_tensor(x[:, :, :], x[:, :, :], xn[:, :, :], ALU.add))
                c["dve_out"] += 1
                c["act_out"] += 1

        def router_act(act, c, m):
            E = MOE[m]["n"]
            c["pe_out"] += 1
            if m == 0:
                act.wait_ge(dve_out, c["dve_out"] + 1)
                nc.scalar.activation(lg2[:, :, 0:E], lg2[:, :, 0:E], ACT.Exp).then_inc(act_out, 1)
                act.wait_ge(pe_out, c["pe_out"] + 1)
                nc.scalar.activation(gateT[0:E, :], ring[0:E, 0:4, :].rearrange("p q n -> p (q n)"),
                                     ACT.Copy).then_inc(act_out, 1)
                c["dve_out"] += 3
                c["act_out"] += 2
                c["pe_out"] += 2
            elif m == 1:
                act.wait_ge(dve_out, c["dve_out"] + 1)
                nc.scalar.activation(mx[:, 2, :], mx[:, 2, :], ACT.Exp).then_inc(act_out, 1)
                c["dve_out"] += 1
                c["act_out"] += 1

        UNITS = [M["n"] * M["f"] for M in MOE]
        HR = 4
        take = carve()
        hb = take(HR * 512).rearrange("p (r n) -> p r n", r=HR)
        sg = take(HR * 512).rearrange("p (r n) -> p r n", r=HR)

        def experts_pe(pe, m):
            M = MOE[m]
            n, f, gated = M["n"], M["f"], M["gated"]
            F = f * P * (2 if gated else 1)
            w1 = col(M["region"], M["plan"], "w1")
            w2 = col(M["region"], M["plan"], "w2")
            banks = 2 if gated else 4
            with pe.Fori(0, 4) as i:
                base = i * UNITS[m]

                def up(k):
                    e, fc = divmod(k, f)
                    pe.wait_ge(h_ready, 1 + base + max(k - banks + 1, 0))
                    rows = xT[:, bass.ds(i * 512, 512)]
                    if gated:
                        for part in range(2):
                            ins = nc.tensor.matmul(ring[:, 2 * (k % 2) + part, :],
                                                   w1[:, e * F + part * f * P + fc * P:e * F + part * f * P + fc * P + P],
                                                   rows, start=True, stop=True)
                    else:
                        ins = nc.tensor.matmul(ring[:, k % 4, :], w1[:, e * F + fc * P:e * F + fc * P + P], rows,
                                               start=True, stop=True)
                    ins.then_inc(up_done, 1)

                def down(k):
                    e, fc = divmod(k, f)
                    pe.wait_ge(h_ready, 1 + base + k + 1)
                    if fc == 0:
                        pe.wait_ge(y_added, 1 + i * n + max(e - 1, 0))
                    for t in range(4):
                        ins = nc.tensor.matmul(ring[:, 4 + e % 2, t * P:(t + 1) * P], hb[:, k % HR, t * P:(t + 1) * P],
                                               w2[:, (e * f + fc) * P:(e * f + fc + 1) * P],
                                               start=(fc == 0 and t == 0), stop=(fc == f - 1), skip_group_check=True)
                    ins.then_inc(y_done, 1)

                ahead = banks - 1 if gated else 2
                for k in range(ahead):
                    up(k)
                for k in range(n * f):
                    if k + ahead < n * f:
                        up(k + ahead)
                    down(k)

        def experts_act(act, m):
            M = MOE[m]
            n, f, gated = M["n"], M["f"], M["gated"]
            with act.Fori(0, 4) as i:
                base = i * UNITS[m]
                for k in range(n * f):
                    act.wait_ge(up_done, base + k + 1)
                    if gated:
                        act.wait_ge(h_ready, 1 + base + max(k - HR + 1, 0))
                        nc.scalar.activation(sg[:, k % HR, :], ring[:, 2 * (k % 2) + 1, :], M["act"]).then_inc(gate_done, 1)
                    else:
                        act.wait_ge(y_done, 1 + base + max(k - HR + 1, 0))
                        nc.scalar.activation(hb[:, k % HR, :], ring[:, k % 4, :], M["act"]).then_inc(h_ready, 1)

        def experts_dve(dve, m):
            M = MOE[m]
            n, f, gated = M["n"], M["f"], M["gated"]
            g = nc.vector
            with dve.Fori(0, 4) as i:
                base = i * UNITS[m]

                def add(e):
                    dve.wait_ge(y_done, 1 + base + e * f + f)
                    dve.wait_ge(y_added, 1 + i * n + e)
                    for t in range(4):
                        row = x[:, bass.ds(4 * i + t, 1), :]
                        ins = g.scalar_tensor_tensor(out=row, in0=ring[:, 4 + e % 2, t * P:(t + 1) * P].unsqueeze(1),
                                                     scalar=gate[:, bass.ds(4 * i + t, 1), e], in1=row,
                                                     op0=ALU.mult, op1=ALU.add)
                    ins.then_inc(y_added, 1)

                for k in range(n * f):
                    if gated:
                        dve.wait_ge(gate_done, i * UNITS[m] + k + 1)
                        dve.wait_ge(y_done, 1 + base + max(k - HR + 1, 0))
                        g.tensor_tensor(hb[:, k % HR, :], sg[:, k % HR, :], ring[:, 2 * (k % 2), :],
                                        ALU.mult).then_inc(h_ready, 1)
                    if k % f == 0 and k > 0:
                        add(k // f - 1)
                add(n - 1)

        take = carve()
        sorted_y = take(sorted_tiles(L0E) * P).rearrange("p (t n) -> p t n", n=P)
        sorted_rows = take(4 * P).rearrange("p (r n) -> p r n", r=4)
        sorted_rowsT = take(2 * P).rearrange("p (r n) -> p r n", r=2)
        sorted_h = take(2 * 512).rearrange("p (r n) -> p r n", r=2)
        w1t = take(2 * 516).rearrange("p (r n) -> p r n", r=2)
        w2t = take(2 * 512).rearrange("p (r n) -> p r n", r=2)
        rows_back = xT.rearrange("p (t n) -> p t n", n=P)
        TBANK = (bank6, bank7)

        def tile_no(m, j):
            return j + (sorted_tiles(L0E) if m else 0)

        def earlier(eng, s, m, j):
            if m or not isinstance(j, int) or j > 1:
                eng.wait_ge(s, tile_no(m, 0) + j)

        def over_tiles(eng, m, step, lead=1, tail=1):
            J = sorted_tiles(MOE[m]["n"])
            for j in range(lead):
                step(j, j % 4, j // 4)
            groups = (J - lead - tail) // 4
            with eng.Fori(0, groups) as i:
                for k in range(4):
                    step(4 * i + lead + k, (lead + k) % 4, i + (lead + k) // 4)
            for j in range(lead + 4 * groups, J):
                step(j, j % 4, j // 4)

        def sorted_sp(sp, m):
            J = sorted_tiles(MOE[m]["n"])
            first = tile_no(m, 0)

            def load(j, slot):
                sp.dma_start(sorted_rows[:, slot, :], sorted_in[bass.ds(j * P, P), :]).then_inc(rows_in[slot], 16)

            sp.wait_ge(scattered, 16 * TILES * (m // 2 + 1))
            for j in range(4):
                load(j, j)

            def step(j, slot, turn):
                sp.wait_ge(rows_T, first + j + 1)
                load(j + 4, slot)
            groups = (J - 4) // 4
            with sp.Fori(0, groups) as i:
                for k in range(4):
                    step(4 * i + k, k, i)
            for j in range(4 * groups, J - 4):
                step(j, j % 4, j // 4)

        def sorted_pe(pe, m):
            M = MOE[m]
            J, f, first = sorted_tiles(M["n"]), M["f"], tile_no(m, 0)

            def T(j, slot, turn):
                used = len(range(slot, sorted_tiles(L0E), 4)) if m else 0
                pe.wait_ge(rows_in[slot], 16 * (used + turn + 1))
                earlier(pe, rows_evac, m, j)
                nc.tensor.transpose(TBANK[slot % 2][:, 0:P], sorted_rows[:, slot, :], ident).then_inc(rows_T, 1)

            def up(j, s):
                pe.wait_ge(w1_ready, first + j + 1)
                pe.wait_ge(rows_evac, first + j + 2)
                earlier(pe, tile_h, m, j)
                for fc in range(f):
                    ins = nc.tensor.matmul(ring[:, s, fc * P:(fc + 1) * P], w1t[:, s, fc * P:(fc + 1) * P],
                                           sorted_rowsT[:, s, :], start=True, stop=True)
                ins.then_inc(tile_up, 1)

            def down(j, s):
                pe.wait_ge(tile_h, first + j + 2)
                pe.wait_ge(w2_ready, first + j + 1)
                earlier(pe, tile_y, m, j)
                for fc in range(f):
                    ins = nc.tensor.matmul(ring[:, 2 + s, 0:P], sorted_h[:, s, fc * P:(fc + 1) * P],
                                           w2t[:, s, fc * P:(fc + 1) * P], start=(fc == 0), stop=(fc == f - 1))
                ins.then_inc(tile_down, 1)

            def step(j, slot, turn):
                if not (isinstance(j, int) and j == J - 1):
                    T(j + 1, (slot + 1) % 4, turn + (slot + 1) // 4)
                up(j, slot % 2)
                if not (isinstance(j, int) and j == 0):
                    down(j - 1, (slot + 1) % 2)

            T(0, 0, 0)
            over_tiles(pe, m, step)
            down(J - 1, (J - 1) % 2)

        def sorted_dve(dve, own, m):
            M = MOE[m]
            J, first, W = sorted_tiles(M["n"]), tile_no(m, 0), SORTED[m]["w2_width"]
            g = nc.vector
            w2 = col(M["region"], M["plan"], "w2")

            def rows_out_of_bank(j, s):
                dve.wait_ge(rows_T, first + j + 1)
                earlier(dve, tile_up, m, j)
                if m == 0:
                    ins = g.tensor_copy(sorted_rowsT[:, s, :], TBANK[s][:, 0:P])
                else:
                    ins = g.tensor_scalar(sorted_rowsT[:, s, :], TBANK[s][:, 0:P], col(region_b, PACK3, "ln2w"),
                                          col(region_b, PACK3, "ln2b"), ALU.mult, ALU.add)
                ins.then_inc(rows_evac, 1)

            def y_out_of_bank(j, s):
                dve.wait_ge(tile_down, first + j + 2)
                g.tensor_copy(sorted_y[:, bass.ds(j, 1), :], ring[:, 2 + s, 0:P].unsqueeze(1)).then_inc(tile_y, 1)

            def step(j, slot, turn):
                s = slot % 2
                if not (isinstance(j, int) and j == J - 1):
                    rows_out_of_bank(j + 1, 1 - s)
                at = dve.value_load(tile_col[0:1, 1, bass.ds(j, 1)], min_val=0, max_val=(M["n"] - 1) * W)
                earlier(dve, tile_down, m, j)
                g.tensor_copy(w2t[:, s, 0:W], w2[:, bass.ds(at, W)]).then_inc(w2_ready, 1)
                if not (isinstance(j, int) and j == 0):
                    y_out_of_bank(j - 1, 1 - s)

            dve.wait_ge(tiles_ready, m // 2 + 1)
            rows_out_of_bank(0, 0)
            over_tiles(dve, m, step)
            y_out_of_bank(J - 1, (J - 1) % 2)
            for q in range(4):
                dve.wait_ge(gathered[q], 16 * 4 * (m // 2 + 1))
                if m == 0:
                    for t in range(4 * q, 4 * q + 4):
                        g.scalar_tensor_tensor(out=x[:, t, :], in0=rows_back[:, t, :], scalar=mx[:, 2, t:t + 1], in1=x[:, t, :],
                                               op0=ALU.mult, op1=ALU.add)
                else:
                    g.tensor_tensor(x[:, 4 * q:4 * q + 4, :], x[:, 4 * q:4 * q + 4, :], rows_back[:, 4 * q:4 * q + 4, :], ALU.add)

        def sorted_act(act, m):
            M = MOE[m]
            J, first, f = sorted_tiles(M["n"]), tile_no(m, 0), M["f"]

            def store(j):
                act.wait_ge(tile_y, first + j + 2)
                nc.scalar.dma_start(sorted_out[bass.ds(j * P, P), :], sorted_y[:, bass.ds(j, 1), :].rearrange("p t n -> p (t n)")
                                    ).then_inc(rows_out, 16)

            def step(j, slot, turn):
                s = slot % 2
                act.wait_ge(tile_up, first + j + 2)
                earlier(act, tile_down, m, j)
                if m == 0:
                    for fc in range(f):
                        ins = nc.scalar.activation(sorted_h[:, s, fc * P:(fc + 1) * P], ring[:, s, fc * P:(fc + 1) * P], M["act"],
                                                   bias=w1t[:, s, f * P + fc:f * P + fc + 1])
                else:
                    ins = nc.scalar.activation(sorted_h[:, s, 0:f * P], ring[:, s, 0:f * P], M["act"])
                ins.then_inc(tile_h, 1)
                if not (isinstance(j, int) and j < 2):
                    store(j - 2)

            over_tiles(act, m, step, lead=2)
            store(J - 2)
            store(J - 1)

        def sorted_pool(pool, m):
            M = MOE[m]
            J, first, W = sorted_tiles(M["n"]), tile_no(m, 0), SORTED[m]["w1_width"]
            source = xn if m == 0 else y
            w1 = col(M["region"], M["plan"], "w1")
            pool.wait_ge(place_ready, m // 2 + 1)
            for t in range(TILES):
                nc.gpsimd.indirect_dma_start(sorted_in, bass.IndirectOffsetOnAxis(place[:, t:t + 1], 0), source[:, t, :],
                                             None).then_inc(scattered, 16)
            pool.wait_ge(tiles_ready, m // 2 + 1)
            for j in range(J):
                at = pool.value_load(tile_col[0:1, 0, j:j + 1], min_val=0, max_val=(M["n"] - 1) * W)
                earlier(pool, tile_h, m, j)
                nc.gpsimd.tensor_copy(w1t[:, j % 2, 0:W], w1[:, bass.ds(at, W)]).then_inc(w1_ready, 1)
            pool.wait_ge(rows_out, 16 * tile_no(m, J))
            for t in range(TILES):
                nc.gpsimd.indirect_dma_start(rows_back[:, t, :], None, sorted_out,
                                             bass.IndirectOffsetOnAxis(place[:, t:t + 1], 0)).then_inc(gathered[t // 4], 16)

        take = carve()
        xc, qu, qv, kk, ap, t1, t2 = (take(512) for _ in range(7))
        vs, sgl, Pm, PTs, wv, wvT = (take(1024).rearrange("p (t n) -> p t n", t=4) for _ in range(6))
        neg_max = sb("neg_max", [P, 4])
        row_sum = sb("row_sum", [P, 4])
        row_rec = sb("row_rec", [P, 4])
        r_pe, r_dve, r_act, r_pool = (sem("rel_" + k) for k in ("pe", "dve", "act", "pool"))
        both = lambda *names: [n + s for n in names for s in "01"]
        REL = dict(pe=["qk0", "vg0", "qk1", "vg1"] + both("a", "scores", "PT", "av", "wvT", "res"),
                   dve=["k0", "v0", "k1", "v1"] + both("ap", "max", "PT", "wv", "x"),
                   act=["q0", "q1"] + both("silu", "exp", "wvT"))
        REL_FROM = 16

        def rel_at(i, who, what, back=0):
            return REL_FROM + (i - back) * len(REL[who]) + REL[who].index(what) + 1

        def rel_banks(s):
            return ring[:, 3 * s, :], ring[:, 3 * s + 1, :], ring[:, 3 * s + 2, :], (bank6, bank7)[s][:, :]

        def half(v, s):
            return v[:, s * SEQ:(s + 1) * SEQ]

        def rel_pe(pe):
            R = lambda name: col(region_a, PACK2, name)
            mm = nc.tensor.matmul
            with pe.Fori(0, 4) as i:
                def dve_did(what, s, back=0):
                    pe.wait_ge(r_dve, rel_at(i, "dve", f"{what}{s}", back))

                def act_did(what, s, back=0):
                    pe.wait_ge(r_act, rel_at(i, "act", f"{what}{s}", back))

                for s in range(2):
                    b0, b1, b2, b3 = rel_banks(s)
                    rows = xT[:, bass.ds(i * 512 + s * SEQ, SEQ)]
                    act_did("wvT", s, 1)
                    mm(b0[:, 0:256], R("wq"), rows, start=True, stop=True)
                    mm(b0[:, 256:512], R("wk"), rows, start=True, stop=True).then_inc(r_pe, 1)
                    dve_did("wv", s, 1)
                    if s == 0:
                        pe.wait_ge(r_pool, i + 1)
                    for t in range(2):
                        lhs = half(xc, s)[:, t * P:(t + 1) * P]
                        mm(b1[:, t * 256:t * 256 + 256], lhs, R("wvg")[:, 0:256], start=True, stop=True)
                        ins = mm(b2[:, t * 256:t * 256 + 256], lhs, R("wvg")[:, 256:512], start=True, stop=True)
                    ins.then_inc(r_pe, 1)
                for s in range(2):
                    b0, b1, b2, b3 = rel_banks(s)
                    act_did("q", s)
                    dve_did("x", s, 1)
                    mm(b3[:, 0:256], R("wrT"), half(qv, s), start=True, stop=True)
                    mm(b3[:, 256:512], R("wrTs"), half(qv, s), start=True, stop=True).then_inc(r_pe, 1)
                for s in range(2):
                    b0, b1, b2, b3 = rel_banks(s)
                    dve_did("ap", s)
                    for t in range(2):
                        o = b0[:, t * 256:(t + 1) * 256]
                        here = slice(t * P, (t + 1) * P)
                        mm(o, identb[:, :], maskb[:, t, :], start=True, stop=False)
                        mm(o, half(qu, s)[:, here], half(kk, s), start=False, stop=False)
                        ins = mm(o, half(ap, s)[:, here], R("pos"), start=False, stop=True)
                    ins.then_inc(r_pe, 1)
                for s in range(2):
                    b0, b1, b2, b3 = rel_banks(s)
                    act_did("exp", s)
                    for j in range(2):
                        for t in range(2):
                            ins = nc.tensor.transpose(b1[:, j * 256 + t * P:j * 256 + (t + 1) * P],
                                                      Pm[:, 2 * s + t, j * P:(j + 1) * P], ident)
                    ins.then_inc(r_pe, 1)
                for s in range(2):
                    b0, b1, b2, b3 = rel_banks(s)
                    dve_did("PT", s)
                    act_did("silu", s)
                    for t in range(2):
                        for j in range(2):
                            ins = mm(b2[:, t * 256:(t + 1) * 256], PTs[:, 2 * s + j, t * P:(t + 1) * P],
                                     vs[:, 2 * s + j, :], start=(j == 0), stop=(j == 1))
                    ins.then_inc(r_pe, 1)
                for s in range(2):
                    b0, b1, b2, b3 = rel_banks(s)
                    dve_did("wv", s)
                    for t in range(2):
                        for j in range(2):
                            ins = nc.tensor.transpose(b0[:, t * 256 + j * P:t * 256 + (j + 1) * P],
                                                      wv[:, 2 * s + t, j * P:(j + 1) * P], ident)
                    ins.then_inc(r_pe, 1)
                for s in range(2):
                    b0, b1, b2, b3 = rel_banks(s)
                    act_did("wvT", s)
                    for t in range(2):
                        for j in range(2):
                            ins = mm(b3[:, t * P:(t + 1) * P], wvT[:, 2 * s + t, j * P:(j + 1) * P],
                                     R("wo")[:, j * P:(j + 1) * P], start=(j == 0), stop=(j == 1))
                    ins.then_inc(r_pe, 1)

        def rel_dve(dve, own):
            g = nc.vector
            R = lambda name: col(region_a, PACK2, name)
            tiles = lambda b: b.rearrange("p (t n) -> p t n", t=2)
            with dve.Fori(0, 4) as i:
                own.enter(i, 6)

                def pe_did(what, s):
                    dve.wait_ge(r_pe, rel_at(i, "pe", f"{what}{s}"))

                for s in range(2):
                    b0, b1, b2, b3 = rel_banks(s)
                    pe_did("qk", s)
                    g.tensor_copy(half(kk, s), b0[:, 256:512]).then_inc(r_dve, 1)
                    pe_did("vg", s)
                    g.tensor_copy(vs[:, 2 * s:2 * s + 2, :], tiles(b1)).then_inc(r_dve, 1)
                for s in range(2):
                    b0, b1, b2, b3 = rel_banks(s)
                    pe_did("a", s)
                    own.inc(g.tensor_tensor(half(t1, s), b3[:, 0:256], R("rot_a"), ALU.mult))
                    own.inc(g.tensor_tensor(half(t2, s), b3[:, 256:512], R("rot_b"), ALU.mult))
                    own.wait(dve)
                    g.tensor_tensor(half(ap, s), half(t1, s), half(t2, s), ALU.add).then_inc(r_dve, 1)
                for s in range(2):
                    b0, b1, b2, b3 = rel_banks(s)
                    pe_did("scores", s)
                    g.tensor_reduce(neg_max[:, 2 * s:2 * s + 2], tiles(b0), AX_X, ALU.max, negate=True).then_inc(r_dve, 1)
                for s in range(2):
                    b0, b1, b2, b3 = rel_banks(s)
                    dve.wait_ge(r_act, rel_at(i, "act", f"exp{s}"))
                    own.inc(g.reciprocal(row_rec[:, 2 * s:2 * s + 2], row_sum[:, 2 * s:2 * s + 2]))
                    pe_did("PT", s)
                    g.tensor_copy(PTs[:, 2 * s:2 * s + 2, :], tiles(b1)).then_inc(r_dve, 1)
                own.wait(dve)
                for s in range(2):
                    b0, b1, b2, b3 = rel_banks(s)
                    pe_did("av", s)
                    for t in range(2):
                        ins = g.scalar_tensor_tensor(out=wv[:, 2 * s + t, :], in0=b2[:, t * 256:(t + 1) * 256],
                                                     scalar=row_rec[:, 2 * s + t:2 * s + t + 1], in1=sgl[:, 2 * s + t, :],
                                                     op0=ALU.mult, op1=ALU.mult)
                    ins.then_inc(r_dve, 1)
                for s in range(2):
                    b0, b1, b2, b3 = rel_banks(s)
                    pe_did("res", s)
                    rows = x[:, bass.ds(4 * i + 2 * s, 2), :]
                    g.tensor_tensor(rows, rows, b3[:, 0:256].rearrange("p (t c) -> p t c", t=2), ALU.add).then_inc(r_dve, 1)
                own.leave(4)

        def rel_act(act):
            g = nc.scalar
            R = lambda name: col(region_a, PACK2, name)
            tiles = lambda b: b.rearrange("p (t n) -> p t n", t=2)
            with act.Fori(0, 4) as i:
                def pe_did(what, s):
                    act.wait_ge(r_pe, rel_at(i, "pe", f"{what}{s}"))

                for s in range(2):
                    b0, b1, b2, b3 = rel_banks(s)
                    pe_did("qk", s)
                    act.wait_ge(r_dve, rel_at(i, "dve", f"k{s}"))
                    tau = float(P) ** -0.5
                    g.activation(half(qu, s), b0[:, 0:256], ACT.Identity, scale=tau, bias=R("u"))
                    g.activation(half(qv, s), b0[:, 0:256], ACT.Identity, scale=tau, bias=R("v")).then_inc(r_act, 1)
                for s in range(2):
                    b0, b1, b2, b3 = rel_banks(s)
                    pe_did("vg", s)
                    g.activation(sgl[:, 2 * s:2 * s + 2, :], tiles(b2), ACT.Silu).then_inc(r_act, 1)
                for s in range(2):
                    b0, b1, b2, b3 = rel_banks(s)
                    act.wait_ge(r_dve, rel_at(i, "dve", f"max{s}"))
                    for t in range(2):
                        ins = g.activation(Pm[:, 2 * s + t, :], b0[:, t * 256:t * 256 + 256], ACT.Exp,
                                           bias=neg_max[:, 2 * s + t:2 * s + t + 1],
                                           accum_out=row_sum[:, 2 * s + t:2 * s + t + 1])
                    ins.then_inc(r_act, 1)
                for s in range(2):
                    b0, b1, b2, b3 = rel_banks(s)
                    pe_did("wvT", s)
                    g.activation(wvT[:, 2 * s:2 * s + 2, :], tiles(b0), ACT.Copy).then_inc(r_act, 1)

        def rel_pool(pool):
            for i in range(4):
                if i:
                    pool.wait_ge(r_pe, rel_at(i, "pe", "vg1", 1))
                nc.gpsimd.tensor_copy(xc, xT[:, bass.ds(i * 512, 512)]).then_inc(r_pool, 1)

        take = carve()
        H = take(BATCH * 512)
        Sel = take(2 * 1024).rearrange("p (b t n) -> p b t n", b=2, t=2)
        Gsel = take(2 * 1024).rearrange("p (b t n) -> p b t n", b=2, t=2)
        pr, cur0, cur1, cum, slot = (take(SEQ) for _ in range(5))
        xg = [sb(f"xg{b}", [P, TPB, P]) for b in range(2)]
        spread = sb("spread", [P, 2, 512], BF16)
        slotb = sb("slotb", [P, SEQ], BF16)
        spT = sb("spT", [P, 4, P])
        top8 = sb("top8", [P, 8])
        vals = sb("vals", [P, BATCH * 4])
        k1 = sb("k1", [P, 4])
        h12 = take(4 * SEQ).rearrange("p (r n) -> p r n", r=4)
        Hc = Gsel[:, :, 0, 0:512]
        hs = Gsel[:, :, 1, 0:512]
        ST = Sel
        g_pool, g_sel, g_val, g_rows, g_H = (sem("g_" + k) for k in ("pool", "sel", "val", "rows", "H"))
        m_pe, m_act, m_dve = (sem("mlp_" + k) for k in ("pe", "act", "dve"))
        c_rows = sem("c_rows")
        c_pool, c_tr, c_sb, c_hs, c_st, c_out, c_add = (sem("c_" + k) for k in
                                                        ("pool", "tr", "sb", "hs", "st", "out", "add"))

        def top_pe(pe, c):
            mm = nc.tensor.matmul
            router = col(region_a, PACK2, "router")
            for b in range(BATCH):
                ins = mm(bank6[:, 0:SEQ], router[:, 112 - 16 * b:240 - 16 * b], xT[:, b * SEQ:(b + 1) * SEQ],
                         start=(b == 0), stop=(b == BATCH - 1))
            ins.then_inc(pe_out, 1)
            pe.wait_ge(dve_out, c["dve_out"] + 2)
            for t in range(TPB):
                nc.tensor.transpose(bank7[:, t * P:(t + 1) * P], slot[:, t * P:(t + 1) * P], ident)
                ins = nc.tensor.transpose(bank7[:, (2 + t) * P:(3 + t) * P], pr[:, t * P:(t + 1) * P], ident)
            ins.then_inc(pe_out, 1)
            with pe.Fori(0, BATCH // 2) as i:
                for par in range(2):
                    b = 2 * i + par
                    pe.wait_ge(g_pool, b + 1)
                    pe.wait_ge(g_sel, b + 1)
                    pe.wait_ge(g_H, b + 1)
                    for t in range(TPB):
                        ins = mm(ring[:, par, :], xg[par][:, t, :], Sel[:, par, t, :], start=(t == 0), stop=(t == TPB - 1))
                    ins.then_inc(g_rows, 1)
                    pe.wait_ge(g_val, b + 1)
                    for q in range(4):
                        for t in range(TPB):
                            ins = mm(ring[:, 2 + par, q:q + 1], Gsel[:, par, t, q * P:(q + 1) * P], ones[:, 0:1],
                                     start=(t == 0), stop=(t == TPB - 1))
                    ins.then_inc(g_rows, 1)
            Hv = H.rearrange("p (b e k) -> p b e k", b=BATCH, e=L2E)
            pe.wait_ge(g_H, 2 + BATCH)
            for s in range(L2E + 2):
                for layer in range(3):
                    e = s - layer
                    if not 0 <= e < L2E:
                        continue
                    w = col(region_a, PACK2, f"w{layer + 1}", e * P, P)
                    o = ring[:, 2 * layer + e % 2, 0:SEQ]
                    if layer == 0:
                        if e >= 2:
                            pe.wait_ge(m_act, MLP_ACT.index((0, e - 2)) + 1)
                        rhs, o = Hv[:, :, e, :], o.rearrange("p (b k) -> p b k", b=BATCH)
                    else:
                        pe.wait_ge(m_act, MLP_ACT.index((layer - 1, e)) + 1)
                        if layer == 2 and e >= 2:
                            pe.wait_ge(m_dve, e - 1)
                        rhs = h12[:, 2 * (layer - 1) + e % 2, :]
                    mm(o, w, rhs, start=True, stop=True).then_inc(m_pe, 1)
            pe.wait_ge(m_dve, L2E)
            with pe.Fori(0, BATCH // 2) as i:
                for par in range(2):
                    b = 2 * i + par
                    pe.wait_ge(c_rows, b + 1)
                    pe.wait_ge(c_hs, b + 1)
                    for q in range(4):
                        ins = nc.tensor.transpose(ring[:, par, q * P:(q + 1) * P], Hc[:, par, q * P:(q + 1) * P], ident)
                    ins.then_inc(c_tr, 1)
                    pe.wait_ge(c_pool, b + 1)
                    pe.wait_ge(c_st, b + 1)
                    for q in range(4):
                        ins = mm(ring[:, 2 + 2 * par + q // 2, (q % 2) * SEQ:(q % 2 + 1) * SEQ],
                                 spread[:, par, q * P:(q + 1) * P], slotb[:, :], start=True, stop=True)
                    ins.then_inc(c_sb, 1)
                for par in range(2):
                    b = 2 * i + par
                    pe.wait_ge(c_hs, 2 + b + 1)
                    pe.wait_ge(c_st, 2 + b + 1)
                    pe.wait_ge(c_add, b + 1)
                    bank = (bank6, bank7)[par]
                    for t in range(TPB):
                        for q in range(4):
                            ins = mm(bank[:, t * P:(t + 1) * P], STv(par)[:, q, t * P:(t + 1) * P],
                                     hs[:, par, q * P:(q + 1) * P], start=(q == 0), stop=(q == 3))
                    ins.then_inc(c_out, 1)
            c["pe_out"] += 2
            c["dve_out"] += 2
            c["act_out"] += 2

        def STv(par):
            return ST[:, par, :, :].rearrange("p t (q n) -> p (t q) n", q=2)

        MLP_ORDER = [(s - layer, layer) for s in range(L2E + 2) for layer in range(3) if 0 <= s - layer < L2E]
        MLP_ACT = [(layer, e) for e, layer in MLP_ORDER if layer < 2]

        def top_dve(dve, own, c):
            g = nc.vector

            def step(ins):
                own.inc(ins)
                own.wait(dve)

            dve.wait_ge(pe_out, c["pe_out"] + 1)
            step(g.tensor_scalar(cur0, bank6[:, 0:SEQ], col(region_a, PACK2, "rb"), None, ALU.add))
            g.tensor_reduce(k1[:, 0:1], cur0, AX_X, ALU.max, negate=True).then_inc(dve_out, 1)
            dve.wait_ge(act_out, c["act_out"] + 1)
            step(g.reciprocal(k1[:, 2:3], k1[:, 1:2]))
            step(g.tensor_scalar(pr, cur1, k1[:, 2:3], None, ALU.mult))
            cur, nxt = pr, cur0
            for r in range(L2K // 8):
                step(g.max(top8[:, :], cur))
                step(g.match_replace(out=nxt, in_to_replace=top8[:, :], in_values=cur, imm_value=-1.0))
                cur, nxt = nxt, (cur1 if nxt is cur0 else cur0)
            taken = nxt
            step(g.tensor_scalar(taken, cur, 0.0, None, ALU.is_lt))
            step(g.tensor_tensor_scan(cum, col_ones(), taken, 0.0, ALU.mult, ALU.add))
            step(g.tensor_tensor(cum, cum, taken, ALU.mult))
            step(g.tensor_scalar(slotb[:, :], cum, -1.0, None, ALU.add))
            g.tensor_scalar(slot, cum, -1.0, None, ALU.add).then_inc(dve_out, 1)
            dve.wait_ge(act_out, c["act_out"] + 2)
            number = col(common, COMMON, "slot_no").unsqueeze(1).to_broadcast([P, L2E, L2K])
            with dve.Fori(0, BATCH // 2) as i:
                for par in range(2):
                    b = 2 * i + par
                    dve.wait_ge(g_rows, 2 * b + 1)
                    for t in range(TPB):
                        of = spT[:, t, bass.ds(16 * b, 16)].unsqueeze(2).to_broadcast([P, L2E, L2K])
                        ins = g.tensor_tensor(Sel[:, par, t, :].rearrange("p (e k) -> p e k", e=L2E), of, number,
                                              ALU.is_equal)
                    ins.then_inc(g_sel, 1)
                    dve.wait_ge(g_sel, b + 1)
                    for t in range(TPB):
                        pt = spT[:, 2 + t, bass.ds(16 * b, 16)].unsqueeze(2).to_broadcast([P, L2E, L2K])
                        ins = g.tensor_tensor(Gsel[:, par, t, :].rearrange("p (e k) -> p e k", e=L2E),
                                              Sel[:, par, t, :].rearrange("p (e k) -> p e k", e=L2E), pt, ALU.mult)
                    ins.then_inc(g_val, 1)
            Hv = H.rearrange("p (b e k) -> p b e k", b=BATCH, e=L2E)
            for e in range(L2E):
                dve.wait_ge(m_pe, MLP_ORDER.index((e, 2)) + 1)
                g.tensor_scalar(Hv[:, :, e, :], ring[:, 4 + e % 2, 0:SEQ].rearrange("p (b k) -> p b k", b=BATCH),
                                col(region_a, PACK2, "b3", e, 1), None, ALU.add).then_inc(m_dve, 1)
            dve.wait_ge(g_H, 2 + BATCH)
            with dve.Fori(0, BATCH // 2) as i:
                for par in range(2):
                    b = 2 * i + par
                    dve.wait_ge(c_tr, 2 + b + 1)
                    dve.wait_ge(c_out, b + 1)
                    g.tensor_tensor(hs[:, par, :].rearrange("p (q n) -> p q n", q=4),
                                    ring[:, par, :].rearrange("p (q n) -> p q n", q=4),
                                    vals[:, bass.ds(4 * b, 4)].unsqueeze(2).to_broadcast([P, 4, P]),
                                    ALU.mult).then_inc(c_hs, 1)
                    dve.wait_ge(c_sb, 2 + b + 1)
                    g.tensor_scalar(STv(par), ring[:, 2 + 2 * par:4 + 2 * par, :].rearrange("p a (q n) -> p (a q) n", q=2),
                                    col(common, COMMON, "slot_of_row"), None, ALU.is_equal).then_inc(c_st, 1)
                for par in range(2):
                    b = 2 * i + par
                    dve.wait_ge(c_out, 2 + b + 1)
                    rows = x[:, bass.ds(2 * b, 2), :]
                    g.tensor_tensor(rows, rows, (bank6, bank7)[par][:, 0:SEQ].rearrange("p (t c) -> p t c", t=2),
                                    ALU.add).then_inc(c_add, 1)
            c["pe_out"] += 2
            c["dve_out"] += 2
            c["act_out"] += 2

        def col_ones():
            return ones[:, 0:1].to_broadcast([P, SEQ])

        def top_act(act, c):
            g = nc.scalar
            act.wait_ge(dve_out, c["dve_out"] + 1)
            g.activation(cur1, cur0, ACT.Exp, bias=k1[:, 0:1], accum_out=k1[:, 1:2]).then_inc(act_out, 1)
            act.wait_ge(pe_out, c["pe_out"] + 2)
            g.activation(spT[:, :, :], bank7[:, :].rearrange("p (t n) -> p t n", t=4), ACT.Copy).then_inc(act_out, 1)
            with act.Fori(0, BATCH // 2) as i:
                for par in range(2):
                    b = 2 * i + par
                    act.wait_ge(g_rows, 3 + 2 * b + 1)
                    g.activation(H[:, bass.ds(b * 512, 512)], ring[:, par, :], ACT.Copy)
                    act.wait_ge(g_rows, 3 + 2 * b + 2)
                    g.activation(vals[:, bass.ds(4 * b, 4)], ring[:, 2 + par, 0:4], ACT.Copy).then_inc(g_H, 1)
            for layer, e in MLP_ACT:
                act.wait_ge(m_pe, MLP_ORDER.index((e, layer)) + 1)
                if e >= 2:
                    act.wait_ge(m_pe, MLP_ORDER.index((e - 2, layer + 1)) + 1)
                g.activation(h12[:, 2 * layer + e % 2, :], ring[:, 2 * layer + e % 2, 0:SEQ], ACT.Relu,
                             bias=col(region_a, PACK2, f"b{layer + 1}", e, 1)).then_inc(m_act, 1)
            act.wait_ge(m_dve, L2E)
            with act.Fori(0, BATCH // 2) as i:
                for par in range(2):
                    b = 2 * i + par
                    act.wait_ge(c_tr, b + 1)
                    g.activation(Hc[:, par, :], H[:, bass.ds(b * 512, 512)], ACT.Copy).then_inc(c_rows, 1)
            c["pe_out"] += 2
            c["dve_out"] += 2
            c["act_out"] += 2

        def top_pool(pool, c):
            g = nc.gpsimd
            for i in range(BATCH // 2):
                for par in range(2):
                    b = 2 * i + par
                    pool.wait_ge(g_rows, 2 * b + 1)
                    g.tensor_copy(xg[par][:, :, :], xn[:, bass.ds(2 * b, 2), :]).then_inc(g_pool, 1)
            for i in range(BATCH // 2):
                for par in range(2):
                    b = 2 * i + par
                    pool.wait_ge(c_sb, b + 1)
                    g.tensor_copy(spread[:, par, :].rearrange("p (e k) -> p e k", e=L2E),
                                  identb[:, bass.ds(16 * b, 16)].unsqueeze(2).to_broadcast([P, L2E, L2K])
                                  ).then_inc(c_pool, 1)
            c["pe_out"] += 2
            c["dve_out"] += 2
            c["act_out"] += 2

        def fold_pe(pe, c):
            R = lambda name: col(region_b, PACK3, name)
            nc.tensor.matmul(bank6[:, 0:P], R("wqT"), R("rope"), start=True, stop=True)
            nc.tensor.matmul(bank6[:, P:2 * P], R("wkT"), R("rope"), start=True, stop=True)
            nc.tensor.matmul(bank6[:, 2 * P:3 * P], R("bq").to_broadcast([P, P]), R("rope"), start=True, stop=True)
            nc.tensor.matmul(bank6[:, 3 * P:4 * P], R("bk").to_broadcast([P, P]), R("rope"), start=True,
                             stop=True).then_inc(pe_out, 1)
            c["pe_out"] += 1

        def fold_dve(dve, c):
            dve.wait_ge(pe_out, c["pe_out"] + 1)
            nc.vector.tensor_copy(r3[:, 0:256], bank6[:, 0:256])
            nc.vector.tensor_copy(r3[:, 384:640], bank6[:, 256:512])
            nc.vector.tensor_copy(r3[:, 256:384], col(region_b, PACK3, "wv"))
            c["pe_out"] += 1

        w3 = lambda name: col(region_b, PACK3, name)
        PHASES = [
            ("setup",),
            ("norm", x, xn, False, 1e-5, None), ("attention", 0), ("experts", 0),
            ("norm", x, xn, False, 1e-5, None), ("attention", 1),
            ("norm", xn, y, True, 1e-6, (col(region_b, PACK1, "scale"), None)), ("experts", 1),
            ("norm", x, xn, False, 1e-5, None), ("top",),
            ("norm", xn, y, True, 1e-6, (col(region_a, PACK2, "g"), None)), ("relative",),
            ("norm", x, xn, False, 1e-5, None), ("fold",), ("attention", 2),
            ("norm", xn, y, False, 1e-5, (w3("ln1w"), w3("ln1b"))), ("attention", 3),
            ("norm", z, y, False, 1e-5, (w3("ln2w"), w3("ln2b"))), ("experts", 2),
        ][:stop]
        AFTER_A, AFTER_B = 4, 8

        @block.sync
        def _(sp):
            sp.dma_start(x[:, :, :], x_in.rearrange("(t p) c -> p t c", p=P)).then_inc(loaded[1], 16)
            sp.dma_start(common[:, :], packs["common"]).then_inc(loaded[0], 16)
            sp.dma_start(work[:, 0:4 * SEQ], packs["masks"]).then_inc(loaded[0], 16)
            early = PACK0["router"][0]
            sp.dma_start(region_a[:, 0:early], packs["pack0"][:, 0:early]).then_inc(loaded[0], 16)
            sp.dma_start(region_a[:, early:PACK0_W], packs["pack0"][:, early:PACK0_W]).then_inc(loaded[2], 16)
            sp.dma_start(region_b[:, 0:PACK1_W], packs["pack1"]).then_inc(loaded[3], 16)
            sp.wait_ge(zeroed, 1)
            for a in range(0, sorted_tiles(L0E), TILES):
                n = min(TILES, sorted_tiles(L0E) - a)
                sp.dma_start(sorted_in[a * P:(a + n) * P, :].rearrange("(t p) c -> p t c", p=P), z[:, 0:n, :]
                             ).then_inc(cleared, 16)
            if len(PHASES) > 3:
                sorted_sp(sp, 0)
            if len(PHASES) > AFTER_A:
                sp.wait_ge(phase_end, 4 * AFTER_A)
                sp.dma_start(region_a[:, 0:PACK2_W], packs["pack2"]).then_inc(loaded[4], 16)
            if len(PHASES) > AFTER_B:
                sp.wait_ge(phase_end, 4 * AFTER_B)
                sp.dma_start(region_b[:, 0:PACK3_W], packs["pack3"]).then_inc(loaded[5], 16)
            if len(PHASES) > 18:
                sorted_sp(sp, 2)
            sp.wait_ge(phase_end, 4 * len(PHASES))
            sp.dma_start(out.rearrange("(t p) c -> p t c", p=P), x[:, :, :]).then_inc(stored, 16)
            sp.wait_ge(stored, 16)

        def arrivals(eng, phase, n):
            if phase[0] == "setup":
                eng.wait_ge(loaded[0], 16 * 3)
                eng.wait_ge(loaded[1], 16)
            if phase[0] == "experts" and phase[1] == 0:
                eng.wait_ge(loaded[2], 16)
                eng.wait_ge(cleared, 16 * 2)
            if phase[0] == "attention" and phase[1] == 1:
                eng.wait_ge(loaded[3], 16)
            if phase[0] == "top":
                eng.wait_ge(loaded[4], 16)
            if phase[0] == "fold":
                eng.wait_ge(loaded[5], 16)

        @block.tensor
        def _(pe):
            c = new_counts()
            for n, phase in enumerate(PHASES):
                arrivals(pe, phase, n)
                if phase[0] == "norm":
                    norm_pe(pe, c, phase[2])
                elif phase[0] == "attention":
                    attention_pe(pe, phase[1])
                elif phase[0] == "experts":
                    router_pe(pe, c, phase[1])
                    if phase[1] == 1:
                        experts_pe(pe, phase[1])
                    else:
                        sorted_pe(pe, phase[1])
                elif phase[0] == "top":
                    top_pe(pe, c)
                elif phase[0] == "relative":
                    rel_pe(pe)
                elif phase[0] == "fold":
                    fold_pe(pe, c)
                fence(pe, c)

        @block.vector
        def _(dve):
            c = new_counts()
            own = Own(dve_done)
            for n, phase in enumerate(PHASES):
                arrivals(dve, phase, n)
                if phase[0] == "setup":
                    for b in range(2):
                        own.inc(nc.vector.memset(Zb[b][:, 0, :, :, :], 0.0))
                        own.inc(nc.vector.memset(Zb[b][:, 1, :, :, :], 0.0))
                    own.wait(dve)
                    for b in range(2):
                        nc.vector.memset(Zb[b][:, 1, :, :, MAXROW:MAXROW + 2], -1.0)
                    nc.vector.memset(kT[:, :, :, :], 0.0)
                    nc.vector.memset(onesb[:, :], 1.0)
                    nc.vector.tensor_copy(identb[:, :], ident)
                    flat = lambda v: v[:, :, :].rearrange("p a b -> p (a b)")
                    nc.vector.tensor_copy(flat(maskb), work[:, 0:2 * SEQ])
                    nc.vector.tensor_copy(flat(maskTb), work[:, 2 * SEQ:4 * SEQ])
                    nc.vector.tensor_scalar(before[:, :], work[:, 2 * SEQ:2 * SEQ + P], 0.0, None, ALU.is_equal)
                elif phase[0] == "norm":
                    norm_dve(dve, own, c, *phase[1:])
                elif phase[0] == "attention":
                    attention_dve(dve, own, phase[1])
                elif phase[0] == "experts":
                    router_dve(dve, own, c, phase[1])
                    if phase[1] == 1:
                        experts_dve(dve, phase[1])
                    else:
                        sorted_dve(dve, own, phase[1])
                elif phase[0] == "top":
                    top_dve(dve, own, c)
                elif phase[0] == "relative":
                    rel_dve(dve, own)
                elif phase[0] == "fold":
                    fold_dve(dve, c)
                fence(dve, c)

        @block.scalar
        def _(act):
            c = new_counts()
            for n, phase in enumerate(PHASES):
                arrivals(act, phase, n)
                if phase[0] == "norm":
                    norm_act(act, c, *phase[1:4], phase[5])
                elif phase[0] == "attention":
                    attention_act(act, phase[1])
                elif phase[0] == "experts":
                    router_act(act, c, phase[1])
                    if phase[1] == 1:
                        experts_act(act, phase[1])
                    else:
                        sorted_act(act, phase[1])
                elif phase[0] == "top":
                    top_act(act, c)
                elif phase[0] == "relative":
                    rel_act(act)
                elif phase[0] == "fold":
                    c["pe_out"] += 1
                fence(act, c)

        @block.gpsimd
        def _(pool):
            c = new_counts()
            own = Own(pool_done)
            for n, phase in enumerate(PHASES):
                arrivals(pool, phase, n)
                if phase[0] == "setup":
                    for s in (proj_done, qk_evac, v_evac, z_ready, t2_done, red_done, q2_evac, s2_done,
                              exp_done, av_done, tr_done, ot_done, outp_done, x_added, h_ready, y_done,
                              y_added, rows_evac, tile_up, tile_h, tile_down, tile_y, onorm_done):
                        nc.gpsimd.sem_inc(s, 1)
                    nc.gpsimd.sem_inc(g_rows, 3)
                    for s in (g_H, c_tr, c_sb, c_hs, c_st, c_out, c_add):
                        nc.gpsimd.sem_inc(s, 2)
                    for s in (r_pe, r_dve, r_act):
                        nc.gpsimd.sem_inc(s, REL_FROM)
                    nc.gpsimd.memset(z[:, :, :], 0.0).then_inc(zeroed, 1)
                    for b in range(2):
                        own.inc(nc.gpsimd.memset(Vaug[:, b, :, :], 0.0))
                    own.wait(pool)
                    for b in range(2):
                        nc.gpsimd.memset(Vaug[:, b, :, :].rearrange("p t (h c) -> p (t h) c", c=32)[:, :, HD:HD + 1], 1.0)
                elif phase[0] == "attention":
                    attention_pool(pool, own, phase[1])
                elif phase[0] == "relative":
                    rel_pool(pool)
                elif phase[0] == "experts" and phase[1] != 1:
                    sorted_pool(pool, phase[1])
                elif phase[0] == "top":
                    top_pool(pool, c)
                fence(pool, c)


def constants():
    f = np.float32
    common = np.zeros((P, COMMON_W), f)

    def put(name, v):
        at, w = COMMON[name]
        common[:, at:at + w] = v
    put("ident", np.eye(P, dtype=f))
    put("ones", 1.0)
    put("tie", (16 - np.arange(16)).astype(f)[None, :])
    put("slot_no", np.arange(L2K, dtype=f)[None, :])
    put("slot_of_row", (np.arange(P) % L2K).astype(f)[:, None])
    query = (np.arange(P)[:, None, None] + P * np.arange(TPB)[None, :, None])
    other = np.arange(SEQ)[None, None, :]
    mask = np.where(other > query, f(NEG), f(0)).reshape(P, -1)
    maskT = np.where(query > other, f(NEG), f(0)).reshape(P, -1)
    inv = f(1.0) / np.power(f(10000.0), np.arange(0, P, 2, dtype=f) / f(P))
    pre = (np.arange(SEQ, dtype=f)[:, None] * inv[None, :]).T.astype(np.float64)
    sin, cos = np.sin(pre).astype(f), np.cos(pre).astype(f)
    invr = f(1.0) / np.power(f(10000.0), np.arange(0, HD, 2, dtype=f) / f(HD))
    fr = (np.arange(HEADS, dtype=f)[:, None] * invr[None, :]).astype(np.float64)
    rope = np.zeros((P, P), f)
    for h in range(HEADS):
        for k in range(HD // 2):
            e, o = h * HD + 2 * k, h * HD + 2 * k + 1
            cs, sn = f(np.cos(fr[h, k])), f(np.sin(fr[h, k]))
            rope[e, e], rope[o, e], rope[e, o], rope[o, o] = cs, -sn, sn, cs
    return dict(common=common, masks=np.concatenate([mask, maskT], 1),
                rot_a=np.concatenate([-cos, cos]), rot_b=np.concatenate([sin, sin]),
                pos=np.concatenate([sin, cos]), rope=rope)


def pack(plan, width, parts):
    out = np.zeros((P, width), np.float32)
    for name, (at, w) in plan.items():
        v = parts[name]
        out[:v.shape[0], at:at + w] = v
    return out


def kernel(_stop=99, _sim=None, **inputs):
    import concourse.bacc as bacc
    from concourse.bass_utils import run_bass_kernel_spmd

    I = {k: np.asarray(v) for k, v in inputs.items()}
    C = constants()
    column = lambda v: v.reshape(-1, 1)
    row = lambda v: np.broadcast_to(v.reshape(1, -1), (P, v.size))
    experts_in = lambda w: w.transpose(1, 0, 2).reshape(P, -1)
    experts_out = lambda w: w.reshape(w.shape[0], -1, P, w.shape[2]).transpose(2, 0, 1, 3).reshape(P, -1)

    q = "L0_attn_"
    pack0 = pack(PACK0, PACK0_W, dict(
        wqkv=np.concatenate([I[q + n].reshape(P, P).T for n in ("Wq", "Wk", "Wv")], 1),
        bqk=row(np.concatenate([I[q + "bq"].reshape(-1), I[q + "bk"].reshape(-1)])),
        bv=column(I[q + "bv"]), wo=I[q + "Wo"].T, bo=row(I[q + "bo"]), router=I["L0_ffn_router_w"],
        w1=experts_in(np.concatenate([I["L0_ffn_w1"], I["L0_ffn_b1"].reshape(L0E, -1, P).transpose(0, 2, 1)], 2)),
        w2=experts_out(I["L0_ffn_w2"]), b2=I["L0_ffn_b2"]))
    q = "L1_attn_"
    pack1 = pack(PACK1, PACK1_W, dict(
        wqkv=np.concatenate([I[q + n].T for n in ("Wq", "Wk", "Wv")], 1), wo=I[q + "Wo"].T,
        scale=column(I["L1_ffn_norm_scale"]), router=I["L1_ffn_w_router"].T,
        w1=experts_in(I["L1_ffn_w_up"].transpose(0, 2, 1)), w2=experts_out(I["L1_ffn_w_down"].transpose(0, 2, 1))))
    q = "L2_attn_"
    wr = I[q + "W_r"].T
    gate = np.zeros((P, 240), np.float32)
    gate[:, 112:128] = I["L2_ffn_Wg"]
    pack2 = pack(PACK2, PACK2_W, dict(
        g=column(I[q + "g_ln"]), wq=I[q + "W_q"], wk=I[q + "W_k"],
        wvg=np.concatenate([I[q + "W_v"], I[q + "W_g"]], 1), wrT=wr,
        wrTs=np.concatenate([wr[:, 64:], wr[:, :64]], 1), u=column(I[q + "xl_u"]), v=column(I[q + "xl_v"]),
        wo=experts_out(I[q + "W_o"][None]), rot_a=C["rot_a"], rot_b=C["rot_b"], pos=C["pos"],
        router=gate, rb=column(np.tile(I["L2_ffn_bg"], BATCH)),
        w1=experts_in(I["L2_ffn_w1"]), w2=experts_in(I["L2_ffn_w2"]), w3=experts_in(I["L2_ffn_w3"]),
        b1=row(I["L2_ffn_b1"]), b2=row(I["L2_ffn_b2"]), b3=row(I["L2_ffn_b3"])))
    q = "L3_attn_"
    w, b = I[q + "w_qkv"], I[q + "b_qkv"]
    f = "L3_ffn_"
    pack3 = pack(PACK3, PACK3_W, dict(
        wqT=w[:, :P].T, wkT=w[:, P:2 * P].T, wv=w[:, 2 * P:], rope=C["rope"], bq=column(b[:P]), bk=column(b[P:2 * P]),
        bv=column(b[2 * P:]), wo=I[q + "w_fc"], bo=row(I[q + "b_fc"]), ln1w=column(I[f + "ln1_w"]),
        ln1b=column(I[f + "ln1_b"]), wqkv2=I[f + "w_qkv"], wo2=I[f + "w_proj"], ln2w=column(I[f + "ln2_w"]),
        ln2b=column(I[f + "ln2_b"]), router=I[f + "gate_w"], rbias=row(I[f + "gate_b"]),
        w1=experts_in(I[f + "w1"]), w2=experts_out(I[f + "w2"])))

    x = I["L0_attn_hidden_state"]
    arrays = dict(x_in=np.ascontiguousarray(x.reshape(-1, P)), pack0=pack0, pack1=pack1, pack2=pack2, pack3=pack3,
                  common=C["common"], masks=C["masks"])
    nc = bacc.Bacc("TRN2", target_bir_lowering=False, num_devices=1)
    aps = {k: nc.dram_tensor("in_" + k, v.shape, mybir.dt.from_np(v.dtype), kind="ExternalInput").ap()
           for k, v in arrays.items()}
    out = nc.dram_tensor("out", (BATCH * SEQ, P), F32, kind="ExternalOutput").ap()
    sorted_in, sorted_out = (nc.dram_tensor(n, (sorted_tiles(L0E) * P, P), F32).ap() for n in ("sorted_in", "sorted_out"))
    build(nc, aps, aps["x_in"], out, sorted_in, sorted_out, _stop)
    if _sim is not None:
        return _sim(nc, {"in_" + k: v for k, v in arrays.items()})
    r = run_bass_kernel_spmd(nc, [{"in_" + k: v for k, v in arrays.items()}], core_ids=[0])
    return r.results[0]["out"].reshape(x.shape)
```
